# Optimizing a Trainium2 kernel written in Bass

```python
import numpy as np
import jax
import jax.numpy as jnp

def _softmax(x, axis=-1):
    return jax.nn.softmax(x, axis=axis)

def _gelu(x):
    return jax.nn.gelu(x, approximate=True)

def _silu(x):
    return jax.nn.silu(x)

def _sigmoid(x):
    return jax.nn.sigmoid(x)

def _layernorm(x, axis=-1, eps=1e-05):
    m = jnp.mean(x, axis=axis, keepdims=True)
    v = jnp.var(x, axis=axis, keepdims=True)
    return (x - m) / jnp.sqrt(v + eps)

def _scatter_add(tgt, idx, src, axis=0):
    return tgt.at[idx].add(src)

def _segment_sum(src, seg, n):
    return jax.ops.segment_sum(src, seg, n)
kernel_name = 'mk_decoder_postln_d1_seqx_r4_aad9c2'

def setup_inputs(seed: int=0):
    np.random.seed(seed)
    _w = jnp.asarray

    def _rec_inputs():
        import jax
        import jax.numpy as jnp
        _rk = jax.random.key(seed)
        x = 0.5 + 0.2887 * jax.random.normal(jax.random.fold_in(_rk, 1), (4, 512, 512), jnp.float32)
        _lenS = 512 - jax.random.randint(jax.random.fold_in(_rk, 7), (4,), 0, max(1, 512 // 4) + 1, jnp.int32)
        _lenS2 = 512 - jax.random.randint(jax.random.fold_in(_rk, 8), (4,), 0, max(1, 512 // 4) + 1, jnp.int32)
        _ctx_512P = jax.random.normal(jax.random.fold_in(_rk, 11), (4, 16, 128), jnp.float32)
        _ctx_512c = jax.random.dirichlet(jax.random.fold_in(_rk, 511), 0.3 * jnp.ones((16,), jnp.float32), (4, 512))
        _ctx_512t = jnp.einsum('bsk,bkd->bsd', _ctx_512c, _ctx_512P)
        _ctx_512t = _ctx_512t * jax.lax.rsqrt(jnp.mean(jnp.square(_ctx_512t)) + 1e-12) * 0.953939
        ctx_512 = 7.22013e-05 + 1.00017 * (_ctx_512t + 0.3 * jax.random.normal(jax.random.fold_in(_rk, 611), (4, 512, 128), jnp.float32))
        _validS = jnp.arange(512)[None, :] < _lenS[:, None]
        _validS2 = jnp.arange(512)[None, :] < _lenS2[:, None]
        _causal = jnp.tril(jnp.ones((512, 512), dtype=bool))
        mask_SxS2_bk1 = jnp.broadcast_to(_validS2[0:1, :], (512, 512))
        mask_BxS2_bf0 = jnp.logical_not(jnp.ones((4, 512), dtype=bool))
        return (x, ctx_512, mask_SxS2_bk1, mask_BxS2_bf0)
    x, ctx_512, mask_SxS2_bk1, mask_BxS2_bf0 = _rec_inputs()

    def _L0_attn_setup():
        import jax, jax.numpy as jnp
        import numpy as np
        import math
        HIDDEN = 512
        NUM_HEADS = 16
        HEAD_DIM = HIDDEN // NUM_HEADS
        BATCH = 2
        SEQ = 1024
        BLOCK = 128
        TOPK = 64
        NEG = -1000000000.0

        def _split_heads(x):
            n, t, _ = x.shape
            return x.reshape(n, t, NUM_HEADS, HEAD_DIM).transpose(0, 2, 1, 3)

        def _local_attention(q, k, v):
            n, h, t, d = q.shape
            nb = t // BLOCK
            half = BLOCK // 2
            qb = q.reshape(n, h, nb, BLOCK, d)
            win = jnp.arange(nb)[:, None] * BLOCK - half + jnp.arange(2 * BLOCK)[None, :]
            valid = (win >= 0) & (win < t)
            winc = jnp.clip(win, 0, t - 1)
            kb = k[:, :, winc, :]
            vb = v[:, :, winc, :]
            scores = jnp.einsum('nhbqd,nhbkd->nhbqk', qb, kb) / math.sqrt(d)
            scores = jnp.where(valid[None, None, :, None, :], scores, NEG)
            probs = jax.nn.softmax(scores, axis=-1)
            ctx = jnp.einsum('nhbqk,nhbkd->nhbqd', probs, vb)
            return ctx.reshape(n, h, t, d)

        def _global_index(q):
            n, h, t, d = q.shape
            norm = jnp.linalg.norm(q, axis=-1)
            _, top_idx = jax.lax.top_k(norm, TOPK - 2)
            bos = jnp.zeros((n, h, 1), jnp.int32)
            eos = jnp.full((n, h, 1), t - 1, jnp.int32)
            return jnp.concatenate([bos, top_idx.astype(jnp.int32), eos], axis=-1)
        key = jax.random.key(seed)
        ks = jax.random.split(key, 7)
        s = 1.0 / math.sqrt(HIDDEN)
        return {'hidden_states': jax.random.normal(ks[0], (BATCH, SEQ, HIDDEN), jnp.float32), 'Wq': jax.random.normal(ks[1], (HIDDEN, HIDDEN), jnp.float32) * s, 'bq': jnp.zeros((HIDDEN,), jnp.float32), 'Wk': jax.random.normal(ks[2], (HIDDEN, HIDDEN), jnp.float32) * s, 'bk': jnp.zeros((HIDDEN,), jnp.float32), 'Wv': jax.random.normal(ks[3], (HIDDEN, HIDDEN), jnp.float32) * s, 'bv': jnp.zeros((HIDDEN,), jnp.float32)}
    _L0_attn_all = _L0_attn_setup()
    _L0_attn_in = {k: v for k, v in _L0_attn_all.items() if k in ('Wq', 'bq', 'Wk', 'bk', 'Wv', 'bv')}
    del _L0_attn_all

    def _L0_xattn_setup():
        import jax, jax.numpy as jnp
        import numpy as np
        B, S, H = (8, 512, 128)
        key = jax.random.key(seed)
        kq, kk, kqc, kwq, kwk = jax.random.split(key, 5)
        q = jax.random.normal(kq, (B, S, H), dtype=jnp.float32)
        k = jax.random.normal(kk, (B, S, H), dtype=jnp.float32)
        qc_score = jax.random.uniform(kqc, (B, S, S), dtype=jnp.float32)
        attn_mask = jnp.triu(jnp.ones((S, S), dtype=bool), k=1)
        key_padding_mask = jnp.zeros((B, S), dtype=bool)
        scale = 1.0 / np.sqrt(H)
        Wq = jax.random.normal(kwq, (H, H), dtype=jnp.float32) * scale
        Wk = jax.random.normal(kwk, (H, H), dtype=jnp.float32) * scale
        bq = jnp.zeros((H,), dtype=jnp.float32)
        bk = jnp.zeros((H,), dtype=jnp.float32)
        return {'q': q, 'k': k, 'attn_mask': attn_mask, 'key_padding_mask': key_padding_mask, 'qc_score': qc_score, 'Wq': Wq, 'bq': bq, 'Wk': Wk, 'bk': bk}
    _L0_xattn_all = _L0_xattn_setup()
    _L0_xattn_in = {k: v for k, v in _L0_xattn_all.items() if k in ('Wq', 'bq', 'Wk', 'bk')}
    del _L0_xattn_all

    def _L0_ffn_setup():
        import jax, jax.numpy as jnp
        import numpy as np
        B, S, D = (4, 128, 512)
        E, K, H = (8, 2, 352)
        HS = 2 * 352
        ALPHA = 0.001
        W_SCALE = 0.02

        def _moe_forward(hidden_states, gate_w, w_gate, w_up, w_down, sw_gate, sw_up, sw_down):
            b, s, d = hidden_states.shape
            x = hidden_states.reshape(-1, d)
            T = x.shape[0]
            logits = x @ gate_w
            scores = jax.nn.softmax(logits, axis=-1)
            topk_w, topk_idx = jax.lax.top_k(scores, K)
            mask = jax.nn.one_hot(topk_idx, E, dtype=scores.dtype).sum(axis=1)
            ce = mask.mean(axis=0)
            Pi = scores.mean(axis=0)
            aux_loss = (Pi * ce * E).sum() * ALPHA
            comb = jnp.zeros((T, E), dtype=x.dtype)
            comb = comb.at[jnp.arange(T)[:, None], topk_idx].add(topk_w)
            g = jax.nn.silu(jnp.einsum('td,edh->teh', x, w_gate)) * jnp.einsum('td,edh->teh', x, w_up)
            routed = jnp.einsum('teh,ehd,te->td', g, w_down, comb)
            shared = jax.nn.silu(x @ sw_gate) * (x @ sw_up) @ sw_down
            out = (routed + shared).reshape(b, s, d)
            return (out, aux_loss)
        key = jax.random.key(seed)
        ks = jax.random.split(key, 8)
        rn = lambda k, sh: jax.random.normal(k, sh, dtype=jnp.float32)
        return {'hidden_states': rn(ks[0], (B, S, D)), 'gate_w': rn(ks[1], (D, E)) * W_SCALE, 'w_gate': rn(ks[2], (E, D, H)) * W_SCALE, 'w_up': rn(ks[3], (E, D, H)) * W_SCALE, 'w_down': rn(ks[4], (E, H, D)) * W_SCALE, 'sw_gate': rn(ks[5], (D, HS)) * W_SCALE, 'sw_up': rn(ks[6], (D, HS)) * W_SCALE, 'sw_down': rn(ks[7], (HS, D)) * W_SCALE}
    _L0_ffn_all = _L0_ffn_setup()
    _L0_ffn_in = {k: v for k, v in _L0_ffn_all.items() if k in ('gate_w', 'w_gate', 'w_up', 'w_down', 'sw_gate', 'sw_up', 'sw_down')}
    del _L0_ffn_all
    return {'x': x, 'ctx_512': ctx_512, 'mask_SxS2_bk1': mask_SxS2_bk1, 'mask_BxS2_bf0': mask_BxS2_bf0, 'L0_attn_Wq': _L0_attn_in['Wq'], 'L0_attn_bq': _L0_attn_in['bq'], 'L0_attn_Wk': _L0_attn_in['Wk'], 'L0_attn_bk': _L0_attn_in['bk'], 'L0_attn_Wv': _L0_attn_in['Wv'], 'L0_attn_bv': _L0_attn_in['bv'], 'L0_xattn_Wq': _L0_xattn_in['Wq'], 'L0_xattn_bq': _L0_xattn_in['bq'], 'L0_xattn_Wk': _L0_xattn_in['Wk'], 'L0_xattn_bk': _L0_xattn_in['bk'], 'L0_ffn_gate_w': _L0_ffn_in['gate_w'], 'L0_ffn_w_gate': _L0_ffn_in['w_gate'], 'L0_ffn_w_up': _L0_ffn_in['w_up'], 'L0_ffn_w_down': _L0_ffn_in['w_down'], 'L0_ffn_sw_gate': _L0_ffn_in['sw_gate'], 'L0_ffn_sw_up': _L0_ffn_in['sw_up'], 'L0_ffn_sw_down': _L0_ffn_in['sw_down']}

def reference(x, ctx_512, mask_SxS2_bk1, mask_BxS2_bf0, L0_attn_Wq, L0_attn_bq, L0_attn_Wk, L0_attn_bk, L0_attn_Wv, L0_attn_bv, L0_xattn_Wq, L0_xattn_bq, L0_xattn_Wk, L0_xattn_bk, L0_ffn_gate_w, L0_ffn_w_gate, L0_ffn_w_up, L0_ffn_w_down, L0_ffn_sw_gate, L0_ffn_sw_up, L0_ffn_sw_down):
    import jax
    import jax.numpy as jnp

    def _L0_attn_ref(hidden_states, Wq, bq, Wk, bk, Wv, bv):
        import jax, jax.numpy as jnp
        import numpy as np
        import math
        HIDDEN = 512
        NUM_HEADS = 16
        HEAD_DIM = HIDDEN // NUM_HEADS
        BATCH = 2
        SEQ = 1024
        BLOCK = 128
        TOPK = 64
        NEG = -1000000000.0

        def _split_heads(x):
            n, t, _ = x.shape
            return x.reshape(n, t, NUM_HEADS, HEAD_DIM).transpose(0, 2, 1, 3)

        def _local_attention(q, k, v):
            n, h, t, d = q.shape
            nb = t // BLOCK
            half = BLOCK // 2
            qb = q.reshape(n, h, nb, BLOCK, d)
            win = jnp.arange(nb)[:, None] * BLOCK - half + jnp.arange(2 * BLOCK)[None, :]
            valid = (win >= 0) & (win < t)
            winc = jnp.clip(win, 0, t - 1)
            kb = k[:, :, winc, :]
            vb = v[:, :, winc, :]
            scores = jnp.einsum('nhbqd,nhbkd->nhbqk', qb, kb) / math.sqrt(d)
            scores = jnp.where(valid[None, None, :, None, :], scores, NEG)
            probs = jax.nn.softmax(scores, axis=-1)
            ctx = jnp.einsum('nhbqk,nhbkd->nhbqd', probs, vb)
            return ctx.reshape(n, h, t, d)

        def _global_index(q):
            n, h, t, d = q.shape
            norm = jnp.linalg.norm(q, axis=-1)
            _, top_idx = jax.lax.top_k(norm, TOPK - 2)
            bos = jnp.zeros((n, h, 1), jnp.int32)
            eos = jnp.full((n, h, 1), t - 1, jnp.int32)
            return jnp.concatenate([bos, top_idx.astype(jnp.int32), eos], axis=-1)
        q = _split_heads(hidden_states @ Wq + bq)
        k = _split_heads(hidden_states @ Wk + bk)
        v = _split_heads(hidden_states @ Wv + bv)
        n, h, t, d = q.shape
        ctx = _local_attention(q, k, v)
        idx = _global_index(q)
        qg = jnp.take_along_axis(q, idx[..., None], axis=-2)
        g_scores = jnp.einsum('nhqd,nhkd->nhqk', qg, k) / math.sqrt(d)
        g_probs = jax.nn.softmax(g_scores, axis=-1)
        g_ctx = jnp.einsum('nhqk,nhkd->nhqd', g_probs, v)
        bn = jnp.arange(n)[:, None, None]
        bh = jnp.arange(h)[None, :, None]
        ctx = ctx.at[bn, bh, idx].set(g_ctx)
        out = ctx.transpose(0, 2, 1, 3).reshape(n, t, h * d)
        return out

    def _L0_xattn_ref(q, k, attn_mask, key_padding_mask, qc_score, Wq, bq, Wk, bk):
        import jax, jax.numpy as jnp
        import numpy as np
        B, S, H = (8, 512, 128)
        qp = jnp.einsum('bsh,oh->bso', q, Wq) + bq
        kp = jnp.einsum('bth,oh->bto', k, Wk) + bk
        scaling = jnp.asarray(float(H) ** (-0.5), dtype=qp.dtype)
        scores = jnp.einsum('bsh,bth->bst', qp, kp) * scaling
        scores = scores * qc_score
        mask = attn_mask[None, :, :] | key_padding_mask[:, None, :]
        scores = jnp.where(mask, -jnp.inf, scores)
        return jax.nn.softmax(scores, axis=-1)

    def _L0_ffn_ref(hidden_states, gate_w, w_gate, w_up, w_down, sw_gate, sw_up, sw_down):
        import jax, jax.numpy as jnp
        import numpy as np
        B, S, D = (4, 128, 512)
        E, K, H = (8, 2, 352)
        HS = 2 * 352
        ALPHA = 0.001
        W_SCALE = 0.02

        def _moe_forward(hidden_states, gate_w, w_gate, w_up, w_down, sw_gate, sw_up, sw_down):
            b, s, d = hidden_states.shape
            x = hidden_states.reshape(-1, d)
            T = x.shape[0]
            logits = x @ gate_w
            scores = jax.nn.softmax(logits, axis=-1)
            topk_w, topk_idx = jax.lax.top_k(scores, K)
            mask = jax.nn.one_hot(topk_idx, E, dtype=scores.dtype).sum(axis=1)
            ce = mask.mean(axis=0)
            Pi = scores.mean(axis=0)
            aux_loss = (Pi * ce * E).sum() * ALPHA
            comb = jnp.zeros((T, E), dtype=x.dtype)
            comb = comb.at[jnp.arange(T)[:, None], topk_idx].add(topk_w)
            g = jax.nn.silu(jnp.einsum('td,edh->teh', x, w_gate)) * jnp.einsum('td,edh->teh', x, w_up)
            routed = jnp.einsum('teh,ehd,te->td', g, w_down, comb)
            shared = jax.nn.silu(x @ sw_gate) * (x @ sw_up) @ sw_down
            out = (routed + shared).reshape(b, s, d)
            return (out, aux_loss)
        out, _aux = _moe_forward(hidden_states, gate_w, w_gate, w_up, w_down, sw_gate, sw_up, sw_down)
        return out
    x = _layernorm(x + _L0_attn_ref(x, L0_attn_Wq, L0_attn_bq, L0_attn_Wk, L0_attn_bk, L0_attn_Wv, L0_attn_bv), axis=-1)
    x = _layernorm(x + _L0_xattn_ref(ctx_512, ctx_512, mask_SxS2_bk1, mask_BxS2_bf0, x, L0_xattn_Wq, L0_xattn_bq, L0_xattn_Wk, L0_xattn_bk), axis=-1)
    x = _layernorm(x + _L0_ffn_ref(x, L0_ffn_gate_w, L0_ffn_w_gate, L0_ffn_w_up, L0_ffn_w_down, L0_ffn_sw_gate, L0_ffn_sw_up, L0_ffn_sw_down), axis=-1)
    return x

_drawn_inputs = setup_inputs


def setup_inputs(seed=0):
    import zlib

    import numpy as np

    out = dict(_drawn_inputs(seed))
    spreads = {'L0_attn_bq': (0.0, 0.8),
     'L0_attn_bk': (0.0, 2.0),
     'L0_attn_bv': (0.0, 0.1),
     'L0_xattn_bq': (0.0, 2.0),
     'L0_xattn_bk': (0.0, 2.0)}
    factors = {'ctx_512': 3.886,
     'L0_attn_Wq': 5.603,
     'L0_attn_Wk': 8.0,
     'L0_xattn_Wq': 4.056,
     'L0_xattn_Wk': 3.885,
     'L0_ffn_gate_w': 5.435,
     'L0_ffn_w_gate': 5.736,
     'L0_ffn_w_up': 5.465,
     'L0_ffn_w_down': 5.316,
     'L0_ffn_sw_gate': 5.122,
     'L0_ffn_sw_up': 4.854,
     'L0_ffn_sw_down': 4.886}
    for name, (base, spread) in spreads.items():
        noise = np.random.default_rng([zlib.crc32(name.encode()), seed]).standard_normal(out[name].shape)
        drawn = base * np.exp(spread * noise) if base else spread * noise
        out[name] = jnp.asarray(drawn.astype(out[name].dtype))
    for name, factor in factors.items():
        out[name] = (out[name] * factor).astype(out[name].dtype)
    return out
```

```python
from contextlib import ExitStack

import concourse.bass as bass
from concourse import mybir

P = 128
F32 = mybir.dt.float32
F32R = mybir.dt.float32r
BF16 = mybir.dt.bfloat16
I32 = mybir.dt.int32
U32 = mybir.dt.uint32
U8 = mybir.dt.uint8
ALU = mybir.AluOpType
ACT = mybir.ActivationFunctionType
AX = mybir.AxisListType

B, S, D = 4, 512, 512
H, HD = 16, 32
DC = D // P
TT = S // P
HG = H * HD // P
HPG = P // HD
U = B * HG
BLOCK, TOPK = 128, 64
NEG_SEL = -1.0e30
SENTINEL = 3.0e38


class Memory:

    def __init__(self, nc, ctx):
        self.nc, self.ctx = nc, ctx

    def sb(self, name, shape, dt=F32):
        return self.ctx.enter_context(self.nc.sbuf_tensor(name, shape, dt))

    def ps(self, name, shape, dt=F32):
        return self.ctx.enter_context(self.nc.psum_tensor(name, shape, dt))

    def sem(self, name):
        return self.ctx.enter_context(self.nc.semaphore(name))


def wait_apart(eng, sem, value, passed):
    eng.wait_ge(sem, value)
    eng.sem_inc(passed, 1)


class Kept:
    pass


def build_constants(nc, m, c, table_dram):
    c.ident = m.sb("ident", [P, P])
    c.ident_bf = m.sb("ident_bf", [P, P], BF16)
    c.head_cols = m.sb("head_cols", [P, HG, H])
    c.window = m.sb("window", [P, HPG, TT, P], BF16)
    zeros = m.sb("zeros", [P, table_dram.shape[0] // P], U32)
    built, cleared, table_out = m.sem("constants_step"), m.sem("zeros_done"), m.sem("table_out")
    with nc.Block() as block:
        @block.vector
        def _(dve):
            dve.memset(zeros[:], 0).then_inc(cleared, 1)

        @block.sync
        def _(sp):
            sp.wait_ge(cleared, 1)
            sp.dma_start(table_dram.rearrange("(p n) a -> p (n a)", p=P), zeros[:]).then_inc(table_out, 16)
            sp.wait_ge(table_out, 16)

        @block.gpsimd
        def _(pool):
            pool.memset(c.ident[:], 0.0)
            pool.memset(c.ident_bf[:], 0.0)
            pool.memset(c.window[:], 0.0)
            pool.memset(c.head_cols[:], 1.0).then_inc(built, 1)
            pool.wait_ge(built, 1)
            for t in (c.ident, c.ident_bf):
                pool.affine_select(out=t[:], in_=t[:], compare_op=ALU.not_equal, fill=1.0, base=0,
                                   pattern=[[-1, P]], channel_multiplier=1)
            pool.affine_select(out=c.head_cols[:], in_=c.head_cols[:], compare_op=ALU.is_ge, fill=0.0,
                               base=0, pattern=[[P, HG], [-HD, H]], channel_multiplier=1).then_inc(built, 1)
            pool.wait_ge(built, 2)
            pool.affine_select(out=c.head_cols[:], in_=c.head_cols[:], compare_op=ALU.is_ge, fill=0.0,
                               base=HD - 1, pattern=[[-P, HG], [HD, H]], channel_multiplier=-1)
            n = 2
            for h in range(HPG):
                w = c.window[:, h, :, :].rearrange("p k n -> p (k n)")
                for row in (HD * h, HD * h + 1):
                    pool.affine_select(out=w, in_=w, compare_op=ALU.not_equal, fill=1.0, base=-row,
                                       pattern=[[0, TT * P]], channel_multiplier=1).then_inc(built, 1)
                    n += 1
                    pool.wait_ge(built, n)
                for t in range(TT):
                    lo, hi = max(0, BLOCK * t - BLOCK // 2), min(S, BLOCK * t + 3 * BLOCK // 2)
                    for a, b in ((0, lo), (hi, S)):
                        if b > a:
                            pool.affine_select(out=w[:, a:b], in_=w[:, a:b], compare_op=ALU.not_equal,
                                               fill=1.0, base=-(HD * h + 2 + t), pattern=[[0, b - a]],
                                               channel_multiplier=1).then_inc(built, 1)
                            n += 1
                            pool.wait_ge(built, n)


def project(nc, c, x, wq, bq, wk, bk, wv, bv, qk_dram, norm_dram):
    with ExitStack() as ctx:
        m = Memory(nc, ctx)
        w_raw = c.attn[:, 0:2 * DC, :].rearrange("p (n c) d -> p n c d", c=DC)
        w_hi = m.sb("w_hi", [P, 3, DC, D], F32R)
        w_lo = m.sb("w_lo", [P, 3, DC, D], F32R)
        x_in = m.sb("x_in", [P, TT, D])
        xT_hi = m.sb("xT_hi", [P, DC, S], F32R)
        xT_lo = m.sb("xT_lo", [P, DC, S], F32R)
        bias_qk = m.sb("bias_qk", [P, 2, HG])
        bias_v = m.sb("bias_v", [P, D])
        raw = c.attn[:, 2 * DC:2 * DC + 4, :]
        parts = m.sb("parts", [P, 4, 2, S], F32R)
        squares = c.attn[:, 2 * DC + 4:2 * DC + 8, :]
        norm_sb = m.sb("norm_sb", [H, S])
        ps_tr = m.ps("ps_tr", [P, 2, S])
        ps_proj = m.ps("ps_proj", [P, 4, S])
        ps_norm = m.ps("ps_norm", [H, S])

        w_loaded = [m.sem(f"w_loaded{n}") for n in range(3)]
        bias_loaded, x_loaded = m.sem("bias_loaded"), m.sem("x_loaded")
        w_hi_done, w_split = m.sem("w_hi_done"), m.sem("w_split")
        x_turned, xT_hi_done, xT_lo_done = m.sem("x_turned"), m.sem("xT_hi_done"), m.sem("xT_lo_done")
        proj_done, qk_out, v_out = m.sem("proj_done"), m.sem("qk_out"), m.sem("v_out")
        hi_done, lo_done, raw_used = m.sem("hi_done"), m.sem("lo_done"), m.sem("raw_used")
        parts_stored = [m.sem(f"parts_stored{k}") for k in range(4)]
        squares_done, norm_acc, norm_out, norm_stored = (
            m.sem("squares_done"), m.sem("norm_acc"), m.sem("norm_out"), m.sem("norm_stored"))

        with nc.Block() as block:
            @block.sync
            def _(sp):
                for n, w in enumerate((wq, wk, wv)):
                    if n == 2:
                        sp.wait_ge(w_split, 1)
                    sp.dma_start(w_raw[:, n % 2], w.rearrange("(c p) n -> p c n", p=P)).then_inc(w_loaded[n], 16)
                    if n == 0:
                        sp.dma_start(x_in[:], x[0:1].rearrange("b (t p) d -> p (b t) d", p=P)).then_inc(x_loaded, 16)
                def store_parts(i):
                    for n in range(2 * HG):
                        sp.wait_ge(lo_done, 2 * HG * i + n + 1)
                        sp.dma_start(qk_dram[n // HG, :, bass.ds(i * HG + n % HG, 1)].rearrange("h a p n -> (a p) h n"),
                                     parts[:, n % 4].bitcast(F32)).then_inc(parts_stored[n % 4], 16)

                with sp.Fori(0, B - 1) as i:
                    sp.wait_ge(x_turned, 4 * i + 4)
                    sp.dma_start(x_in[:], x[bass.ds(i + 1, 1)].rearrange("b (t p) d -> p (b t) d", p=P)).then_inc(x_loaded, 16)
                    store_parts(i)
                store_parts(B - 1)
                for k in range(4):
                    sp.wait_ge(parts_stored[k], 32 * B + 16)
                sp.wait_ge(norm_stored, 16 * B + 16)

            @block.scalar
            def _(act):
                act.dma_start(bias_qk[:, 0, :], bq.rearrange("(g p) -> p g", p=P), allow_slow_non_contiguous=True).then_inc(bias_loaded, 16)
                act.dma_start(bias_qk[:, 1, :], bk.rearrange("(g p) -> p g", p=P), allow_slow_non_contiguous=True).then_inc(bias_loaded, 16)
                act.dma_start(bias_v[:], bv.rearrange("(a n) -> a n", a=1).to_broadcast([P, D])).then_inc(bias_loaded, 16)
                for n in range(3):
                    act.wait_ge(w_loaded[n], 16)
                    act.activation(w_hi[:, n], w_raw[:, n % 2], ACT.Copy).then_inc(w_hi_done, 1)
                act.wait_ge(bias_loaded, 48)
                with act.Fori(0, B) as i:
                    for dc in range(DC):
                        act.wait_ge(x_turned, 4 * i + dc + 1)
                        if dc == 0:
                            act.wait_ge(v_out, 4 * i + 4)
                        act.activation(xT_hi[:, dc, :], ps_tr[:, dc % 2, :], ACT.Copy).then_inc(xT_hi_done, 1)
                    for n in range(2 * HG):
                        act.wait_ge(proj_done, 12 * i + n + 1)
                        act.wait_ge(raw_used, 8 * i + n + 1)
                        act.activation(raw[:, n % 4, :], ps_proj[:, n % 4, :], ACT.Identity,
                                       bias=bias_qk[:, n // HG, n % HG:n % HG + 1]).then_inc(qk_out, 1)
                    act.wait_ge(norm_acc, i + 2)
                    act.wait_ge(norm_stored, 16 * i + 16)
                    act.activation(norm_sb[:], ps_norm[:], ACT.Copy).then_inc(norm_out, 1)
                    act.wait_ge(norm_out, i + 2)
                    act.dma_start(norm_dram[bass.ds(i * H, H), :], norm_sb[:]).then_inc(norm_stored, 16)

            @block.vector
            def _(dve):
                for n in range(3):
                    dve.wait_ge(w_hi_done, n + 1)
                    dve.tensor_tensor(w_lo[:, n], w_raw[:, n % 2], w_hi[:, n].bitcast(F32), ALU.subtract).then_inc(w_split, 1)
                dve.wait_ge(bias_loaded, 48)
                with dve.Fori(0, B) as i:
                    for dc in range(DC):
                        dve.wait_ge(xT_hi_done, 4 * i + dc + 1)
                        dve.tensor_tensor(xT_lo[:, dc, :], ps_tr[:, dc % 2, :], xT_hi[:, dc, :].bitcast(F32),
                                          ALU.subtract).then_inc(xT_lo_done, 1)
                    for n in range(2 * HG):
                        dve.wait_ge(qk_out, 8 * i + n + 1)
                        dve.wait_ge(parts_stored[n % 4], 32 * i + 16 * (n // 4) + 16)
                        dve.tensor_copy(parts[:, n % 4, 0, :], raw[:, n % 4, :]).then_inc(hi_done, 1)
                    for t in range(TT):
                        n = 2 * HG + t
                        dve.wait_ge(proj_done, 12 * i + n + 1)
                        dve.tensor_tensor(c.v[:, bass.ds(i * TT + t, 1), :].rearrange("p a n -> p (a n)"),
                                          ps_proj[:, n % 4, :], bias_v[:], ALU.add).then_inc(v_out, 1)

            @block.gpsimd
            def _(pool):
                pool.sem_inc(v_out, 4)
                pool.sem_inc(norm_stored, 16)
                pool.sem_inc(norm_out, 1)
                pool.sem_inc(norm_acc, 1)
                pool.sem_inc(raw_used, 4)
                for k in range(4):
                    pool.sem_inc(parts_stored[k], 16)
                with pool.Fori(0, B) as i:
                    pool.wait_ge(norm_acc, i + 1)
                    for n in range(2 * HG):
                        pool.wait_ge(hi_done, 8 * i + n + 1)
                        if n < HG:
                            pool.tensor_tensor(squares[:, n, :], raw[:, n, :], raw[:, n, :], ALU.mult).then_inc(squares_done, 1)
                        pool.tensor_tensor(parts[:, n % 4, 1, :], raw[:, n % 4, :], parts[:, n % 4, 0, :].bitcast(F32),
                                           ALU.subtract).then_inc(lo_done, 1)
                        pool.wait_ge(lo_done, 8 * i + n + 1)
                        if n < HG:
                            pool.wait_ge(squares_done, 4 * i + n + 1)
                        pool.sem_inc(raw_used, 1)

            @block.tensor
            def _(pe):
                pe.wait_ge(w_split, 3)
                with pe.Fori(0, B) as i:
                    pe.wait_ge(x_loaded, 16 * i + 16)
                    for dc in range(DC):
                        if dc >= 2:
                            pe.wait_ge(xT_lo_done, 4 * i + dc - 1)
                        for t in range(TT):
                            last = pe.transpose(ps_tr[:, dc % 2, t * P:(t + 1) * P],
                                                x_in[:, t, dc * P:(dc + 1) * P], c.ident[:])
                        last.then_inc(x_turned, 1)

                    def product(n, stationary, moving):
                        if n < 4:
                            pe.wait_ge(v_out, 4 * i + n + 1)
                        else:
                            pe.wait_ge(qk_out, 8 * i + n - 3)
                        for dc in range(DC):
                            if n == 0:
                                pe.wait_ge(xT_lo_done, 4 * i + dc + 1)
                            for k, (a, b) in enumerate(((0, 0), (0, 1), (1, 0))):
                                last = pe.matmul(ps_proj[:, n % 4, :], stationary[a](dc), moving[b](dc),
                                                 start=(dc == 0 and k == 0), stop=(dc == DC - 1 and k == 2))
                        last.then_inc(proj_done, 1)

                    for n in range(2 * HG):
                        g, which = n % HG, n // HG
                        product(n, [lambda dc, w=w: w[:, which, dc, g * P:(g + 1) * P] for w in (w_hi, w_lo)],
                                [lambda dc, t=t: t[:, dc, :] for t in (xT_hi, xT_lo)])
                    pe.wait_ge(norm_out, i + 1)
                    for g in range(HG):
                        pe.wait_ge(squares_done, 4 * i + g + 1)
                        last = pe.matmul(ps_norm[:], c.head_cols[:, g, :], squares[:, g, :],
                                         start=(g == 0), stop=(g == HG - 1))
                    last.then_inc(norm_acc, 1)
                    for t in range(TT):
                        product(2 * HG + t, [lambda dc, x=x_: x[:, dc, t * P:(t + 1) * P] for x_ in (xT_hi, xT_lo)],
                                [lambda dc, w=w: w[:, 2, dc, :] for w in (w_hi, w_lo)])


def choose_queries(nc, c, norm_dram, context, x_wq, x_bq, x_wk, x_bk):
    with ExitStack() as ctx:
        m = Memory(nc, ctx)
        work = m.sb("work", [B * H, S + 2])
        top8 = m.sb("top8", [B * H, 8])
        bar = m.sb("bar", [B * H, S])
        w_in = m.sb("xw_in", [P, 2, P])
        w_sb = m.sb("xw_sb", [P, 2, P])
        wT_hi = m.sb("xwT_hi", [P, 2, P], F32R)
        wT_lo = m.sb("xwT_lo", [P, 2, P], F32R)
        bias = m.sb("x_bias", [P, 2])
        c_in = m.sb("c_in", [P, TT, P])
        cT = m.sb("cT", [P, S])
        cT_hi = m.sb("cT_hi", [P, S], F32R)
        cT_lo = m.sb("cT_lo", [P, S], F32R)
        c_raw = m.sb("c_raw", [P, 2, S])
        ps_bar = m.ps("ps_bar", [P, TT, B * H])
        ps_w = m.ps("ps_w", [P, 2, P])
        ps_c = m.ps("ps_c", [P, S])
        ps_qk = m.ps("ps_qk", [P, 2, S])
        loaded, step, turned = m.sem("norms_loaded"), m.sem("choose_step"), m.sem("bar_turned")
        w_loaded, b_loaded, c_loaded = m.sem("xw_loaded"), m.sem("xb_loaded"), m.sem("c_loaded")
        w_turned, w_copied, w_hi_done, w_lo_done = m.sem("xw_turned"), m.sem("xw_copied"), m.sem("xw_hi"), m.sem("xw_lo")
        c_turned, c_copied, c_hi_done, c_lo_done = m.sem("c_turned"), m.sem("c_copied"), m.sem("c_hi"), m.sem("c_lo")
        qk_done, qk_copied, qk_hi_done, qk_lo_done = m.sem("qk_done"), m.sem("qk_copied"), m.sem("qk_hi"), m.sem("qk_lo")
        with nc.Block() as block:
            @block.sync
            def _(sp):
                sp.dma_start(work[:, 0:S], norm_dram[:]).then_inc(loaded, 16)
                sp.dma_start(w_in[:, 0, :], x_wq).then_inc(w_loaded, 16)
                sp.dma_start(w_in[:, 1, :], x_wk).then_inc(w_loaded, 16)
                for n, b in enumerate((x_bq, x_bk)):
                    sp.dma_start(bias[:, n:n + 1], b.rearrange("(p a) -> p a", a=1),
                                 allow_slow_non_contiguous=True).then_inc(b_loaded, 16)
                sp.dma_start(c_in[:], context[0:1].rearrange("b (t p) d -> p (b t) d", p=P)).then_inc(c_loaded, 16)
                with sp.Fori(1, B) as i:
                    sp.wait_ge(c_turned, i)
                    sp.dma_start(c_in[:], context[bass.ds(i, 1)].rearrange("b (t p) d -> p (b t) d", p=P)).then_inc(c_loaded, 16)

            @block.vector
            def _(dve):
                dve.memset(work[:, S:S + 2], SENTINEL).then_inc(step, 1)
                dve.wait_ge(loaded, 16)
                for r in range(TOPK // 8):
                    dve.wait_ge(step, 2 * r + 1)
                    dve.max(top8[:], work[:]).then_inc(step, 1)
                    dve.wait_ge(step, 2 * r + 2)
                    dve.match_replace(work[:], top8[:], work[:], -1.0).then_inc(step, 1)
                n = TOPK // 4 + 1
                dve.wait_ge(step, n)
                dve.tensor_scalar(bar[:], work[:, 0:S], 0.0, NEG_SEL, ALU.is_ge, ALU.mult).then_inc(step, 1)
                dve.wait_ge(step, n + 1)
                dve.memset(bar[:, 0:1], 0.0)
                dve.memset(bar[:, S - 1:S], 0.0).then_inc(step, 1)
                dve.wait_ge(turned, 1)
                dve.tensor_copy(c.bar[:].rearrange("p t n -> p (t n)"),
                                ps_bar[:].rearrange("p t n -> p (t n)"))

            @block.scalar
            def _(act):
                act.wait_ge(w_turned, 1)
                act.activation(w_sb[:], ps_w[:], ACT.Copy).then_inc(w_copied, 1)
                act.activation(wT_hi[:], ps_w[:], ACT.Copy).then_inc(w_hi_done, 1)
                act.wait_ge(b_loaded, 32)
                with act.Fori(0, B) as i:
                    act.wait_ge(c_turned, i + 1)
                    act.wait_ge(c_lo_done, i + 1)
                    act.wait_ge(qk_done, 2 * i + 2)
                    act.activation(cT[:], ps_c[:], ACT.Copy).then_inc(c_copied, 1)
                    act.activation(cT_hi[:], ps_c[:], ACT.Copy).then_inc(c_hi_done, 1)
                    for n in range(2):
                        act.wait_ge(qk_done, 2 * i + n + 3)
                        act.wait_ge(qk_lo_done, 2 * i + n + 1)
                        act.activation(c_raw[:, n, :], ps_qk[:, n, :], ACT.Identity, bias=bias[:, n:n + 1]).then_inc(qk_copied, 1)

            @block.gpsimd
            def _(pool):
                pool.sem_inc(c_lo_done, 1)
                pool.sem_inc(qk_done, 2)
                pool.sem_inc(qk_lo_done, 2)
                pool.wait_ge(w_copied, 1)
                pool.wait_ge(w_hi_done, 1)
                pool.tensor_tensor(wT_lo[:], w_sb[:], wT_hi[:].bitcast(F32), ALU.subtract).then_inc(w_lo_done, 1)
                with pool.Fori(0, B) as i:
                    pool.wait_ge(c_copied, i + 1)
                    pool.wait_ge(c_hi_done, i + 1)
                    pool.tensor_tensor(cT_lo[:], cT[:], cT_hi[:].bitcast(F32), ALU.subtract).then_inc(c_lo_done, 1)
                    for n in range(2):
                        hi, lo = c.qk_ctx[n][0][:, bass.ds(i * S, S)], c.qk_ctx[n][1][:, bass.ds(i * S, S)]
                        pool.wait_ge(qk_copied, 2 * i + n + 1)
                        pool.tensor_copy(hi, c_raw[:, n, :]).then_inc(qk_hi_done, 1)
                        pool.wait_ge(qk_hi_done, 2 * i + n + 1)
                        pool.tensor_tensor(lo, c_raw[:, n, :], hi.bitcast(F32), ALU.subtract).then_inc(qk_lo_done, 1)

            @block.tensor
            def _(pe):
                pe.wait_ge(w_loaded, 32)
                for n in range(2):
                    last = pe.transpose(ps_w[:, n, :], w_in[:, n, :], c.ident[:])
                last.then_inc(w_turned, 1)
                pe.wait_ge(w_lo_done, 1)
                with pe.Fori(0, B) as i:
                    pe.wait_ge(c_loaded, 16 * i + 16)
                    for t in range(TT):
                        last = pe.transpose(ps_c[:, t * P:(t + 1) * P], c_in[:, t, :], c.ident[:])
                    last.then_inc(c_turned, 1)
                    pe.wait_ge(c_lo_done, i + 2)
                    for n in range(2):
                        pe.wait_ge(qk_lo_done, 2 * i + n + 1)
                        for k, (a, b) in enumerate(((wT_hi, cT_hi), (wT_hi, cT_lo), (wT_lo, cT_hi))):
                            last = pe.matmul(ps_qk[:, n, :], a[:, n, :], b[:], start=(k == 0), stop=(k == 2))
                        last.then_inc(qk_done, 1)
                pe.wait_ge(step, TOPK // 4 + 3)
                for t in range(TT):
                    last = pe.transpose(ps_bar[:, t, :], bar[:, t * P:(t + 1) * P], c.ident[0:B * H, 0:B * H])
                last.then_inc(turned, 1)


SCALE = float(HD) ** -0.5
NU = HPG * TT
NDMA = 16 * 8
AHEAD = [2 if s % 3 == 0 else 1 for s in range(12)] + [0] * 4
GW = 10


def need(eng, sem, value):
    if not isinstance(value, int) or value > 0:
        eng.wait_ge(sem, value)


def attend(nc, c, qk_dram):
    with ExitStack() as ctx:
        m = Memory(nc, ctx)
        q4 = m.sb("q4", [P, 2, HPG, S], F32R)
        k4 = m.sb("k4", [P, 2, HPG, S], F32R)
        vu = m.sb("vu", [P, 2, TT, HPG, 2 * HD])
        probs = m.sb("probs", [P, HPG, TT, S])
        outT = m.sb("outT", [P, S])
        maxima = m.sb("maxima", [P, TT * (HPG * GW + 2)])
        m_all = m.sb("m_all", [P, TT, HPG])
        m_win = m.sb("m_win", [P, TT, HPG])
        m_bar = m.sb("m_bar", [P, TT, HPG])
        m_row = m.sb("m_row", [P, TT, HPG])
        turn_in = m.sb("turn_in", [P, TT * (P + 1) + 4], BF16)
        shift = m.sb("shift", [P, 2, S], BF16)
        rsum = m.sb("rsum", [P, TT, 2, 1])
        ps_s = m.ps("ps_s", [P, 2, S])
        ps_st = m.ps("ps_st", [P, 2, S])
        ps_o = m.ps("ps_o", [P, 2, S])
        ps_back = m.ps("ps_back", [P, TT, 2, 2 * HD])
        ps_turn = m.ps("ps_turn", [P, TT * P], BF16)

        pair_in = [[m.sem(f"pair_in{p}{k}") for k in range(2)] for p in range(2)]
        v_in = m.sem("v_in")
        evacuated, backed = m.sem("evacuated"), m.sem("backed")
        s_done, s_reduced = m.sem("s_done"), m.sem("s_reduced")
        st_done, exp_done = m.sem("st_done"), m.sem("exp_done")
        pv_done, normed = m.sem("pv_done"), m.sem("normed")
        row_step, turn_ready, turned, shift_ready = m.sem("row_step"), m.sem("turn_ready"), m.sem("turned"), m.sem("shift_ready")
        recip_done, cleared = m.sem("recip_done"), m.sem("cleared")

        def slot(t, u):
            return t[:, bass.ds(u, 1), :].rearrange("p a n -> p (a n)")

        with nc.Block() as block:
            @block.gpsimd
            def _(pool):
                pool.memset(vu[:], 1.0)
                pool.memset(turn_in[:], 0.0)
                pool.memset(maxima[:], -SENTINEL).then_inc(cleared, 1)

                def gather_v(u, b, g, p):
                    need(pool, pv_done, 2 * (u - 1))
                    pool.tensor_copy(vu[:, p, :, :, 0:HD],
                                     c.v[:, bass.ds(b * TT, TT), g * P:(g + 1) * P].rearrange("p t (j w) -> p t j w", w=HD)
                                     ).then_inc(v_in, 1)

                pool.wait_ge(cleared, 1)
                for g in range(HG):
                    gather_v(g, 0, g, g % 2)
                with pool.Fori(1, B) as b:
                    for g in range(HG):
                        gather_v(HG * b + g, b, g, g % 2)

            @block.sync
            def _(sp):
                def load_unit(u, p, first):
                    for k in range(2):
                        if not first:
                            sp.wait_ge(st_done, NU * (u - 2) + 2 * TT * (k + 1))
                        for r in range(4):
                            for tile, which, part in ((q4, 0, r % 2), (k4, 1, r // 2)):
                                src = qk_dram[which, part, bass.ds(u, 1), 2 * HD * k:2 * HD * (k + 1)]
                                sp.dma_start(tile[HD * r:HD * (r + 1), p, 2 * k:2 * k + 2, :].bitcast(F32),
                                             src.rearrange("a (j p) n -> p (a j) n", p=HD)).then_inc(pair_in[p][k], 16)

                load_unit(0, 0, True)
                load_unit(1, 1, True)
                with sp.Fori(1, U // 2) as i:
                    for p in range(2):
                        load_unit(2 * i + p, p, False)

            def next_tiles(s):
                done = sum(AHEAD[:s])
                return range(done, done + AHEAD[s])

            @block.tensor
            def _(pe):
                def score(u, p, x, uses):
                    j, t = divmod(x, TT)
                    if t == 0 and j % 2 == 0:
                        pe.wait_ge(pair_in[p][j // 2], NDMA * uses)
                    need(pe, s_reduced, NU * u + x - 1)
                    pe.matmul(ps_s[:, x % 2, :], q4[:, p, j, t * P:(t + 1) * P], k4[:, p, j, :],
                              start=True, stop=True).then_inc(s_done, 1)

                def turn(u):
                    pe.wait_ge(turn_ready, u + 1)
                    for t in range(TT):
                        last = pe.transpose(ps_turn[:, t * P:(t + 1) * P], turn_in[:, t * P:(t + 1) * P], c.ident_bf[:])
                    last.then_inc(turned, 1)

                def weigh(u, p, k, kc):
                    if kc == 0:
                        pe.wait_ge(exp_done, NU * u + 2 * TT * (k + 1))
                        need(pe, evacuated, 2 * u + k - 1)
                        if k == 0:
                            pe.wait_ge(v_in, u + 1)
                    for h in range(2):
                        last = pe.matmul(ps_o[2 * HD * h:2 * HD * (h + 1), k, :], vu[:, p, kc, 2 * k + h, :],
                                         probs[:, 2 * k + h, kc, :], start=(kc == 0), stop=(kc == TT - 1))
                    if kc == TT - 1:
                        last.then_inc(pv_done, 1)

                def back(n):
                    pe.wait_ge(evacuated, n + 1)
                    need(pe, normed, n)
                    for t in range(TT):
                        last = pe.transpose(ps_back[:, t].rearrange("p h w -> p (h w)"), outT[:, t * P:(t + 1) * P], c.ident[:])
                    last.then_inc(backed, 1)

                def unit(u, p, uses, first=False, last=False):
                    for s in range(NU):
                        j, kc = divmod(s, TT)
                        k, r = divmod(s, 2 * TT)
                        if s == 0:
                            pe.wait_ge(shift_ready, u + 1)
                        need(pe, exp_done, NU * u + s - 1)
                        pe.matmul(ps_st[:, s % 2, :], c.window[:, j, kc, :], shift[:, p, :], start=True, stop=False)
                        pe.matmul(ps_st[:, s % 2, :], k4[:, p, j, kc * P:(kc + 1) * P], q4[:, p, j, :],
                                  start=False, stop=True).then_inc(st_done, 1)
                        if not last:
                            for x in next_tiles(s):
                                score(u + 1, 1 - p, x, uses + p)
                        if r % 2 == 0:
                            if k:
                                weigh(u, p, 0, r // 2)
                            elif not first:
                                weigh(u - 1, 1 - p, 1, r // 2)
                        if r == 3 and not first:
                            back(2 * u + k - 2)
                        if s == 14 and not last:
                            turn(u + 1)
                    if last:
                        for kc in range(TT):
                            weigh(u, p, 1, kc)
                        back(2 * u)
                        back(2 * u + 1)

                for x in range(NU):
                    score(0, 0, x, 1)
                turn(0)
                unit(0, 0, 1, first=True)
                with pe.Fori(0, U // 2 - 1) as i:
                    unit(2 * i + 1, 1, i + 1)
                    unit(2 * i + 2, 0, i + 2)
                unit(U - 1, 1, U // 2, last=True)

            @block.scalar
            def _(act):
                def take_shift(u, p):
                    act.wait_ge(turned, u + 1)
                    act.activation(shift[:, p, :], ps_turn[:], ACT.Copy).then_inc(shift_ready, 1)

                def evacuate(n, k):
                    act.wait_ge(pv_done, n + 1)
                    need(act, backed, n)
                    act.activation(outT[:], ps_o[:, k, :], ACT.Copy).then_inc(evacuated, 1)

                def unit(u, p, first=False, last=False):
                    for s in range(NU):
                        j, kc = divmod(s, TT)
                        k, r = divmod(s, 2 * TT)
                        act.wait_ge(st_done, NU * u + s + 1)
                        if r == 0:
                            need(act, pv_done, 2 * u + k - 1)
                        act.activation(probs[:, j, kc, :], ps_st[:, s % 2, :], ACT.Exp, scale=SCALE).then_inc(exp_done, 1)
                        if r == 1 and not first:
                            evacuate(2 * u + k - 2, k)
                        if s == 14 and not last:
                            take_shift(u + 1, 1 - p)
                    if last:
                        evacuate(2 * u, 0)
                        evacuate(2 * u + 1, 1)

                take_shift(0, 0)
                unit(0, 0, first=True)
                with act.Fori(0, U // 2 - 1) as i:
                    unit(2 * i + 1, 1)
                    unit(2 * i + 2, 0)
                unit(U - 1, 1, last=True)

            @block.vector
            def _(dve):
                by_tile = maxima[:, 0:TT * HPG * GW].rearrange("p (t j g) -> p t j g", j=HPG, g=GW)
                windows = maxima[:].rearrange("p (t x) -> p t x", t=TT)[:, :, 0:HPG * GW].rearrange(
                    "p t (j g) -> p t j g", g=GW)[:, :, :, 0:4]
                rows = turn_in[:, 0:TT * P].rearrange("p (t j r) -> p t j r", j=HPG, r=HD)
                bar_rows = turn_in[:, 2:2 + TT * (P + 1)].rearrange("p (t x) -> p t x", t=TT)[:, :, 0:P:HD]

                def reduce(u, x):
                    j, t = divmod(x, TT)
                    dve.wait_ge(s_done, NU * u + x + 1)
                    dve.tensor_reduce(by_tile[:, t, j, 1:9], ps_s[:, x % 2, :].rearrange("p (g n) -> p g n", n=S // 8),
                                      axis=AX.X, op=ALU.max).then_inc(s_reduced, 1)

                def row_maxima(u):
                    k = [0]

                    def step(ins):
                        k[0] += 1
                        ins.then_inc(row_step, 1)
                        dve.wait_ge(row_step, 6 * u + k[0])

                    bar = c.bar[:, :, bass.ds(HPG * u, HPG)]
                    dve.wait_ge(s_reduced, NU * u + NU)
                    dve.tensor_reduce(m_win[:].rearrange("p t j -> p t j"), windows, axis=AX.X, op=ALU.max)
                    step(dve.tensor_reduce(m_all[:], by_tile, axis=AX.X, op=ALU.max))
                    step(dve.tensor_tensor(m_bar[:], m_all[:], bar, ALU.add))
                    step(dve.tensor_tensor(m_row[:], m_bar[:], m_win[:], ALU.max))
                    need(dve, turned, u)
                    step(dve.tensor_scalar(rows[:, :, :, 0], m_row[:], -1.0, None, ALU.mult))
                    dve.scalar_tensor_tensor(rows[:, :, :, 1], m_row[:], -1.0, rows[:, :, :, 0],
                                             ALU.mult, ALU.subtract).then_inc(row_step, 1)
                    k[0] += 1
                    step(dve.tensor_copy(bar_rows, bar))
                    dve.sem_inc(turn_ready, 1)

                def normalise(u, k):
                    n = 2 * u + k
                    dve.wait_ge(backed, n + 1)
                    dve.reciprocal(rsum[:], ps_back[:, :, :, HD:HD + 1]).then_inc(recip_done, 1)
                    dve.wait_ge(recip_done, n + 1)
                    out = slot(c.attn, u).rearrange("p (t x) -> p t x", t=TT)[:, :, 2 * HD * k:2 * HD * (k + 1)]
                    dve.tensor_tensor(out.rearrange("p t (h w) -> p t h w", h=2), ps_back[:, :, :, 0:HD],
                                      rsum[:].to_broadcast([P, TT, 2, HD]), ALU.mult).then_inc(normed, 1)

                def unit(u, first=False, last=False):
                    for s in range(NU):
                        k, r = divmod(s, 2 * TT)
                        if not last:
                            for x in next_tiles(s):
                                reduce(u + 1, x)
                        if s == 12 and not last:
                            row_maxima(u + 1)
                        if r == 5 and not first:
                            normalise(u - 1, k)
                    if last:
                        normalise(u, 0)
                        normalise(u, 1)

                dve.wait_ge(cleared, 1)
                for x in range(NU):
                    reduce(0, x)
                row_maxima(0)
                unit(0, first=True)
                with dve.Fori(0, U // 2 - 1) as i:
                    unit(2 * i + 1)
                    unit(2 * i + 2)
                unit(U - 1, last=True)


EPS = 1e-5
C = 128
XSCALE = float(C) ** -0.5
E, FH = 8, 352
FC = 3
FCR = FH - 2 * P
WCOLS = 2 * DC * FH + FC * D
T = B * S
NT = T // P
MASKED = -1.0e30


def gate_cols(w, up, dc):
    return w[:, (up * DC + dc) * FH:(up * DC + dc + 1) * FH]


def down_cols(w, fc):
    return w[:, 2 * DC * FH + fc * D:2 * DC * FH + (fc + 1) * D]


def cross_and_shared(nc, c, x, mask, pad_mask, gate_w, sw_gate, sw_up, sw_down, x2_dram, table_dram):
    with ExitStack() as ctx:
        m = Memory(nc, ctx)
        sw_hi = m.sb("sw_hi", [P, 2, WCOLS], F32R)
        sw_lo = m.sb("sw_lo", [P, 2, WCOLS], F32R)
        with ExitStack() as ctx2:
            m2 = Memory(nc, ctx2)
            sw_raw = m2.sb("sw_raw", [P, 2, WCOLS])
            zeroed, loaded, hi_done = m.sem("sw_zeroed"), m.sem("sw_loaded"), m.sem("sw_hi_done")
            with nc.Block() as block:
                @block.sync
                def _(sp):
                    for k in range(2):
                        cols = slice(FH * k, FH * (k + 1))
                        for up, w in enumerate((sw_gate, sw_up)):
                            sp.dma_start(sw_raw[:, k, up * DC * FH:(up + 1) * DC * FH].rearrange("p (c h) -> p c h", h=FH),
                                         w.rearrange("(c p) h -> p c h", p=P)[:, :, cols]).then_inc(loaded, 16)
                        down = sw_raw[:, k, 2 * DC * FH:].rearrange("p (c d) -> p c d", d=D)
                        rows = sw_down[FH * k:FH * (k + 1), :]
                        sp.dma_start(down[:, 0:2, :], rows[0:2 * P].rearrange("(c p) d -> p c d", p=P)).then_inc(loaded, 16)
                        sp.dma_start(down[0:FCR, 2, :], rows[2 * P:FH]).then_inc(loaded, 16)

                @block.scalar
                def _(act):
                    act.wait_ge(zeroed, 1)
                    act.wait_ge(loaded, 128)
                    for k in range(2):
                        act.activation(sw_hi[:, k], sw_raw[:, k], ACT.Copy).then_inc(hi_done, 1)

                @block.vector
                def _(dve):
                    for k in range(2):
                        last = dve.memset(sw_raw[FCR:P, k, WCOLS - D:WCOLS], 0.0)
                    last.then_inc(zeroed, 1)
                    for k in range(2):
                        dve.wait_ge(hi_done, k + 1)
                        dve.tensor_tensor(sw_lo[:, k], sw_raw[:, k], sw_hi[:, k].bitcast(F32), ALU.subtract)

        am = m.sb("am", [P, TT, S])
        pm = m.sb("pm", [P, B, S])
        am8 = m.sb("am8", [P, TT, S], U8)
        pm8 = m.sb("pm8", [P, B, S], U8)
        gw = m.sb("gw", [P, DC, E])
        gw_hi = m.sb("gw_hi", [P, DC, E], F32R)
        gw_lo = m.sb("gw_lo", [P, DC, E], F32R)
        before = m.sb("before", [P, P], BF16)
        ones = m.sb("ones", [P, P], BF16)
        expert = m.sb("expert", [P, E])
        region = m.sb("region", [P, E])
        expert_i = m.sb("expert_i", [P, E], I32)
        token_i = m.sb("token_i", [P, NT], U32)
        token = m.sb("token", [P, 1], U32)
        half = m.sb("half", [P, 1])
        q_tile = m.sb("q_tile", [P, 2, 2, P], F32R)
        x_in = m.sb("x_tile", [P, 2, D])
        r1 = m.sb("r1", [P, 2, D])
        stats = m.sb("stats", [P, 2, 6])
        mv = m.sb("mv", [P, 2, 2])
        rstd = m.sb("rstd", [P, 2, 2])
        x1 = m.sb("x1", [P, 2, D])
        sc = m.sb("sc", [P, 2, D])
        small = m.sb("small", [P, 8])
        x2 = m.sb("x2", [P, 2, D])
        xT_hi = m.sb("x2T_hi", [P, DC, P], F32R)
        xT_lo = m.sb("x2T_lo", [P, DC, P], F32R)
        act_g = m.sb("act_g", [P, 2, FH])
        g = m.sb("g", [P, 2, FC * P])
        gT_hi = m.sb("gT_hi", [P, 2, FC * P], F32R)
        gT_lo = m.sb("gT_lo", [P, 2, FC * P], F32R)
        r_small = m.sb("r_small", [P, 4])
        r_exp = m.sb("r_exp", [P, E])
        score = m.sb("score", [P, E])
        top = m.sb("top", [P, E])
        top_i = m.sb("top_i", [P, E], U32)
        top_f = m.sb("top_f", [P, E])
        chosen = m.sb("chosen", [P, 2, E])
        both = m.sb("both", [P, E], BF16)
        both_sum = c.both_sum
        place = m.sb("place", [P, E])
        placed = m.sb("placed", [P, 2, E])
        slot_f = m.sb("slot_f", [P, 2])
        slot_u = m.sb("slot_u", [P, 2], U32)

        ps_sc = m.ps("ps_sc", [P, S])
        ps_xT = m.ps("ps_xT", [P, D])
        ps_r = m.ps("ps_r", [P, 2, E])
        ps_gu = m.ps("ps_gu", [P, 2, S])
        ps_gT = m.ps("ps_gT", [P, FC * P])
        ps_y = m.ps("ps_y", [P, D])

        names = ("masks_in gate_in const_step x_ld0 x_ld1 r1_done stats1 mv1 ve1 rstd1 x1_done q_tile_done sc_done "
                 "scaled masked0 masked nmax e_done guard0 guard sum_ok rinv r2_done stats2 mv2 ve2 rstd2 x2_done x2_st0 x2_st1 "
                 "x2_turned hi_done2 lo_done2 r_logits r_max r_e r_step rank_done slots_done scat token_done "
                 "g_done u_done silu_done g_ready gT_turned gT_hi_done gT_lo_done y_done y_out both_done setup").split()
        s = {k: m.sem("p4_" + k) for k in names}

        x_rows = x.rearrange("b (t p) d -> p (b t) d", p=P)
        x2_rows = x2_dram.rearrange("(n p) d -> p n d", p=P)

        def attn_tile(b, t):
            return c.attn[:, bass.ds(b * HG, HG), t * P:(t + 1) * P]

        def tiles(eng, one):
            for t in range(TT):
                one(t, 0, t, False)
            with eng.Fori(1, B - 1) as b:
                for t in range(TT):
                    one(b * TT + t, b, t, False)
            for t in range(TT):
                one((B - 1) * TT + t, B - 1, t, t == TT - 1)

        def following(n, b, t):
            return (n + 1, b, t + 1) if t < TT - 1 else (n + 1, b + 1, 0)

        with nc.Block() as block:
            @block.sync
            def _(sp):
                sp.dma_start(am8[:], mask.rearrange("(t p) k -> p t k", p=P)).then_inc(s["masks_in"], 16)
                sp.dma_start(pm8[:].rearrange("p b k -> p (b k)"),
                             pad_mask.rearrange("(a b) k -> a (b k)", a=1).to_broadcast([P, B * S])).then_inc(s["masks_in"], 16)
                sp.dma_start(gw[:], gate_w.rearrange("(c p) e -> p c e", p=P)).then_inc(s["gate_in"], 16)

                def load_x(n, t, first):
                    if not first:
                        sp.wait_ge(s["r1_done"], n - 1)
                    sp.dma_start(x_in[:, t % 2, :], x_rows[:, bass.ds(n, 1), :].rearrange("p a d -> p (a d)")).then_inc(s[f"x_ld{t % 2}"], 16)

                load_x(0, 0, True)
                load_x(1, 1, True)

                def one(n, b, t, last):
                    sp.wait_ge(s["x2_done"], n + 1)
                    sp.dma_start(x2_rows[:, bass.ds(n, 1), :].rearrange("p a d -> p (a d)"), x2[:, t % 2, :]).then_inc(s[f"x2_st{t % 2}"], 16)
                    if not (isinstance(n, int) and n + 2 >= NT):
                        load_x(n + 2, t, False)

                tiles(sp, one)
                for k in range(2):
                    sp.wait_ge(s[f"x2_st{k}"], 8 * NT)

            @block.gpsimd
            def _(pool):
                step = s["const_step"]
                pool.memset(before[:], 1.0)
                pool.memset(ones[:], 1.0)
                pool.memset(half[:], -0.5)
                pool.memset(both_sum[:], 0.0)
                pool.memset(g[:], 0.0)
                pool.iota(token_i[:], pattern=[[P, NT]], base=0, channel_multiplier=1)
                pool.iota(expert_i[:], pattern=[[1, E]], base=0, channel_multiplier=0).then_inc(step, 1)
                pool.wait_ge(step, 1)
                pool.affine_select(out=before[:], in_=before[:], compare_op=ALU.is_gt, fill=0.0, base=0,
                                   pattern=[[1, P]], channel_multiplier=-1)
                pool.tensor_copy(expert[:], expert_i[:]).then_inc(step, 1)
                pool.wait_ge(step, 2)
                pool.tensor_scalar(region[:], expert[:], float(T), None, ALU.mult).then_inc(step, 1)

                def first_half(n, b, t):
                    p = t % 2
                    need(pool, s["sc_done"], n - 1)
                    for k in range(2):
                        src = c.qk_ctx[0][k][:, bass.ds(n * P, P)].bitcast(F32)
                        last = pool.tensor_copy(q_tile[:, p, k, :], src)
                    last.then_inc(s["q_tile_done"], 1)
                    pool.wait_ge(s[f"x_ld{p}"], 32 * b + 16 * (t // 2) + 16)
                    need(pool, s["x2_done"], n - 1)
                    pool.tensor_tensor(r1[:, p, :].rearrange("p (g d) -> p g d", g=HG),
                                       x_in[:, p, :].rearrange("p (g d) -> p g d", g=HG), attn_tile(b, t), ALU.add).then_inc(s["r1_done"], 1)
                    root(n, 0, s["mv1"], s["ve1"], s["rstd1"])
                    pool.wait_ge(s["scaled"], n + 1)
                    pool.tensor_tensor(sc[:, p, :], sc[:, p, :], am[:, t, :], ALU.add).then_inc(s["masked0"], 1)
                    wait_apart(pool, s["masked0"], n + 1, c.pool_passed)
                    pool.tensor_tensor(sc[:, p, :], sc[:, p, :], pm[:, bass.ds(b, 1), :].rearrange("p a k -> p (a k)"), ALU.add).then_inc(s["masked"], 1)
                    wait_apart(pool, s["nmax"], n + 1, c.pool_passed)
                    pool.tensor_scalar(small[:, 2:3], small[:, 0:1], -0.1 * MASKED, 0.0, ALU.subtract, ALU.max).then_inc(s["guard0"], 1)
                    wait_apart(pool, s["guard0"], n + 1, c.pool_passed)
                    pool.tensor_scalar(small[:, 3:4], small[:, 2:3], 1.0e38, 0.0, ALU.mult, ALU.mult).then_inc(s["guard"], 1)
                    root(n, 1, s["mv2"], s["ve2"], s["rstd2"])

                def root(n, k, ready, mid, done):
                    wait_apart(pool, ready, n + 1, c.pool_passed)
                    pool.tensor_scalar(rstd[:, k, 0:1], mv[:, k, 1:2], EPS, None, ALU.add).then_inc(mid, 1)
                    pool.wait_ge(mid, n + 1)
                    pool.tensor_tensor(rstd[:, k, 1:2], rstd[:, k, 0:1], half[:], ALU.pow).then_inc(done, 1)

                def send(n):
                    need(pool, s["scat"], 32 * n)
                    pool.tensor_copy(token[:], token_i[:, bass.ds(n, 1)]).then_inc(s["token_done"], 1)
                    pool.wait_ge(s["token_done"], n + 1)
                    wait_apart(pool, s["slots_done"], n + 1, c.pool_passed)
                    for k in range(2):
                        pool.indirect_dma_start(out=table_dram[:], out_offset=bass.IndirectOffsetOnAxis(ap=slot_u[:, k:k + 1], axis=0),
                                                in_=token[:], in_offset=None).then_inc(s["scat"], 16)

                pool.wait_ge(s["setup"], 1)
                first_half(0, 0, 0)

                def one(n, b, t, last):
                    if not last:
                        first_half(*following(n, b, t))
                    send(n)

                tiles(pool, one)
                pool.wait_ge(s["scat"], 32 * NT)

            @block.scalar
            def _(act):
                act.wait_ge(s["gate_in"], 16)
                act.activation(gw_hi[:], gw[:], ACT.Copy).then_inc(s["gate_in"], 1)

                def soft(n, t):
                    act.wait_ge(s["nmax"], n + 1)
                    act.activation(sc[:, t % 2, :], sc[:, t % 2, :], ACT.Exp, bias=small[:, 0:1], accum_out=small[:, 1:2]).then_inc(s["e_done"], 1)

                def one(n, b, t, last):
                    act.wait_ge(s["x2_turned"], n + 1)
                    act.activation(xT_hi[:].rearrange("p c k -> p (c k)"), ps_xT[:], ACT.Copy).then_inc(s["hi_done2"], 1)
                    for k in range(2):
                        act.wait_ge(s["g_done"], 2 * n + k + 1)
                        need(act, s["g_ready"], 2 * n + k - 1)
                        act.activation(act_g[:, k, :], ps_gu[:, 0, 0:FH], ACT.Silu).then_inc(s["silu_done"], 1)
                        if k == 0:
                            act.wait_ge(s["r_max"], n + 1)
                            act.activation(r_exp[:], ps_r[:, 0, :], ACT.Exp, bias=r_small[:, 0:1], accum_out=r_small[:, 1:2]).then_inc(s["r_e"], 1)
                        act.wait_ge(s["gT_turned"], 2 * n + k + 1)
                        act.activation(gT_hi[:, k, :], ps_gT[:], ACT.Copy).then_inc(s["gT_hi_done"], 1)
                        if k == 0 and not last:
                            soft(n + 1, t + 1)

                soft(0, 0)
                tiles(act, one)

            @block.vector
            def _(dve):
                dve.wait_ge(s["masks_in"], 32)
                dve.tensor_scalar(am[:], am8[:], MASKED, None, ALU.mult)
                dve.tensor_scalar(pm[:], pm8[:], MASKED, None, ALU.mult)
                dve.wait_ge(s["gate_in"], 17)
                dve.tensor_tensor(gw_lo[:], gw[:], gw_hi[:].bitcast(F32), ALU.subtract).then_inc(s["setup"], 1)
                dve.wait_ge(s["const_step"], 3)

                def norm(n, p, src, dst, k, ready, mid, rooted, done):
                    dve.bn_stats(stats[:, k, :], src).then_inc(ready, 1)
                    wait_apart(dve, ready, n + 1, c.dve_passed)
                    dve.bn_aggr(mv[:, k, :], stats[:, k, :]).then_inc(mid, 1)
                    dve.wait_ge(rooted, n + 1)
                    dve.tensor_scalar(dst, src, mv[:, k, 0:1], rstd[:, k, 1:2], ALU.subtract, ALU.mult).then_inc(done, 1)

                def before_soft(n, b, t):
                    p = t % 2
                    dve.wait_ge(s["r1_done"], n + 1)
                    norm(n, p, r1[:, p, :], x1[:, p, :], 0, s["stats1"], s["mv1"], s["rstd1"], s["x1_done"])
                    dve.wait_ge(s["sc_done"], n + 1)
                    dve.wait_ge(s["x1_done"], n + 1)
                    dve.scalar_tensor_tensor(sc[:, p, :], ps_sc[:], XSCALE, x1[:, p, :], ALU.mult, ALU.mult).then_inc(s["scaled"], 1)
                    dve.wait_ge(s["masked"], n + 1)
                    dve.tensor_reduce(small[:, 0:1], sc[:, p, :], axis=AX.X, op=ALU.max, negate=True).then_inc(s["nmax"], 1)

                def after_soft(n, b, t):
                    p = t % 2
                    dve.wait_ge(s["e_done"], n + 1)
                    dve.wait_ge(s["guard"], n + 1)
                    dve.tensor_tensor(small[:, 4:5], small[:, 1:2], small[:, 3:4], ALU.add).then_inc(s["sum_ok"], 1)
                    dve.wait_ge(s["sum_ok"], n + 1)
                    dve.reciprocal(small[:, 5:6], small[:, 4:5]).then_inc(s["rinv"], 1)
                    dve.wait_ge(s["rinv"], n + 1)
                    dve.scalar_tensor_tensor(r1[:, p, :], sc[:, p, :], small[:, 5:6], x1[:, p, :], ALU.mult, ALU.add).then_inc(s["r2_done"], 1)
                    dve.wait_ge(s["r2_done"], n + 1)
                    need(dve, s[f"x2_st{p}"], 32 * b + 16 * (t // 2))
                    norm(n, p, r1[:, p, :], x2[:, p, :], 1, s["stats2"], s["mv2"], s["rstd2"], s["x2_done"])

                RSTEPS = 11

                def route(n, t):
                    k = [0]

                    def step(ins):
                        k[0] += 1
                        ins.then_inc(s["r_step"], 1)
                        dve.wait_ge(s["r_step"], RSTEPS * n + k[0])

                    dve.wait_ge(s["r_logits"], n + 1)
                    dve.tensor_reduce(r_small[:, 0:1], ps_r[:, 0, :], axis=AX.X, op=ALU.max, negate=True).then_inc(s["r_max"], 1)
                    dve.wait_ge(s["r_e"], n + 1)
                    step(dve.reciprocal(r_small[:, 2:3], r_small[:, 1:2]))
                    step(dve.tensor_scalar(score[:], r_exp[:], r_small[:, 2:3], None, ALU.mult))
                    dve.sem_inc(c.dve_passed, 1)
                    step(dve.max(top[:], score[:]))
                    dve.tensor_copy(c.weights[:, bass.ds(n, 1), :].rearrange("p a k -> p (a k)"), top[:, 0:2])
                    step(dve.max_index(top_i[:], top[:], score[:]))
                    step(dve.tensor_copy(top_f[:], top_i[:]))
                    dve.tensor_copy(c.choice[:, bass.ds(n, 1), :].rearrange("p a k -> p (a k)"), top_f[:, 0:2])
                    dve.tensor_scalar(chosen[:, 0, :], expert[:], top_f[:, 0:1], None, ALU.is_equal)
                    step(dve.tensor_scalar(chosen[:, 1, :], expert[:], top_f[:, 1:2], None, ALU.is_equal))
                    dve.tensor_tensor(both[:], chosen[:, 0, :], chosen[:, 1, :], ALU.add).then_inc(s["both_done"], 1)
                    dve.wait_ge(s["rank_done"], n + 1)
                    step(dve.tensor_tensor(place[:], ps_r[:, 1, :], region[:], ALU.add))
                    step(dve.tensor_tensor(both_sum[:], both_sum[:], both[:], ALU.add))
                    step(dve.tensor_tensor(placed[:], chosen[:], place[:].rearrange("p (a e) -> p a e", a=1).to_broadcast([P, 2, E]), ALU.mult))
                    step(dve.tensor_reduce(slot_f[:], placed[:], axis=AX.X, op=ALU.add))
                    dve.tensor_copy(c.listed[:, bass.ds(n, 1), :].rearrange("p a k -> p (a k)"), slot_f[:])
                    need(dve, s["scat"], 32 * n)
                    step(dve.tensor_copy(slot_u[:], slot_f[:]))
                    dve.sem_inc(s["slots_done"], 1)

                def one(n, b, t, last):
                    dve.wait_ge(s["hi_done2"], n + 1)
                    dve.tensor_tensor(xT_lo[:].rearrange("p c k -> p (c k)"), ps_xT[:], xT_hi[:].rearrange("p c k -> p (c k)").bitcast(F32),
                                      ALU.subtract).then_inc(s["lo_done2"], 1)
                    for k in range(2):
                        if k == 0:
                            if not last:
                                before_soft(*following(n, b, t))
                        elif not last:
                            after_soft(*following(n, b, t))
                        dve.wait_ge(s["u_done"], 2 * n + k + 1)
                        dve.wait_ge(s["silu_done"], 2 * n + k + 1)
                        dve.tensor_tensor(g[:, k, 0:FH], act_g[:, k, :], ps_gu[:, 1, 0:FH], ALU.mult).then_inc(s["g_ready"], 1)
                        if k == 0:
                            route(n, t)
                        dve.wait_ge(s["gT_hi_done"], 2 * n + k + 1)
                        dve.tensor_tensor(gT_lo[:, k, :], ps_gT[:], gT_hi[:, k, :].bitcast(F32), ALU.subtract).then_inc(s["gT_lo_done"], 1)
                    dve.wait_ge(s["y_done"], n + 1)
                    dve.tensor_tensor(attn_tile(b, t), ps_y[:].rearrange("p (g d) -> p g d", g=HG),
                                      x2[:, t % 2, :].rearrange("p (g d) -> p g d", g=HG), ALU.add).then_inc(s["y_out"], 1)

                before_soft(0, 0, 0)
                after_soft(0, 0, 0)
                tiles(dve, one)

            @block.tensor
            def _(pe):
                def scores(n, b, t):
                    p = t % 2
                    pe.wait_ge(s["q_tile_done"], n + 1)
                    need(pe, s["scaled"], n)
                    for k, (a, z) in enumerate(((0, 0), (0, 1), (1, 0))):
                        last = pe.matmul(ps_sc[:], q_tile[:, p, a, :], c.qk_ctx[1][z][:, bass.ds(b * S, S)],
                                         start=(k == 0), stop=(k == 2))
                    last.then_inc(s["sc_done"], 1)

                def passes(out, stationary, moving, chunks):
                    for q in range(chunks):
                        for k, (a, z) in enumerate(((0, 0), (0, 1), (1, 0))):
                            last = pe.matmul(out, stationary[a](q), moving[z](q), start=(q == 0 and k == 0),
                                             stop=(q == chunks - 1 and k == 2))
                    return last

                xT = [lambda q, w=w: w[:, q, :] for w in (xT_hi, xT_lo)]

                def gate(n, k):
                    need(pe, s["silu_done"], 2 * n + k)
                    passes(ps_gu[:, 0, 0:FH], xT, [lambda q, w=w: gate_cols(w[:, k, :], 0, q) for w in (sw_hi, sw_lo)], DC).then_inc(s["g_done"], 1)

                def up(n, k):
                    need(pe, s["g_ready"], 2 * n + k)
                    passes(ps_gu[:, 1, 0:FH], xT, [lambda q, w=w: gate_cols(w[:, k, :], 1, q) for w in (sw_hi, sw_lo)], DC).then_inc(s["u_done"], 1)

                def turn(n, k):
                    pe.wait_ge(s["g_ready"], 2 * n + k + 1)
                    need(pe, s["gT_lo_done"], 2 * n + k)
                    for q in range(FC):
                        last = pe.transpose(ps_gT[:, q * P:(q + 1) * P], g[:, k, q * P:(q + 1) * P], c.ident[:])
                    last.then_inc(s["gT_turned"], 1)

                def down(n, k):
                    pe.wait_ge(s["gT_lo_done"], 2 * n + k + 1)
                    if k == 0:
                        need(pe, s["y_out"], n)
                    gT = [lambda q, w=w: w[:, k, q * P:(q + 1) * P] for w in (gT_hi, gT_lo)]
                    ws = [lambda q, w=w: down_cols(w[:, k, :], q) for w in (sw_hi, sw_lo)]
                    for q in range(FC):
                        for j, (a, z) in enumerate(((0, 0), (0, 1), (1, 0))):
                            last = pe.matmul(ps_y[:], gT[a](q), ws[z](q), start=(k == 0 and q == 0 and j == 0),
                                             stop=(k == 1 and q == FC - 1 and j == 2))
                    if k == 1:
                        last.then_inc(s["y_done"], 1)

                def router(n):
                    need(pe, s["slots_done"], n)
                    passes(ps_r[:, 0, :], xT, [lambda q, w=w: w[:, q, :] for w in (gw_hi, gw_lo)], DC).then_inc(s["r_logits"], 1)

                def ranks(n):
                    pe.wait_ge(s["both_done"], n + 1)
                    pe.matmul(ps_r[:, 1, :], before[:], both[:], start=True, stop=False)
                    pe.matmul(ps_r[:, 1, :], ones[:], both_sum[:], start=False, stop=True).then_inc(s["rank_done"], 1)

                def one(n, b, t, last):
                    pe.wait_ge(s["x2_done"], n + 1)
                    for q in range(DC):
                        z = pe.transpose(ps_xT[:, q * P:(q + 1) * P], x2[:, t % 2, q * P:(q + 1) * P], c.ident[:])
                    z.then_inc(s["x2_turned"], 1)
                    if not last:
                        scores(*following(n, b, t))
                    pe.wait_ge(s["lo_done2"], n + 1)
                    gate(n, 0)
                    up(n, 0)
                    router(n)
                    gate(n, 1)
                    turn(n, 0)
                    ranks(n)
                    up(n, 1)
                    down(n, 0)
                    turn(n, 1)
                    down(n, 1)

                pe.wait_ge(s["setup"], 1)
                pe.wait_ge(s["const_step"], 3)
                scores(0, 0, 0)
                tiles(pe, one)


NJ = 2 * T // P + E - 1
ROWS = E * T + NJ * P


def plan(nc, c):
    with ExitStack() as ctx:
        m = Memory(nc, ctx)
        ones = m.sb("plan_ones", [P, P], BF16)
        count = m.sb("count", [P, E])
        at_i = m.sb("at_i", [P, NT], I32)
        at = m.sb("at", [P, NT])
        more = m.sb("more", [P, E, NT])
        length = m.sb("length", [P, E])
        end = m.sb("end", [P, E])
        tile_i = m.sb("tile_i", [P, NJ], I32)
        tile = m.sb("tile", [P, NJ])
        past = m.sb("past", [P, NJ, E])
        gone = m.sb("gone", [P, NJ, E])
        e_of = m.sb("e_of", [P, NJ])
        start = m.sb("start", [P, NJ])
        row = m.sb("row", [P, NJ])
        shift = m.sb("shift_e", [P, E])
        is_e = m.sb("is_e", [P, NT * 2, E])
        moved = m.sb("moved", [P, NT * 2])
        ps_count = m.ps("ps_count", [P, E])
        built, counted, step = m.sem("plan_built"), m.sem("counted"), m.sem("plan_step")
        with nc.Block() as block:
            @block.gpsimd
            def _(pool):
                pool.memset(ones[:], 1.0)
                pool.iota(at_i[:], pattern=[[P, NT]], base=0, channel_multiplier=0)
                pool.iota(tile_i[:], pattern=[[1, NJ]], base=0, channel_multiplier=0).then_inc(built, 1)

            @block.tensor
            def _(pe):
                pe.wait_ge(built, 1)
                pe.matmul(ps_count[:], ones[:], c.both_sum[:], start=True, stop=True).then_inc(counted, 1)

            @block.vector
            def _(dve):
                k = [0]

                def link(ins):
                    k[0] += 1
                    ins.then_inc(step, 1)
                    dve.wait_ge(step, k[0])

                dve.wait_ge(built, 1)
                dve.tensor_copy(at[:], at_i[:])
                link(dve.tensor_copy(tile[:], tile_i[:]))
                dve.wait_ge(counted, 1)
                link(dve.tensor_copy(count[:], ps_count[:]))
                link(dve.tensor_tensor(more[:], count[:].rearrange("p (e a) -> p e a", a=1).to_broadcast([P, E, NT]),
                                       at[:].rearrange("p (a n) -> p a n", a=1).to_broadcast([P, E, NT]), ALU.is_gt))
                link(dve.tensor_reduce(length[:], more[:], axis=AX.X, op=ALU.add))
                link(dve.tensor_copy(end[:], length[:]))
                for e in range(1, E):
                    link(dve.tensor_tensor(end[:, e:e + 1], end[:, e:e + 1], end[:, e - 1:e], ALU.add))
                link(dve.tensor_tensor(past[:], tile[:].rearrange("p (j a) -> p j a", a=1).to_broadcast([P, NJ, E]),
                                       end[:].rearrange("p (a e) -> p a e", a=1).to_broadcast([P, NJ, E]), ALU.is_ge))
                dve.tensor_tensor(gone[:], past[:], length[:].rearrange("p (a e) -> p a e", a=1).to_broadcast([P, NJ, E]), ALU.mult)
                link(dve.tensor_reduce(e_of[:], past[:], axis=AX.X, op=ALU.add))
                link(dve.tensor_reduce(start[:], gone[:], axis=AX.X, op=ALU.add))
                link(dve.tensor_tensor(row[:], tile[:], start[:], ALU.subtract))
                link(dve.tensor_scalar(row[:], row[:], float(P), None, ALU.mult))
                link(dve.scalar_tensor_tensor(row[:], e_of[:], float(T), row[:], ALU.mult, ALU.add))
                dve.tensor_copy(c.first_row[:], row[0:1, :])
                link(dve.tensor_tensor(shift[:], end[:], length[:], ALU.subtract))
                link(dve.tensor_scalar(shift[:], shift[:], float(P), None, ALU.mult))
                link(dve.scalar_tensor_tensor(shift[:], tile[:, 0:E], -float(T), shift[:], ALU.mult, ALU.add))
                link(dve.tensor_tensor(is_e[:], c.choice[:].rearrange("p n (k a) -> p (n k) a", a=1).to_broadcast([P, NT * 2, E]),
                                       tile[:, 0:E].rearrange("p (a e) -> p a e", a=1).to_broadcast([P, NT * 2, E]), ALU.is_equal))
                link(dve.tensor_tensor(is_e[:], is_e[:], shift[:].rearrange("p (a e) -> p a e", a=1).to_broadcast([P, NT * 2, E]), ALU.mult))
                link(dve.tensor_reduce(moved[:], is_e[:], axis=AX.X, op=ALU.add))
                dve.tensor_tensor(c.slots[:].rearrange("p n k -> p (n k)"), c.listed[:].rearrange("p n k -> p (n k)"), moved[:], ALU.add)
                dve.tensor_scalar(c.expert_of[:], e_of[0:1, :], float(E - 1), None, ALU.min)


def experts(nc, c, w_gate, w_up, w_down, x2_dram, table_dram, y_dram):
    with ExitStack() as ctx:
        m = Memory(nc, ctx)
        w = m.sb("w_all", [P, E * WCOLS])
        who = m.sb("who", [P, 2, 1], U32)
        xg = m.sb("xg", [P, 2, D])
        xT = m.sb("xgT", [P, 2, D])
        act_g = m.sb("e_act", [P, 2, FH])
        g = m.sb("e_g", [P, 2, FC * P])
        gT = m.sb("e_gT", [P, 2, FC * P])
        y = m.sb("e_y", [P, 2, D])
        ps_xT = m.ps("e_ps_xT", [P, D])
        ps_g = m.ps("e_ps_g", [P, S])
        ps_u = m.ps("e_ps_u", [P, S])
        ps_gT = m.ps("e_ps_gT", [P, FC * P])
        ps_y = m.ps("e_ps_y", [P, D])
        names = "w_in who0 who1 x_in0 x_in1 turned xT_done g_done silu_done u_done g_ready gT_turned gT_done y_done y_out y_st0 y_st1 padded".split()
        s = {k: m.sem("e_" + k) for k in names}
        top = E * T + (NJ - 1) * P

        def pairs(eng, one, first, last):
            assert first % 2 == 1 and (last - first) % 2 == 1
            one(first, 1)
            one(first + 1, 0)
            with eng.Fori(1, (last - first + 1) // 2) as i:
                one(2 * i + first, 1)
                one(2 * i + first + 1, 0)

        with nc.Block() as block:
            @block.sync
            def _(sp):
                def list_in(j, p):
                    need(sp, s[f"x_in{p}"], 16 * ((j - p) // 2) if isinstance(j, int) else 8 * (j - p))
                    row = sp.value_load(c.first_row[0:1, bass.ds(j, 1)], min_val=0, max_val=top)
                    sp.dma_start(who[:, p, :], table_dram[bass.ds(row, P), :], allow_slow_non_contiguous=True).then_inc(s[f"who{p}"], 16)

                def weights_in(e):
                    base = e * WCOLS
                    src = [w_gate[e].rearrange("(c p) h -> p c h", p=P), w_up[e].rearrange("(c p) h -> p c h", p=P)]
                    for up in range(2):
                        sp.dma_start(w[:, base + up * DC * FH:base + (up + 1) * DC * FH].rearrange("p (c h) -> p c h", h=FH),
                                     src[up]).then_inc(s["w_in"], 16)
                    down = w[:, base + 2 * DC * FH:base + WCOLS].rearrange("p (c d) -> p c d", d=D)
                    sp.dma_start(down[:, 0:2, :], w_down[e, 0:2 * P, :].rearrange("(c p) d -> p c d", p=P)).then_inc(s["w_in"], 16)
                    sp.dma_start(down[0:FCR, 2, :], w_down[e, 2 * P:FH, :]).then_inc(s["w_in"], 16)

                list_in(0, 0)
                list_in(1, 1)
                for e in range(E):
                    if e:
                        sp.wait_ge(s["w_in"], 64 * e)
                    weights_in(e)
                    list_in(e + 2, e % 2)
                first = E + 2
                with sp.Fori(0, (NJ - first) // 2) as i:
                    list_in(2 * i + first, 0)
                    list_in(2 * i + first + 1, 1)
                if (NJ - first) % 2:
                    list_in(NJ - 1, 0)

            @block.gpsimd
            def _(pool):
                def gather(j, p):
                    pool.wait_ge(s[f"who{p}"], 16 * ((j - p) // 2) + 16 if isinstance(j, int) else 8 * (j - p) + 16)
                    need(pool, s["turned"], j - 1)
                    pool.sem_inc(c.pool_passed, 1)
                    pool.indirect_dma_start(out=xg[:, p, :], out_offset=None, in_=x2_dram[:],
                                            in_offset=bass.IndirectOffsetOnAxis(ap=who[:, p, :], axis=0)).then_inc(s[f"x_in{p}"], 16)

                pool.memset(g[:], 0.0).then_inc(s["padded"], 1)
                gather(0, 0)
                pairs(pool, gather, 1, NJ - 1)

            @block.scalar
            def _(act):
                def x_out(j, p):
                    act.wait_ge(s["turned"], j + 1)
                    act.activation(xT[:, p, :], ps_xT[:], ACT.Copy).then_inc(s["xT_done"], 1)

                def silu(j, p):
                    act.wait_ge(s["g_done"], j + 1)
                    act.activation(act_g[:, p, :], ps_g[:, 0:FH], ACT.Silu).then_inc(s["silu_done"], 1)

                def y_store(j, p):
                    act.wait_ge(s["y_done"], j + 1)
                    need(act, s[f"y_st{p}"], 16 * ((j - p) // 2) if isinstance(j, int) else 8 * (j - p))
                    act.activation(y[:, p, :], ps_y[:], ACT.Copy).then_inc(s["y_out"], 1)
                    act.wait_ge(s["y_out"], j + 1)
                    act.dma_start(y_dram[bass.ds(j * P, P), :], y[:, p, :]).then_inc(s[f"y_st{p}"], 16)

                def one(j, p, first=False, last=False):
                    if not last:
                        x_out(j + 1, 1 - p)
                    silu(j, p)
                    if not first:
                        y_store(j - 1, 1 - p)

                x_out(0, 0)
                one(0, 0, first=True)
                pairs(act, one, 1, NJ - 3)
                one(NJ - 2, 1)
                one(NJ - 1, 0, last=True)
                y_store(NJ - 1, 0)
                act.wait_ge(s["y_st0"], 16 * ((NJ + 1) // 2))
                act.wait_ge(s["y_st1"], 16 * (NJ // 2))

            @block.vector
            def _(dve):
                def multiply(j, p):
                    dve.wait_ge(s["u_done"], j + 1)
                    dve.wait_ge(s["silu_done"], j + 1)
                    dve.tensor_tensor(g[:, p, 0:FH], act_g[:, p, :], ps_u[:, 0:FH], ALU.mult).then_inc(s["g_ready"], 1)

                def gT_out(j, p):
                    dve.wait_ge(s["gT_turned"], j + 1)
                    dve.tensor_copy(gT[:, p, :], ps_gT[:]).then_inc(s["gT_done"], 1)

                def one(j, p, first=False):
                    if not first:
                        gT_out(j - 1, 1 - p)
                    multiply(j, p)

                dve.wait_ge(s["padded"], 1)
                one(0, 0, first=True)
                pairs(dve, one, 1, NJ - 1)
                gT_out(NJ - 1, 0)

            @block.tensor
            def _(pe):
                def weights_of(j):
                    e = pe.value_load(c.expert_of[0:1, bass.ds(j, 1)], min_val=0, max_val=E - 1)
                    pe.wait_ge(s["w_in"], 64 * e + 64)
                    return e * WCOLS

                def x_turn(j, p):
                    pe.wait_ge(s[f"x_in{p}"], 16 * ((j - p) // 2) + 16 if isinstance(j, int) else 8 * (j - p) + 16)
                    need(pe, s["xT_done"], j)
                    for q in range(DC):
                        last = pe.transpose(ps_xT[:, q * P:(q + 1) * P], xg[:, p, q * P:(q + 1) * P], c.ident[:])
                    last.then_inc(s["turned"], 1)

                def hidden(j, p, base, up):
                    if not up:
                        pe.wait_ge(s["xT_done"], j + 1)
                    need(pe, s["g_ready"] if up else s["silu_done"], j)
                    for q in range(DC):
                        last = pe.matmul((ps_u if up else ps_g)[:, 0:FH], xT[:, p, q * P:(q + 1) * P],
                                         w[:, bass.ds(base + (up * DC + q) * FH, FH)], start=(q == 0), stop=(q == DC - 1))
                    last.then_inc(s["u_done"] if up else s["g_done"], 1)

                def g_turn(j, p):
                    pe.wait_ge(s["g_ready"], j + 1)
                    need(pe, s["gT_done"], j)
                    for q in range(FC):
                        last = pe.transpose(ps_gT[:, q * P:(q + 1) * P], g[:, p, q * P:(q + 1) * P], c.ident[:])
                    last.then_inc(s["gT_turned"], 1)

                def down(j, p, base):
                    pe.wait_ge(s["gT_done"], j + 1)
                    need(pe, s["y_out"], j)
                    for q in range(FC):
                        rows = P if q < FC - 1 else FCR
                        last = pe.matmul(ps_y[:], gT[0:rows, p, q * P:(q + 1) * P],
                                         w[0:rows, bass.ds(base + 2 * DC * FH + q * D, D)], start=(q == 0), stop=(q == FC - 1))
                    last.then_inc(s["y_done"], 1)

                def one(j, p, first=False, last=False):
                    if not last:
                        x_turn(j + 1, 1 - p)
                    base = weights_of(j)
                    hidden(j, p, base, 0)
                    if not first:
                        g_turn(j - 1, 1 - p)
                    hidden(j, p, base, 1)
                    if not first:
                        down(j - 1, 1 - p, weights_of(j - 1))

                x_turn(0, 0)
                one(0, 0, first=True)
                pairs(pe, one, 1, NJ - 3)
                one(NJ - 2, 1)
                one(NJ - 1, 0, last=True)
                g_turn(NJ - 1, 0)
                down(NJ - 1, 0, weights_of(NJ - 1))


def combine(nc, c, y_dram, out):
    with ExitStack() as ctx:
        m = Memory(nc, ctx)
        place = m.sb("place_now", [P, 2, 2, 1], U32)
        yy = m.sb("yy", [P, 2, 2, D])
        r3 = m.sb("r3", [P, 2, 2, D])
        stats = m.sb("stats3", [P, 6])
        mv = m.sb("mv3", [P, 2])
        rstd = m.sb("rstd3", [P, 2])
        half = m.sb("half3", [P, 1])
        o = m.sb("o", [P, 2, D])
        names = "half place y_in0 y_in1 add0 add1 stats mv ve rstd o_done o_st0 o_st1".split()
        s = {k: m.sem("c_" + k) for k in names}
        out_rows = out.rearrange("b (t p) d -> p (b t) d", p=P)

        def tiles(eng, one):
            for t in range(2):
                one(t, 0, t, True)
            for t in range(2, TT):
                one(t, 0, t, False)
            with eng.Fori(1, B) as b:
                for t in range(TT):
                    one(b * TT + t, b, t, False)

        def uses(b, t):
            return 2 * b + t // 2

        with nc.Block() as block:
            @block.gpsimd
            def _(pool):
                pool.memset(half[:], -0.5).then_inc(s["half"], 1)
                pool.wait_ge(s["half"], 1)

                def fetch(n, b, t, fresh):
                    p = t % 2
                    if not fresh:
                        pool.wait_ge(s["add1"], n - 1)
                        pool.wait_ge(s[f"y_in{p}"], 32 * uses(b, t))
                    for k in range(2):
                        last = pool.tensor_copy(place[:, p, k, :], c.slots[:, bass.ds(n, 1), k:k + 1].rearrange("p a k -> p (a k)"))
                    last.then_inc(s["place"], 1)
                    wait_apart(pool, s["place"], n + 1, c.pool_passed)
                    for k in range(2):
                        pool.indirect_dma_start(out=yy[:, p, k, :], out_offset=None, in_=y_dram[:],
                                                in_offset=bass.IndirectOffsetOnAxis(ap=place[:, p, k, :], axis=0)).then_inc(s[f"y_in{p}"], 16)

                def root(n):
                    wait_apart(pool, s["mv"], n + 1, c.pool_passed)
                    pool.tensor_scalar(rstd[:, 0:1], mv[:, 1:2], EPS, None, ALU.add).then_inc(s["ve"], 1)
                    pool.wait_ge(s["ve"], n + 1)
                    pool.tensor_tensor(rstd[:, 1:2], rstd[:, 0:1], half[:], ALU.pow).then_inc(s["rstd"], 1)

                fetch(0, 0, 0, True)
                fetch(1, 0, 1, True)
                with pool.Fori(0, B - 1) as b:
                    for t in range(TT):
                        root(b * TT + t)
                        nb, nt = (b, t + 2) if t < 2 else (b + 1, t - 2)
                        fetch(b * TT + t + 2, nb, nt, False)
                for t in range(TT):
                    n = (B - 1) * TT + t
                    root(n)
                    if t < 2:
                        fetch(n + 2, B - 1, t + 2, False)

            @block.vector
            def _(dve):
                dve.wait_ge(s["half"], 1)

                def one(n, b, t, fresh):
                    p = t % 2
                    base = c.attn[:, bass.ds(b * HG, HG), t * P:(t + 1) * P]
                    wt = [c.weights[:, bass.ds(n, 1), k:k + 1].rearrange("p a k -> p (a k)") for k in range(2)]
                    dve.wait_ge(s[f"y_in{p}"], 32 * uses(b, t) + 32)
                    dve.scalar_tensor_tensor(r3[:, p, 0, :].rearrange("p (g d) -> p g d", g=HG), yy[:, p, 0, :].rearrange("p (g d) -> p g d", g=HG),
                                             wt[0], base, ALU.mult, ALU.add).then_inc(s["add0"], 1)
                    dve.wait_ge(s["add0"], n + 1)
                    dve.scalar_tensor_tensor(r3[:, p, 1, :], yy[:, p, 1, :], wt[1], r3[:, p, 0, :], ALU.mult, ALU.add).then_inc(s["add1"], 1)
                    dve.wait_ge(s["add1"], n + 1)
                    dve.bn_stats(stats[:], r3[:, p, 1, :]).then_inc(s["stats"], 1)
                    wait_apart(dve, s["stats"], n + 1, c.dve_passed)
                    dve.bn_aggr(mv[:], stats[:]).then_inc(s["mv"], 1)
                    dve.wait_ge(s["rstd"], n + 1)
                    if not fresh:
                        dve.wait_ge(s[f"o_st{p}"], 16 * uses(b, t))
                    dve.tensor_scalar(o[:, p, :], r3[:, p, 1, :], mv[:, 0:1], rstd[:, 1:2], ALU.subtract, ALU.mult).then_inc(s["o_done"], 1)

                tiles(dve, one)

            @block.sync
            def _(sp):
                def one(n, b, t, fresh):
                    sp.wait_ge(s["o_done"], n + 1)
                    sp.dma_start(out_rows[:, bass.ds(n, 1), :].rearrange("p a d -> p (a d)"), o[:, t % 2, :]).then_inc(s[f"o_st{t % 2}"], 16)

                tiles(sp, one)
                for k in range(2):
                    sp.wait_ge(s[f"o_st{k}"], 8 * NT)


def decoder(nc, x, ctx_512, mask_SxS2_bk1, mask_BxS2_bf0, L0_attn_Wq, L0_attn_bq, L0_attn_Wk, L0_attn_bk,
            L0_attn_Wv, L0_attn_bv, L0_xattn_Wq, L0_xattn_bq, L0_xattn_Wk, L0_xattn_bk, L0_ffn_gate_w,
            L0_ffn_w_gate, L0_ffn_w_up, L0_ffn_w_down, L0_ffn_sw_gate, L0_ffn_sw_up, L0_ffn_sw_down, out):
    def dram(name, shape, dt=F32):
        return nc.dram_tensor(name, shape, dt, kind="Internal").ap()

    qk_dram = dram("qk_dram", [2, 2, U, P, S])
    norm_dram = dram("norm_dram", [B * H, S])
    x2_dram = dram("x2_dram", [T, D])
    table_dram = dram("table_dram", [ROWS, 1], U32)
    y_dram = dram("y_dram", [NJ * P, D])

    with ExitStack() as ctx:
        m = Memory(nc, ctx)
        c = Kept()
        c.pool_passed, c.dve_passed = m.sem("pool_passed"), m.sem("dve_passed")
        build_constants(nc, m, c, table_dram)
        c.weights = m.sb("weights", [P, NT, 2])
        c.slots = m.sb("slots", [P, NT, 2], U32)
        c.listed = m.sb("listed", [P, NT, 2])
        c.choice = m.sb("choice", [P, NT, 2])
        c.both_sum = m.sb("both_sum", [P, E], BF16)
        c.first_row = m.sb("first_row", [1, NJ], I32)
        c.expert_of = m.sb("expert_of", [1, NJ], I32)
        c.bar = m.sb("bar_kept", [P, TT, B * H])
        c.attn = m.sb("attn", [P, U, S])
        with ExitStack() as ctx2:
            m2 = Memory(nc, ctx2)
            c.qk_ctx = [[m2.sb(f"qk_ctx{a}{b}", [P, B * S], F32R) for b in range(2)] for a in range(2)]
            with ExitStack() as ctx3:
                c.v = Memory(nc, ctx3).sb("v", [P, B * TT, D])
                project(nc, c, x, L0_attn_Wq, L0_attn_bq, L0_attn_Wk, L0_attn_bk, L0_attn_Wv, L0_attn_bv, qk_dram, norm_dram)
                choose_queries(nc, c, norm_dram, ctx_512, L0_xattn_Wq, L0_xattn_bq, L0_xattn_Wk, L0_xattn_bk)
                attend(nc, c, qk_dram)
            cross_and_shared(nc, c, x, mask_SxS2_bk1, mask_BxS2_bf0, L0_ffn_gate_w, L0_ffn_sw_gate, L0_ffn_sw_up,
                             L0_ffn_sw_down, x2_dram, table_dram)
        plan(nc, c)
        experts(nc, c, L0_ffn_w_gate, L0_ffn_w_up, L0_ffn_w_down, x2_dram, table_dram, y_dram)
        combine(nc, c, y_dram, out)


_INS = ["x", "ctx_512", "mask_SxS2_bk1", "mask_BxS2_bf0", "L0_attn_Wq", "L0_attn_bq", "L0_attn_Wk", "L0_attn_bk",
        "L0_attn_Wv", "L0_attn_bv", "L0_xattn_Wq", "L0_xattn_bq", "L0_xattn_Wk", "L0_xattn_bk", "L0_ffn_gate_w",
        "L0_ffn_w_gate", "L0_ffn_w_up", "L0_ffn_w_down", "L0_ffn_sw_gate", "L0_ffn_sw_up", "L0_ffn_sw_down"]


def kernel(**inputs):
    import numpy as _np
    import concourse.bacc as _bacc
    from concourse import mybir as _mybir
    from concourse.bass_utils import run_bass_kernel_spmd as _run

    nc = _bacc.Bacc("TRN2", target_bir_lowering=False, num_devices=1)
    arrays, args = {}, []
    for name in _INS:
        a = _np.ascontiguousarray(inputs[name])
        arrays[f"in_{name}_dram"] = a
        args.append(nc.dram_tensor(f"in_{name}_dram", a.shape, _mybir.dt.from_np(a.dtype), kind="ExternalInput").ap())
    shape = tuple(inputs["x"].shape)
    out = nc.dram_tensor("out_0_dram", shape, _mybir.dt.float32, kind="ExternalOutput").ap()
    decoder(nc, *args, out)
    r = _run(nc, [arrays], core_ids=[0])
    return r.results[0]["out_0_dram"]
```

```python
from contextlib import ExitStack

import concourse.bass as bass
from concourse import mybir

P = 128
F32 = mybir.dt.float32
F32R = mybir.dt.float32r
BF16 = mybir.dt.bfloat16
I32 = mybir.dt.int32
U32 = mybir.dt.uint32
U8 = mybir.dt.uint8
ALU = mybir.AluOpType
ACT = mybir.ActivationFunctionType
AX = mybir.AxisListType

B, S, D = 4, 512, 512
H, HD = 16, 32
DC = D // P
TT = S // P
HG = H * HD // P
HPG = P // HD
U = B * HG
BLOCK, TOPK = 128, 64
NEG_SEL = -1.0e30
SENTINEL = 3.0e38


class Memory:

    def __init__(self, nc, ctx):
        self.nc, self.ctx, self.sems = nc, ctx, []

    def sb(self, name, shape, dt=F32):
        return self.ctx.enter_context(self.nc.sbuf_tensor(name, shape, dt))

    def ps(self, name, shape, dt=F32):
        return self.ctx.enter_context(self.nc.psum_tensor(name, shape, dt))

    def sem(self, name):
        if not self.sems:
            self.ctx.callback(self.clear)
        self.sems.append(self.nc.alloc_semaphore(name=name))
        return self.sems[-1]

    def clear(self):
        self.nc.clear_and_free_semaphores(self.sems)
        self.nc.all_engine_barrier()


def wait_apart(eng, sem, value, passed):
    eng.wait_ge(sem, value)
    eng.sem_inc(passed, 1)


class Kept:
    pass


def build_constants(nc, m, c, table_dram):
    c.ident = m.sb("ident", [P, P])
    c.ident_bf = m.sb("ident_bf", [P, P], BF16)
    c.head_cols = m.sb("head_cols", [P, HG, H])
    R = 3 * HD
    c.window = m.sb("window", [P, S])
    zeros = m.sb("zeros", [P, table_dram.shape[0] // P], U32)
    built, cleared, table_out = m.sem("constants_step"), m.sem("zeros_done"), m.sem("table_out")
    with nc.Block() as block:
        @block.vector
        def _(dve):
            dve.memset(zeros[:], 0).then_inc(cleared, 1)

        @block.sync
        def _(sp):
            sp.wait_ge(cleared, 1)
            sp.dma_start(table_dram.rearrange("(p n) a -> p (n a)", p=P), zeros[:]).then_inc(table_out, 16)
            sp.wait_ge(table_out, 16)

        @block.gpsimd
        def _(pool):
            pool.memset(c.ident[:], 0.0)
            pool.memset(c.ident_bf[:], 0.0)
            pool.memset(c.window[:], 0.0)
            pool.memset(c.head_cols[:], 1.0).then_inc(built, 1)
            pool.wait_ge(built, 1)
            for t in (c.ident, c.ident_bf):
                pool.affine_select(out=t[:], in_=t[:], compare_op=ALU.not_equal, fill=1.0, base=0,
                                   pattern=[[-1, P]], channel_multiplier=1)
            pool.affine_select(out=c.head_cols[:], in_=c.head_cols[:], compare_op=ALU.is_ge, fill=0.0,
                               base=0, pattern=[[P, HG], [-HD, H]], channel_multiplier=1).then_inc(built, 1)
            pool.wait_ge(built, 2)
            pool.affine_select(out=c.head_cols[:], in_=c.head_cols[:], compare_op=ALU.is_ge, fill=0.0,
                               base=HD - 1, pattern=[[-P, HG], [HD, H]], channel_multiplier=-1)
            n = 2
            for row in (R, R + 1):
                pool.affine_select(out=c.window[:], in_=c.window[:], compare_op=ALU.not_equal, fill=1.0, base=-row,
                                   pattern=[[0, S]], channel_multiplier=1).then_inc(built, 1)
                n += 1
                pool.wait_ge(built, n)
            for t in range(TT):
                lo, hi = max(0, BLOCK * t - BLOCK // 2), min(S, BLOCK * t + 3 * BLOCK // 2)
                for a, b in ((0, lo), (hi, S)):
                    if b > a:
                        pool.affine_select(out=c.window[:, a:b], in_=c.window[:, a:b], compare_op=ALU.not_equal,
                                           fill=1.0, base=-(R + 2 + t), pattern=[[0, b - a]],
                                           channel_multiplier=1).then_inc(built, 1)
                        n += 1
                        pool.wait_ge(built, n)


def project(nc, c, x, wq, bq, wk, bk, wv, bv, qk_dram, norm_dram):
    with ExitStack() as ctx:
        m = Memory(nc, ctx)
        w_raw = c.attn[:, 0:2 * DC, :].rearrange("p (n c) d -> p n c d", c=DC)
        w_hi = m.sb("w_hi", [P, 3, DC, D], F32R)
        w_lo = m.sb("w_lo", [P, 3, DC, D], F32R)
        x_in = m.sb("x_in", [P, TT, D])
        xT_hi = m.sb("xT_hi", [P, DC, S], F32R)
        xT_lo = m.sb("xT_lo", [P, DC, S], F32R)
        bias_qk = m.sb("bias_qk", [P, 2, HG])
        bias_v = m.sb("bias_v", [P, D])
        raw = c.attn[:, 2 * DC:2 * DC + 4, :]
        parts = m.sb("parts", [P, 4, 2, S], F32R)
        squares = c.attn[:, 2 * DC + 4:2 * DC + 8, :]
        norm_sb = m.sb("norm_sb", [H, S])
        ps_tr = m.ps("ps_tr", [P, 2, S])
        ps_proj = m.ps("ps_proj", [P, 4, S])
        ps_norm = m.ps("ps_norm", [H, S])

        w_loaded = [m.sem(f"w_loaded{n}") for n in range(3)]
        bias_loaded, x_loaded = m.sem("bias_loaded"), m.sem("x_loaded")
        w_hi_done, w_split = m.sem("w_hi_done"), m.sem("w_split")
        x_turned, xT_hi_done, xT_lo_done = m.sem("x_turned"), m.sem("xT_hi_done"), m.sem("xT_lo_done")
        proj_done, qk_out, v_out = m.sem("proj_done"), m.sem("qk_out"), m.sem("v_out")
        hi_done, lo_done, raw_used = m.sem("hi_done"), m.sem("lo_done"), m.sem("raw_used")
        parts_stored = [m.sem(f"parts_stored{k}") for k in range(4)]
        squares_done, norm_acc, norm_out, norm_stored = (
            m.sem("squares_done"), m.sem("norm_acc"), m.sem("norm_out"), m.sem("norm_stored"))

        with nc.Block() as block:
            @block.sync
            def _(sp):
                for n, w in enumerate((wq, wk, wv)):
                    if n == 2:
                        sp.wait_ge(w_split, 1)
                    sp.dma_start(w_raw[:, n % 2], w.rearrange("(c p) n -> p c n", p=P)).then_inc(w_loaded[n], 16)
                    if n == 0:
                        sp.dma_start(x_in[:], x[0:1].rearrange("b (t p) d -> p (b t) d", p=P)).then_inc(x_loaded, 16)
                def store_parts(i):
                    for n in range(2 * HG):
                        sp.wait_ge(lo_done, 2 * HG * i + n + 1)
                        sp.dma_start(qk_dram[n // HG, :, bass.ds(i * HG + n % HG, 1)].rearrange("h a p n -> (a p) h n"),
                                     parts[:, n % 4].bitcast(F32)).then_inc(parts_stored[n % 4], 16)

                with sp.Fori(0, B - 1) as i:
                    sp.wait_ge(x_turned, 4 * i + 4)
                    sp.dma_start(x_in[:], x[bass.ds(i + 1, 1)].rearrange("b (t p) d -> p (b t) d", p=P)).then_inc(x_loaded, 16)
                    store_parts(i)
                store_parts(B - 1)
                for k in range(4):
                    sp.wait_ge(parts_stored[k], 32 * B + 16)
                sp.wait_ge(norm_stored, 16 * B + 16)

            @block.scalar
            def _(act):
                act.dma_start(bias_qk[:, 0, :], bq.rearrange("(g p) -> p g", p=P), allow_slow_non_contiguous=True).then_inc(bias_loaded, 16)
                act.dma_start(bias_qk[:, 1, :], bk.rearrange("(g p) -> p g", p=P), allow_slow_non_contiguous=True).then_inc(bias_loaded, 16)
                act.dma_start(bias_v[:], bv.rearrange("(a n) -> a n", a=1).to_broadcast([P, D])).then_inc(bias_loaded, 16)
                for n in range(3):
                    act.wait_ge(w_loaded[n], 16)
                    act.activation(w_hi[:, n], w_raw[:, n % 2], ACT.Copy).then_inc(w_hi_done, 1)
                act.wait_ge(bias_loaded, 48)
                with act.Fori(0, B) as i:
                    for dc in range(DC):
                        act.wait_ge(x_turned, 4 * i + dc + 1)
                        if dc == 0:
                            act.wait_ge(v_out, 4 * i + 4)
                        act.activation(xT_hi[:, dc, :], ps_tr[:, dc % 2, :], ACT.Copy).then_inc(xT_hi_done, 1)
                    for n in range(2 * HG):
                        act.wait_ge(proj_done, 12 * i + n + 1)
                        act.wait_ge(raw_used, 8 * i + n + 1)
                        act.activation(raw[:, n % 4, :], ps_proj[:, n % 4, :], ACT.Identity,
                                       bias=bias_qk[:, n // HG, n % HG:n % HG + 1]).then_inc(qk_out, 1)
                    act.wait_ge(norm_acc, i + 2)
                    act.wait_ge(norm_stored, 16 * i + 16)
                    act.activation(norm_sb[:], ps_norm[:], ACT.Copy).then_inc(norm_out, 1)
                    act.wait_ge(norm_out, i + 2)
                    act.dma_start(norm_dram[bass.ds(i * H, H), :], norm_sb[:]).then_inc(norm_stored, 16)

            @block.vector
            def _(dve):
                for n in range(3):
                    dve.wait_ge(w_hi_done, n + 1)
                    dve.tensor_tensor(w_lo[:, n], w_raw[:, n % 2], w_hi[:, n].bitcast(F32), ALU.subtract).then_inc(w_split, 1)
                dve.wait_ge(bias_loaded, 48)
                with dve.Fori(0, B) as i:
                    for dc in range(DC):
                        dve.wait_ge(xT_hi_done, 4 * i + dc + 1)
                        dve.tensor_tensor(xT_lo[:, dc, :], ps_tr[:, dc % 2, :], xT_hi[:, dc, :].bitcast(F32),
                                          ALU.subtract).then_inc(xT_lo_done, 1)
                    for n in range(2 * HG):
                        dve.wait_ge(qk_out, 8 * i + n + 1)
                        dve.wait_ge(parts_stored[n % 4], 32 * i + 16 * (n // 4) + 16)
                        dve.tensor_copy(parts[:, n % 4, 0, :], raw[:, n % 4, :]).then_inc(hi_done, 1)
                    for t in range(TT):
                        n = 2 * HG + t
                        dve.wait_ge(proj_done, 12 * i + n + 1)
                        dve.tensor_tensor(c.v[:, bass.ds(i * HG, HG), t * P:(t + 1) * P],
                                          ps_proj[:, n % 4, :].rearrange("p (g d) -> p g d", g=HG),
                                          bias_v[:].rearrange("p (g d) -> p g d", g=HG), ALU.add).then_inc(v_out, 1)

            @block.gpsimd
            def _(pool):
                pool.sem_inc(v_out, 4)
                pool.sem_inc(norm_stored, 16)
                pool.sem_inc(norm_out, 1)
                pool.sem_inc(norm_acc, 1)
                pool.sem_inc(raw_used, 4)
                for k in range(4):
                    pool.sem_inc(parts_stored[k], 16)
                with pool.Fori(0, B) as i:
                    pool.wait_ge(norm_acc, i + 1)
                    for n in range(2 * HG):
                        pool.wait_ge(hi_done, 8 * i + n + 1)
                        if n < HG:
                            pool.tensor_tensor(squares[:, n, :], raw[:, n, :], raw[:, n, :], ALU.mult).then_inc(squares_done, 1)
                        pool.tensor_tensor(parts[:, n % 4, 1, :], raw[:, n % 4, :], parts[:, n % 4, 0, :].bitcast(F32),
                                           ALU.subtract).then_inc(lo_done, 1)
                        pool.wait_ge(lo_done, 8 * i + n + 1)
                        if n < HG:
                            pool.wait_ge(squares_done, 4 * i + n + 1)
                        pool.sem_inc(raw_used, 1)

            @block.tensor
            def _(pe):
                pe.wait_ge(w_split, 3)
                with pe.Fori(0, B) as i:
                    pe.wait_ge(x_loaded, 16 * i + 16)
                    for dc in range(DC):
                        if dc >= 2:
                            pe.wait_ge(xT_lo_done, 4 * i + dc - 1)
                        for t in range(TT):
                            last = pe.transpose(ps_tr[:, dc % 2, t * P:(t + 1) * P],
                                                x_in[:, t, dc * P:(dc + 1) * P], c.ident[:])
                        last.then_inc(x_turned, 1)

                    def product(n, stationary, moving):
                        if n < 4:
                            pe.wait_ge(v_out, 4 * i + n + 1)
                        else:
                            pe.wait_ge(qk_out, 8 * i + n - 3)
                        for dc in range(DC):
                            if n == 0:
                                pe.wait_ge(xT_lo_done, 4 * i + dc + 1)
                            for k, (a, b) in enumerate(((0, 0), (0, 1), (1, 0))):
                                last = pe.matmul(ps_proj[:, n % 4, :], stationary[a](dc), moving[b](dc),
                                                 start=(dc == 0 and k == 0), stop=(dc == DC - 1 and k == 2))
                        last.then_inc(proj_done, 1)

                    for n in range(2 * HG):
                        g, which = n % HG, n // HG
                        product(n, [lambda dc, w=w: w[:, which, dc, g * P:(g + 1) * P] for w in (w_hi, w_lo)],
                                [lambda dc, t=t: t[:, dc, :] for t in (xT_hi, xT_lo)])
                    pe.wait_ge(norm_out, i + 1)
                    for g in range(HG):
                        pe.wait_ge(squares_done, 4 * i + g + 1)
                        last = pe.matmul(ps_norm[:], c.head_cols[:, g, :], squares[:, g, :],
                                         start=(g == 0), stop=(g == HG - 1))
                    last.then_inc(norm_acc, 1)
                    for t in range(TT):
                        product(2 * HG + t, [lambda dc, x=x_: x[:, dc, t * P:(t + 1) * P] for x_ in (xT_hi, xT_lo)],
                                [lambda dc, w=w: w[:, 2, dc, :] for w in (w_hi, w_lo)])


def choose_queries(nc, c, norm_dram, context, x_wq, x_bq, x_wk, x_bk):
    with ExitStack() as ctx:
        m = Memory(nc, ctx)
        work = m.sb("work", [B * H, S + 2])
        top8 = m.sb("top8", [B * H, 8])
        bar = m.sb("bar", [B * H, S])
        w_in = m.sb("xw_in", [P, 2, P])
        w_sb = m.sb("xw_sb", [P, 2, P])
        wT_hi = m.sb("xwT_hi", [P, 2, P], F32R)
        wT_lo = m.sb("xwT_lo", [P, 2, P], F32R)
        bias = m.sb("x_bias", [P, 2])
        c_in = m.sb("c_in", [P, TT, P])
        cT = m.sb("cT", [P, S])
        cT_hi = m.sb("cT_hi", [P, S], F32R)
        cT_lo = m.sb("cT_lo", [P, S], F32R)
        c_raw = m.sb("c_raw", [P, 2, S])
        ps_bar = m.ps("ps_bar", [P, TT, B * H])
        ps_w = m.ps("ps_w", [P, 2, P])
        ps_c = m.ps("ps_c", [P, S])
        ps_qk = m.ps("ps_qk", [P, 2, S])
        loaded, step, turned = m.sem("norms_loaded"), m.sem("choose_step"), m.sem("bar_turned")
        w_loaded, b_loaded, c_loaded = m.sem("xw_loaded"), m.sem("xb_loaded"), m.sem("c_loaded")
        w_turned, w_copied, w_hi_done, w_lo_done = m.sem("xw_turned"), m.sem("xw_copied"), m.sem("xw_hi"), m.sem("xw_lo")
        c_turned, c_copied, c_hi_done, c_lo_done = m.sem("c_turned"), m.sem("c_copied"), m.sem("c_hi"), m.sem("c_lo")
        qk_done, qk_copied, qk_hi_done, qk_lo_done = m.sem("qk_done"), m.sem("qk_copied"), m.sem("qk_hi"), m.sem("qk_lo")
        with nc.Block() as block:
            @block.sync
            def _(sp):
                sp.dma_start(work[:, 0:S], norm_dram[:]).then_inc(loaded, 16)
                sp.dma_start(w_in[:, 0, :], x_wq).then_inc(w_loaded, 16)
                sp.dma_start(w_in[:, 1, :], x_wk).then_inc(w_loaded, 16)
                for n, b in enumerate((x_bq, x_bk)):
                    sp.dma_start(bias[:, n:n + 1], b.rearrange("(p a) -> p a", a=1),
                                 allow_slow_non_contiguous=True).then_inc(b_loaded, 16)
                sp.dma_start(c_in[:], context[0:1].rearrange("b (t p) d -> p (b t) d", p=P)).then_inc(c_loaded, 16)
                with sp.Fori(1, B) as i:
                    sp.wait_ge(c_turned, i)
                    sp.dma_start(c_in[:], context[bass.ds(i, 1)].rearrange("b (t p) d -> p (b t) d", p=P)).then_inc(c_loaded, 16)

            @block.vector
            def _(dve):
                dve.memset(work[:, S:S + 2], SENTINEL).then_inc(step, 1)
                dve.wait_ge(loaded, 16)
                for r in range(TOPK // 8):
                    dve.wait_ge(step, 2 * r + 1)
                    dve.max(top8[:], work[:]).then_inc(step, 1)
                    dve.wait_ge(step, 2 * r + 2)
                    dve.match_replace(work[:], top8[:], work[:], -1.0).then_inc(step, 1)
                n = TOPK // 4 + 1
                dve.wait_ge(step, n)
                dve.tensor_scalar(bar[:], work[:, 0:S], 0.0, NEG_SEL, ALU.is_ge, ALU.mult).then_inc(step, 1)
                dve.wait_ge(step, n + 1)
                dve.memset(bar[:, 0:1], 0.0)
                dve.memset(bar[:, S - 1:S], 0.0).then_inc(step, 1)
                dve.wait_ge(turned, 1)
                dve.tensor_copy(c.bar[:].rearrange("p t n -> p (t n)"),
                                ps_bar[:].rearrange("p t n -> p (t n)"))

            @block.scalar
            def _(act):
                act.wait_ge(w_turned, 1)
                act.activation(w_sb[:], ps_w[:], ACT.Copy).then_inc(w_copied, 1)
                act.activation(wT_hi[:], ps_w[:], ACT.Copy).then_inc(w_hi_done, 1)
                act.wait_ge(b_loaded, 32)
                with act.Fori(0, B) as i:
                    act.wait_ge(c_turned, i + 1)
                    act.wait_ge(c_lo_done, i + 1)
                    act.wait_ge(qk_done, 2 * i + 2)
                    act.activation(cT[:], ps_c[:], ACT.Copy).then_inc(c_copied, 1)
                    act.activation(cT_hi[:], ps_c[:], ACT.Copy).then_inc(c_hi_done, 1)
                    for n in range(2):
                        act.wait_ge(qk_done, 2 * i + n + 3)
                        act.wait_ge(qk_lo_done, 2 * i + n + 1)
                        act.activation(c_raw[:, n, :], ps_qk[:, n, :], ACT.Identity, bias=bias[:, n:n + 1]).then_inc(qk_copied, 1)

            @block.gpsimd
            def _(pool):
                pool.sem_inc(c_lo_done, 1)
                pool.sem_inc(qk_done, 2)
                pool.sem_inc(qk_lo_done, 2)
                pool.wait_ge(w_copied, 1)
                pool.wait_ge(w_hi_done, 1)
                pool.tensor_tensor(wT_lo[:], w_sb[:], wT_hi[:].bitcast(F32), ALU.subtract).then_inc(w_lo_done, 1)
                with pool.Fori(0, B) as i:
                    pool.wait_ge(c_copied, i + 1)
                    pool.wait_ge(c_hi_done, i + 1)
                    pool.tensor_tensor(cT_lo[:], cT[:], cT_hi[:].bitcast(F32), ALU.subtract).then_inc(c_lo_done, 1)
                    for n in range(2):
                        hi, lo = c.qk_ctx[n][0][:, bass.ds(i * S, S)], c.qk_ctx[n][1][:, bass.ds(i * S, S)]
                        pool.wait_ge(qk_copied, 2 * i + n + 1)
                        pool.tensor_copy(hi, c_raw[:, n, :]).then_inc(qk_hi_done, 1)
                        pool.wait_ge(qk_hi_done, 2 * i + n + 1)
                        pool.tensor_tensor(lo, c_raw[:, n, :], hi.bitcast(F32), ALU.subtract).then_inc(qk_lo_done, 1)

            @block.tensor
            def _(pe):
                pe.wait_ge(w_loaded, 32)
                for n in range(2):
                    last = pe.transpose(ps_w[:, n, :], w_in[:, n, :], c.ident[:])
                last.then_inc(w_turned, 1)
                pe.wait_ge(w_lo_done, 1)
                with pe.Fori(0, B) as i:
                    pe.wait_ge(c_loaded, 16 * i + 16)
                    for t in range(TT):
                        last = pe.transpose(ps_c[:, t * P:(t + 1) * P], c_in[:, t, :], c.ident[:])
                    last.then_inc(c_turned, 1)
                    pe.wait_ge(c_lo_done, i + 2)
                    for n in range(2):
                        pe.wait_ge(qk_lo_done, 2 * i + n + 1)
                        for k, (a, b) in enumerate(((wT_hi, cT_hi), (wT_hi, cT_lo), (wT_lo, cT_hi))):
                            last = pe.matmul(ps_qk[:, n, :], a[:, n, :], b[:], start=(k == 0), stop=(k == 2))
                        last.then_inc(qk_done, 1)
                pe.wait_ge(step, TOPK // 4 + 3)
                for t in range(TT):
                    last = pe.transpose(ps_bar[:, t, :], bar[:, t * P:(t + 1) * P], c.ident[0:B * H, 0:B * H])
                last.then_inc(turned, 1)


SCALE = float(HD) ** -0.5
NU = HPG * TT
BR = 3 * HD
NDMA = 16 * 12
SLOTS = 3
EARLY = 5
GW = 10


def need(eng, sem, value):
    if not isinstance(value, int) or value > 0:
        eng.wait_ge(sem, value)


def attend(nc, c, qk_dram):
    with ExitStack() as ctx:
        m = Memory(nc, ctx)
        q4 = m.sb("q4", [P, SLOTS, HPG, S], F32R)
        k4 = m.sb("k4", [P, SLOTS, HPG, S], F32R)
        vu = m.sb("vu", [P, TT, P])
        ones = m.sb("ones_sum", [P, HD])
        probs = m.sb("probs", [P, TT, HPG, S])
        pair_sum = m.sb("pair_sum", [P, 2, HPG, S])
        outT = m.sb("outT", [P, S])
        sumT = m.sb("sumT", [P, S])
        first_rows = m.sb("first_rows", [P, HPG])
        rsum = m.sb("rsum", [P, TT, HPG])
        maxima = m.sb("maxima", [P, TT * (HPG * GW + 2)])
        m_all = m.sb("m_all", [P, TT, HPG])
        m_win = m.sb("m_win", [P, TT, HPG])
        m_bar = m.sb("m_bar", [P, TT, HPG])
        m_row = m.sb("m_row", [P, TT, HPG])
        turn_in = m.sb("turn_in", [P, TT * (P + 1) + 4], BF16)
        ps_s = m.ps("ps_s", [P, 2, S])
        ps_st = m.ps("ps_st", [P, 2, S])
        ps_o = m.ps("ps_o", [P, S])
        ps_sum = m.ps("ps_sum", [P, S])
        ps_back = m.ps("ps_back", [P, S])
        ps_both = m.ps("ps_turn_rows", [P, S])
        ps_turn = ps_both[:, 0:S // 2].bitcast(BF16)
        ps_rows = ps_both[:, S // 2:S // 2 + TT * HPG].rearrange("p (t j) -> p t j", j=HPG)

        unit_in = [m.sem(f"unit_in{p}") for p in range(SLOTS)]
        v_in = m.sem("v_in")
        s_done, s_reduced = m.sem("s_done"), m.sem("s_reduced")
        st_done, exp_done = m.sem("st_done"), m.sem("exp_done")
        pv_done, added, sums_done = m.sem("pv_done"), m.sem("added"), m.sem("sums_done")
        evacuated, backed, recip_done, normed = m.sem("evacuated"), m.sem("backed"), m.sem("recip_done"), m.sem("normed")
        row_step, turn_ready, turned, shift_ready = m.sem("row_step"), m.sem("turn_ready"), m.sem("turned"), m.sem("shift_ready")
        cleared, window_in = m.sem("cleared"), m.sem("window_in")

        def slot(t, u):
            return t[:, bass.ds(u, 1), :].rearrange("p a n -> p (a n)")

        def units(eng, unit):
            unit(0, 0, 0)
            rounds = (U - 2) // SLOTS
            with eng.Fori(0, rounds) as i:
                for k in range(1, SLOTS + 1):
                    unit(SLOTS * i + k, k % SLOTS, i + k // SLOTS)
            for u in range(SLOTS * rounds + 1, U):
                unit(u, u % SLOTS, u // SLOTS)

        def is_last(u):
            return isinstance(u, int) and u == U - 1

        with nc.Block() as block:
            @block.gpsimd
            def _(pool):
                pool.sem_inc(backed, 1)
                pool.sem_inc(normed, 1)
                pool.memset(ones[:], 1.0)
                pool.memset(turn_in[:], 0.0)
                pool.memset(first_rows[:], 0.0)
                pool.memset(maxima[:], -SENTINEL).then_inc(cleared, 1)
                pool.wait_ge(cleared, 1)
                pool.affine_select(out=first_rows[:], in_=first_rows[:], compare_op=ALU.not_equal, fill=1.0, base=0,
                                   pattern=[[-HD, HPG]], channel_multiplier=1).then_inc(cleared, 1)

                def unit(u, p, uses):
                    need(pool, pv_done, TT * u)
                    pool.tensor_copy(vu[:].rearrange("p t d -> p (t d)"), slot(c.v, u)).then_inc(v_in, 1)
                    for h in range(2):
                        pool.wait_ge(exp_done, NU * u + 2 * HPG * (h + 1))
                        need(pool, sums_done, 2 * (u - 1) + h + 1)
                        pool.tensor_tensor(pair_sum[:, h], probs[:, 2 * h], probs[:, 2 * h + 1], ALU.add).then_inc(added, 1)

                units(pool, unit)

            @block.sync
            def _(sp):
                def load_unit(u, p, first):
                    if not first:
                        sp.wait_ge(st_done, NU * (u - SLOTS + 1))
                    for k in range(2):
                        for r in range(3):
                            for tile, which, part in ((q4, 0, r // 2), (k4, 1, r % 2)):
                                src = qk_dram[which, part, bass.ds(u, 1), 2 * HD * k:2 * HD * (k + 1)]
                                sp.dma_start(tile[HD * r:HD * (r + 1), p, 2 * k:2 * k + 2, :].bitcast(F32),
                                             src.rearrange("a (j p) n -> p (a j) n", p=HD)).then_inc(unit_in[p], 16)

                for u in range(SLOTS):
                    load_unit(u, u, True)
                with sp.Fori(1, U // SLOTS) as i:
                    for p in range(SLOTS):
                        load_unit(SLOTS * i + p, p, False)
                for u in range(U // SLOTS * SLOTS, U):
                    load_unit(u, u % SLOTS, False)

            @block.tensor
            def _(pe):
                def score(u, p, x, uses):
                    j, t = divmod(x, TT)
                    if x == 0:
                        pe.wait_ge(unit_in[p], NDMA * uses + NDMA)
                    need(pe, s_reduced, NU * u + x - 1)
                    pe.matmul(ps_s[:, x % 2, :], q4[0:BR, p, j, t * P:(t + 1) * P], k4[0:BR, p, j, :],
                              start=True, stop=True).then_inc(s_done, 1)

                def turn(u):
                    pe.wait_ge(turn_ready, u + 1)
                    need(pe, shift_ready, HPG * u)
                    need(pe, recip_done, u - 1)
                    for t in range(TT):
                        last = pe.transpose(ps_turn[:, t * P:(t + 1) * P], turn_in[:, t * P:(t + 1) * P], c.ident_bf[:])
                    last.then_inc(turned, 1)

                def weigh(u, kc):
                    pe.wait_ge(exp_done, NU * u + HPG * (kc + 1))
                    if kc == 0:
                        pe.wait_ge(v_in, u + 1)
                        need(pe, evacuated, 2 * u)
                    for j in range(HPG):
                        last = pe.matmul(ps_o[HD * j:HD * (j + 1), :], vu[:, kc, HD * j:HD * (j + 1)],
                                         probs[:, kc, j, :], start=(kc == 0), stop=(kc == TT - 1))
                    last.then_inc(pv_done, 1)

                def sums(u, h):
                    pe.wait_ge(added, 2 * u + h + 1)
                    if h == 0:
                        need(pe, evacuated, 2 * u)
                    for j in range(HPG):
                        last = pe.matmul(ps_sum[HD * j:HD * (j + 1), :], ones[:], pair_sum[:, h, j, :],
                                         start=(h == 0), stop=(h == 1))
                    last.then_inc(sums_done, 1)

                def back(u):
                    pe.wait_ge(evacuated, 2 * u + 2)
                    pe.wait_ge(normed, u + 1)
                    for t in range(TT):
                        pe.matmul(ps_rows[:, t, :], sumT[:, t * P:(t + 1) * P], first_rows[:], start=True, stop=True)
                        last = pe.transpose(ps_back[:, t * P:(t + 1) * P], outT[:, t * P:(t + 1) * P], c.ident[:])
                    last.then_inc(backed, 1)

                def unit(u, p, uses):
                    first, last = isinstance(u, int) and u == 0, is_last(u)
                    for s in range(NU):
                        kc, j = divmod(s, HPG)
                        if kc == 0:
                            pe.wait_ge(shift_ready, HPG * u + j + 1)
                        need(pe, exp_done, NU * u + s - 1)
                        pe.matmul(ps_st[:, s % 2, :], k4[:, p, j, kc * P:(kc + 1) * P], q4[:, p, j, :],
                                  start=True, stop=True).then_inc(st_done, 1)
                        if s < NU - EARLY and not last:
                            score(u + 1, (p + 1) % SLOTS, s + EARLY, uses + (p + 1) // SLOTS)
                        if s >= NU - EARLY and not (isinstance(u, int) and u > U - 3):
                            score(u + 2, (p + 2) % SLOTS, s - (NU - EARLY), uses + (p + 2) // SLOTS)
                        if not first:
                            if s == 1:
                                weigh(u - 1, 3)
                            if s == 7:
                                sums(u - 1, 1)
                            if s == 10:
                                back(u - 1)
                        if s in (11, 12, 13):
                            weigh(u, s - 11)
                        if s == 14 and not last:
                            turn(u + 1)
                        if s == 15:
                            sums(u, 0)
                    if last:
                        weigh(u, 3)
                        sums(u, 1)
                        back(u)

                pe.wait_ge(window_in, SLOTS * HPG)
                pe.wait_ge(cleared, 2)
                for x in range(NU):
                    score(0, 0, x, 0)
                turn(0)
                for x in range(EARLY):
                    score(1, 1, x, 0)
                units(pe, unit)

            @block.scalar
            def _(act):
                def take_shift(u, p, j):
                    if j == 0:
                        act.wait_ge(turned, u + 1)
                        need(act, st_done, NU * (u - SLOTS + 1))
                    act.activation(q4[BR:P, p, j, :], ps_turn[HD * j:HD * (j + 1), :], ACT.Copy).then_inc(shift_ready, 1)

                def evacuate(u):
                    act.wait_ge(pv_done, TT * u + TT)
                    act.wait_ge(sums_done, 2 * u + 2)
                    act.wait_ge(backed, u + 1)
                    act.activation(outT[:], ps_o[:], ACT.Copy).then_inc(evacuated, 1)
                    act.activation(sumT[:], ps_sum[:], ACT.Copy).then_inc(evacuated, 1)

                def unit(u, p, uses):
                    first, last = isinstance(u, int) and u == 0, is_last(u)
                    for s in range(NU):
                        kc, j = divmod(s, HPG)
                        act.wait_ge(st_done, NU * u + s + 1)
                        if j == 0:
                            need(act, pv_done, TT * (u - 1) + kc + 1)
                            if kc % 2 == 0:
                                need(act, added, 2 * (u - 1) + kc // 2 + 1)
                        act.activation(probs[:, kc, j, :], ps_st[:, s % 2, :], ACT.Exp, scale=SCALE).then_inc(exp_done, 1)
                        if s == 8 and not first:
                            evacuate(u - 1)
                        if s >= 14 and not last:
                            for j in range(2):
                                take_shift(u + 1, (p + 1) % SLOTS, 2 * (s - 14) + j)
                    if last:
                        evacuate(u)

                for j in range(HPG):
                    take_shift(0, 0, j)
                units(act, unit)

            @block.vector
            def _(dve):
                by_tile = maxima[:, 0:TT * HPG * GW].rearrange("p (t j g) -> p t j g", j=HPG, g=GW)
                windows = maxima[:].rearrange("p (t x) -> p t x", t=TT)[:, :, 0:HPG * GW].rearrange(
                    "p t (j g) -> p t j g", g=GW)[:, :, :, 0:4]
                rows = turn_in[:, 0:TT * P].rearrange("p (t j r) -> p t j r", j=HPG, r=HD)
                bar_rows = turn_in[:, 2:2 + TT * (P + 1)].rearrange("p (t x) -> p t x", t=TT)[:, :, 0:P:HD]

                def reduce(u, x):
                    j, t = divmod(x, TT)
                    dve.wait_ge(s_done, NU * u + x + 1)
                    dve.tensor_reduce(by_tile[:, t, j, 1:9], ps_s[:, x % 2, :].rearrange("p (g n) -> p g n", n=S // 8),
                                      axis=AX.X, op=ALU.max).then_inc(s_reduced, 1)

                def row_maxima(u):
                    k = [0]

                    def step(ins):
                        k[0] += 1
                        ins.then_inc(row_step, 1)
                        dve.wait_ge(row_step, 6 * u + k[0])

                    bar = c.bar[:, :, bass.ds(HPG * u, HPG)]
                    dve.wait_ge(s_reduced, NU * u + NU)
                    dve.tensor_reduce(m_win[:].rearrange("p t j -> p t j"), windows, axis=AX.X, op=ALU.max)
                    step(dve.tensor_reduce(m_all[:], by_tile, axis=AX.X, op=ALU.max))
                    step(dve.tensor_tensor(m_bar[:], m_all[:], bar, ALU.add))
                    step(dve.tensor_tensor(m_row[:], m_bar[:], m_win[:], ALU.max))
                    need(dve, turned, u)
                    step(dve.tensor_scalar(rows[:, :, :, 0], m_row[:], -1.0, None, ALU.mult))
                    dve.scalar_tensor_tensor(rows[:, :, :, 1], m_row[:], -1.0, rows[:, :, :, 0],
                                             ALU.mult, ALU.subtract).then_inc(row_step, 1)
                    k[0] += 1
                    step(dve.tensor_copy(bar_rows, bar))
                    dve.sem_inc(turn_ready, 1)

                def normalise(u):
                    dve.wait_ge(backed, u + 2)
                    dve.reciprocal(rsum[:], ps_rows).then_inc(recip_done, 1)
                    dve.wait_ge(recip_done, u + 1)
                    dve.tensor_tensor(slot(c.attn, u).rearrange("p (t w) -> p t w", w=HD), ps_back[:].rearrange("p (t w) -> p t w", w=HD),
                                      rsum[:].rearrange("p t (j a) -> p (t j) a", a=1).to_broadcast([P, TT * HPG, HD]),
                                      ALU.mult).then_inc(normed, 1)

                def unit(u, p, uses):
                    first, last = isinstance(u, int) and u == 0, is_last(u)
                    if not last:
                        for x in range(EARLY, NU):
                            reduce(u + 1, x)
                        row_maxima(u + 1)
                    if not first:
                        normalise(u - 1)
                    if not (isinstance(u, int) and u > U - 3):
                        for x in range(EARLY):
                            reduce(u + 2, x)
                    if last:
                        normalise(u)

                for p in range(SLOTS):
                    for j in range(HPG):
                        dve.tensor_copy(k4[BR:P, p, j, :], c.window[BR:P, :]).then_inc(window_in, 1)
                dve.wait_ge(cleared, 1)
                for x in range(NU):
                    reduce(0, x)
                row_maxima(0)
                for x in range(EARLY):
                    reduce(1, x)
                units(dve, unit)


EPS = 1e-5
C = 128
XSCALE = float(C) ** -0.5
E, FH = 8, 352
FC = 3
FCR = FH - 2 * P
WCOLS = 2 * DC * FH + FC * D
T = B * S
NT = T // P
MASKED = -1.0e30


def gate_cols(w, up, dc):
    return w[:, (up * DC + dc) * FH:(up * DC + dc + 1) * FH]


def down_cols(w, fc):
    return w[:, 2 * DC * FH + fc * D:2 * DC * FH + (fc + 1) * D]


def cross_and_shared(nc, c, x, mask, pad_mask, gate_w, sw_gate, sw_up, sw_down, x2_dram, table_dram):
    with ExitStack() as ctx:
        m = Memory(nc, ctx)
        sw_hi = m.sb("sw_hi", [P, 2, WCOLS], F32R)
        sw_lo = m.sb("sw_lo", [P, 2, WCOLS], F32R)
        with ExitStack() as ctx2:
            m2 = Memory(nc, ctx2)
            sw_raw = m2.sb("sw_raw", [P, 2, WCOLS])
            zeroed, loaded, hi_done = m.sem("sw_zeroed"), m.sem("sw_loaded"), m.sem("sw_hi_done")
            with nc.Block() as block:
                @block.sync
                def _(sp):
                    for k in range(2):
                        cols = slice(FH * k, FH * (k + 1))
                        for up, w in enumerate((sw_gate, sw_up)):
                            sp.dma_start(sw_raw[:, k, up * DC * FH:(up + 1) * DC * FH].rearrange("p (c h) -> p c h", h=FH),
                                         w.rearrange("(c p) h -> p c h", p=P)[:, :, cols]).then_inc(loaded, 16)
                        down = sw_raw[:, k, 2 * DC * FH:].rearrange("p (c d) -> p c d", d=D)
                        rows = sw_down[FH * k:FH * (k + 1), :]
                        sp.dma_start(down[:, 0:2, :], rows[0:2 * P].rearrange("(c p) d -> p c d", p=P)).then_inc(loaded, 16)
                        sp.dma_start(down[0:FCR, 2, :], rows[2 * P:FH]).then_inc(loaded, 16)

                @block.scalar
                def _(act):
                    act.wait_ge(zeroed, 1)
                    act.wait_ge(loaded, 128)
                    for k in range(2):
                        act.activation(sw_hi[:, k], sw_raw[:, k], ACT.Copy).then_inc(hi_done, 1)

                @block.vector
                def _(dve):
                    for k in range(2):
                        last = dve.memset(sw_raw[FCR:P, k, WCOLS - D:WCOLS], 0.0)
                    last.then_inc(zeroed, 1)
                    for k in range(2):
                        dve.wait_ge(hi_done, k + 1)
                        dve.tensor_tensor(sw_lo[:, k], sw_raw[:, k], sw_hi[:, k].bitcast(F32), ALU.subtract)

        am = m.sb("am", [P, TT, S])
        pm = m.sb("pm", [P, B, S])
        am8 = m.sb("am8", [P, TT, S], U8)
        pm8 = m.sb("pm8", [P, B, S], U8)
        gw = m.sb("gw", [P, DC, E])
        gw_hi = m.sb("gw_hi", [P, DC, E], F32R)
        gw_lo = m.sb("gw_lo", [P, DC, E], F32R)
        before = m.sb("before", [P, P], BF16)
        ones = m.sb("ones", [P, P], BF16)
        expert = m.sb("expert", [P, E])
        region = m.sb("region", [P, E])
        expert_i = m.sb("expert_i", [P, E], I32)
        token_i = m.sb("token_i", [P, NT], U32)
        token = m.sb("token", [P, 1], U32)
        half = m.sb("half", [P, 1])
        q_tile = m.sb("q_tile", [P, 2, 2, P], F32R)
        x_in = m.sb("x_tile", [P, 2, D])
        r1 = m.sb("r1", [P, 2, D])
        stats = m.sb("stats", [P, 2, 6])
        mv = m.sb("mv", [P, 2, 2])
        rstd = m.sb("rstd", [P, 2, 2])
        x1 = m.sb("x1", [P, 2, D])
        sc = m.sb("sc", [P, 2, D])
        small = m.sb("small", [P, 8])
        x2 = m.sb("x2", [P, 2, D])
        xT_hi = m.sb("x2T_hi", [P, DC, P], F32R)
        xT_lo = m.sb("x2T_lo", [P, DC, P], F32R)
        act_g = m.sb("act_g", [P, 2, FH])
        g = m.sb("g", [P, 2, FC * P])
        gT_hi = m.sb("gT_hi", [P, 2, FC * P], F32R)
        gT_lo = m.sb("gT_lo", [P, 2, FC * P], F32R)
        r_small = m.sb("r_small", [P, 4])
        r_exp = m.sb("r_exp", [P, E])
        score = m.sb("score", [P, E])
        top = m.sb("top", [P, E])
        top_i = m.sb("top_i", [P, E], U32)
        top_f = m.sb("top_f", [P, E])
        chosen = m.sb("chosen", [P, 2, E])
        both = m.sb("both", [P, E], BF16)
        both_sum = c.both_sum
        place = m.sb("place", [P, E])
        placed = m.sb("placed", [P, 2, E])
        slot_f = m.sb("slot_f", [P, 2])
        slot_u = m.sb("slot_u", [P, 2], U32)

        ps_sc = m.ps("ps_sc", [P, S])
        ps_xT = m.ps("ps_xT", [P, D])
        ps_r = m.ps("ps_r", [P, 2, E])
        ps_gu = m.ps("ps_gu", [P, 2, S])
        ps_gT = m.ps("ps_gT", [P, FC * P])
        ps_y = m.ps("ps_y", [P, D])

        names = ("masks_in gate_in const_step x_ld0 x_ld1 r1_done stats1 mv1 ve1 rstd1 x1_done q_tile_done sc_done "
                 "scaled masked0 masked nmax e_done guard0 guard sum_ok rinv r2_done stats2 mv2 ve2 rstd2 x2_done x2_st0 x2_st1 "
                 "x2_turned hi_done2 lo_done2 r_logits r_max r_e r_step rank_done slots_done scat token_done "
                 "g_done u_done silu_done g_ready gT_turned gT_hi_done gT_lo_done y_done y_out both_done setup").split()
        s = {k: m.sem("p4_" + k) for k in names}

        x_rows = x.rearrange("b (t p) d -> p (b t) d", p=P)
        x2_rows = x2_dram.rearrange("(n p) d -> p n d", p=P)

        def attn_tile(b, t):
            return c.attn[:, bass.ds(b * HG, HG), t * P:(t + 1) * P]

        def tiles(eng, one):
            for t in range(TT):
                one(t, 0, t, False)
            with eng.Fori(1, B - 1) as b:
                for t in range(TT):
                    one(b * TT + t, b, t, False)
            for t in range(TT):
                one((B - 1) * TT + t, B - 1, t, t == TT - 1)

        def following(n, b, t):
            return (n + 1, b, t + 1) if t < TT - 1 else (n + 1, b + 1, 0)

        with nc.Block() as block:
            @block.sync
            def _(sp):
                sp.dma_start(am8[:], mask.rearrange("(t p) k -> p t k", p=P)).then_inc(s["masks_in"], 16)
                sp.dma_start(pm8[:].rearrange("p b k -> p (b k)"),
                             pad_mask.rearrange("(a b) k -> a (b k)", a=1).to_broadcast([P, B * S])).then_inc(s["masks_in"], 16)
                sp.dma_start(gw[:], gate_w.rearrange("(c p) e -> p c e", p=P)).then_inc(s["gate_in"], 16)

                def load_x(n, t, first):
                    if not first:
                        sp.wait_ge(s["r1_done"], n - 1)
                    sp.dma_start(x_in[:, t % 2, :], x_rows[:, bass.ds(n, 1), :].rearrange("p a d -> p (a d)")).then_inc(s[f"x_ld{t % 2}"], 16)

                load_x(0, 0, True)
                load_x(1, 1, True)

                def one(n, b, t, last):
                    sp.wait_ge(s["x2_done"], n + 1)
                    sp.dma_start(x2_rows[:, bass.ds(n, 1), :].rearrange("p a d -> p (a d)"), x2[:, t % 2, :]).then_inc(s[f"x2_st{t % 2}"], 16)
                    if not (isinstance(n, int) and n + 2 >= NT):
                        load_x(n + 2, t, False)

                tiles(sp, one)
                for k in range(2):
                    sp.wait_ge(s[f"x2_st{k}"], 8 * NT)

            @block.gpsimd
            def _(pool):
                step = s["const_step"]
                pool.memset(before[:], 1.0)
                pool.memset(ones[:], 1.0)
                pool.memset(half[:], -0.5)
                pool.memset(both_sum[:], 0.0)
                pool.memset(g[:], 0.0)
                pool.iota(token_i[:], pattern=[[P, NT]], base=0, channel_multiplier=1)
                pool.iota(expert_i[:], pattern=[[1, E]], base=0, channel_multiplier=0).then_inc(step, 1)
                pool.wait_ge(step, 1)
                pool.affine_select(out=before[:], in_=before[:], compare_op=ALU.is_gt, fill=0.0, base=0,
                                   pattern=[[1, P]], channel_multiplier=-1)
                pool.tensor_copy(expert[:], expert_i[:]).then_inc(step, 1)
                pool.wait_ge(step, 2)
                pool.tensor_scalar(region[:], expert[:], float(T), None, ALU.mult).then_inc(step, 1)

                def first_half(n, b, t):
                    p = t % 2
                    need(pool, s["sc_done"], n - 1)
                    for k in range(2):
                        src = c.qk_ctx[0][k][:, bass.ds(n * P, P)].bitcast(F32)
                        last = pool.tensor_copy(q_tile[:, p, k, :], src)
                    last.then_inc(s["q_tile_done"], 1)
                    pool.wait_ge(s[f"x_ld{p}"], 32 * b + 16 * (t // 2) + 16)
                    need(pool, s["x2_done"], n - 1)
                    pool.tensor_tensor(r1[:, p, :].rearrange("p (g d) -> p g d", g=HG),
                                       x_in[:, p, :].rearrange("p (g d) -> p g d", g=HG), attn_tile(b, t), ALU.add).then_inc(s["r1_done"], 1)
                    root(n, 0, s["mv1"], s["ve1"], s["rstd1"])
                    pool.wait_ge(s["scaled"], n + 1)
                    pool.tensor_tensor(sc[:, p, :], sc[:, p, :], am[:, t, :], ALU.add).then_inc(s["masked0"], 1)
                    wait_apart(pool, s["masked0"], n + 1, c.pool_passed)
                    pool.tensor_tensor(sc[:, p, :], sc[:, p, :], pm[:, bass.ds(b, 1), :].rearrange("p a k -> p (a k)"), ALU.add).then_inc(s["masked"], 1)
                    wait_apart(pool, s["nmax"], n + 1, c.pool_passed)
                    pool.tensor_scalar(small[:, 2:3], small[:, 0:1], -0.1 * MASKED, 0.0, ALU.subtract, ALU.max).then_inc(s["guard0"], 1)
                    wait_apart(pool, s["guard0"], n + 1, c.pool_passed)
                    pool.tensor_scalar(small[:, 3:4], small[:, 2:3], 1.0e38, 0.0, ALU.mult, ALU.mult).then_inc(s["guard"], 1)
                    root(n, 1, s["mv2"], s["ve2"], s["rstd2"])

                def root(n, k, ready, mid, done):
                    wait_apart(pool, ready, n + 1, c.pool_passed)
                    pool.tensor_scalar(rstd[:, k, 0:1], mv[:, k, 1:2], EPS, None, ALU.add).then_inc(mid, 1)
                    pool.wait_ge(mid, n + 1)
                    pool.tensor_tensor(rstd[:, k, 1:2], rstd[:, k, 0:1], half[:], ALU.pow).then_inc(done, 1)

                def send(n):
                    need(pool, s["scat"], 32 * n)
                    pool.tensor_copy(token[:], token_i[:, bass.ds(n, 1)]).then_inc(s["token_done"], 1)
                    pool.wait_ge(s["token_done"], n + 1)
                    wait_apart(pool, s["slots_done"], n + 1, c.pool_passed)
                    for k in range(2):
                        pool.indirect_dma_start(out=table_dram[:], out_offset=bass.IndirectOffsetOnAxis(ap=slot_u[:, k:k + 1], axis=0),
                                                in_=token[:], in_offset=None).then_inc(s["scat"], 16)

                pool.wait_ge(s["setup"], 1)
                first_half(0, 0, 0)

                def one(n, b, t, last):
                    if not last:
                        first_half(*following(n, b, t))
                    send(n)

                tiles(pool, one)
                pool.wait_ge(s["scat"], 32 * NT)

            @block.scalar
            def _(act):
                act.wait_ge(s["gate_in"], 16)
                act.activation(gw_hi[:], gw[:], ACT.Copy).then_inc(s["gate_in"], 1)

                def soft(n, t):
                    act.wait_ge(s["nmax"], n + 1)
                    act.activation(sc[:, t % 2, :], sc[:, t % 2, :], ACT.Exp, bias=small[:, 0:1], accum_out=small[:, 1:2]).then_inc(s["e_done"], 1)

                def one(n, b, t, last):
                    act.wait_ge(s["x2_turned"], n + 1)
                    act.activation(xT_hi[:].rearrange("p c k -> p (c k)"), ps_xT[:], ACT.Copy).then_inc(s["hi_done2"], 1)
                    for k in range(2):
                        act.wait_ge(s["g_done"], 2 * n + k + 1)
                        need(act, s["g_ready"], 2 * n + k - 1)
                        act.activation(act_g[:, k, :], ps_gu[:, 0, 0:FH], ACT.Silu).then_inc(s["silu_done"], 1)
                        if k == 0:
                            act.wait_ge(s["r_max"], n + 1)
                            act.activation(r_exp[:], ps_r[:, 0, :], ACT.Exp, bias=r_small[:, 0:1], accum_out=r_small[:, 1:2]).then_inc(s["r_e"], 1)
                        act.wait_ge(s["gT_turned"], 2 * n + k + 1)
                        act.activation(gT_hi[:, k, :], ps_gT[:], ACT.Copy).then_inc(s["gT_hi_done"], 1)
                        if k == 0 and not last:
                            soft(n + 1, t + 1)

                soft(0, 0)
                tiles(act, one)

            @block.vector
            def _(dve):
                dve.wait_ge(s["masks_in"], 32)
                dve.tensor_scalar(am[:], am8[:], MASKED, None, ALU.mult)
                dve.tensor_scalar(pm[:], pm8[:], MASKED, None, ALU.mult)
                dve.wait_ge(s["gate_in"], 17)
                dve.tensor_tensor(gw_lo[:], gw[:], gw_hi[:].bitcast(F32), ALU.subtract).then_inc(s["setup"], 1)
                dve.wait_ge(s["const_step"], 3)

                def norm(n, p, src, dst, k, ready, mid, rooted, done):
                    dve.bn_stats(stats[:, k, :], src).then_inc(ready, 1)
                    wait_apart(dve, ready, n + 1, c.dve_passed)
                    dve.bn_aggr(mv[:, k, :], stats[:, k, :]).then_inc(mid, 1)
                    dve.wait_ge(rooted, n + 1)
                    dve.tensor_scalar(dst, src, mv[:, k, 0:1], rstd[:, k, 1:2], ALU.subtract, ALU.mult).then_inc(done, 1)

                def before_soft(n, b, t):
                    p = t % 2
                    dve.wait_ge(s["r1_done"], n + 1)
                    norm(n, p, r1[:, p, :], x1[:, p, :], 0, s["stats1"], s["mv1"], s["rstd1"], s["x1_done"])
                    dve.wait_ge(s["sc_done"], n + 1)
                    dve.wait_ge(s["x1_done"], n + 1)
                    dve.scalar_tensor_tensor(sc[:, p, :], ps_sc[:], XSCALE, x1[:, p, :], ALU.mult, ALU.mult).then_inc(s["scaled"], 1)
                    dve.wait_ge(s["masked"], n + 1)
                    dve.tensor_reduce(small[:, 0:1], sc[:, p, :], axis=AX.X, op=ALU.max, negate=True).then_inc(s["nmax"], 1)

                def after_soft(n, b, t):
                    p = t % 2
                    dve.wait_ge(s["e_done"], n + 1)
                    dve.wait_ge(s["guard"], n + 1)
                    dve.tensor_tensor(small[:, 4:5], small[:, 1:2], small[:, 3:4], ALU.add).then_inc(s["sum_ok"], 1)
                    dve.wait_ge(s["sum_ok"], n + 1)
                    dve.reciprocal(small[:, 5:6], small[:, 4:5]).then_inc(s["rinv"], 1)
                    dve.wait_ge(s["rinv"], n + 1)
                    dve.scalar_tensor_tensor(r1[:, p, :], sc[:, p, :], small[:, 5:6], x1[:, p, :], ALU.mult, ALU.add).then_inc(s["r2_done"], 1)
                    dve.wait_ge(s["r2_done"], n + 1)
                    need(dve, s[f"x2_st{p}"], 32 * b + 16 * (t // 2))
                    norm(n, p, r1[:, p, :], x2[:, p, :], 1, s["stats2"], s["mv2"], s["rstd2"], s["x2_done"])

                RSTEPS = 11

                def route(n, t):
                    k = [0]

                    def step(ins):
                        k[0] += 1
                        ins.then_inc(s["r_step"], 1)
                        dve.wait_ge(s["r_step"], RSTEPS * n + k[0])

                    dve.wait_ge(s["r_logits"], n + 1)
                    dve.tensor_reduce(r_small[:, 0:1], ps_r[:, 0, :], axis=AX.X, op=ALU.max, negate=True).then_inc(s["r_max"], 1)
                    dve.wait_ge(s["r_e"], n + 1)
                    step(dve.reciprocal(r_small[:, 2:3], r_small[:, 1:2]))
                    step(dve.tensor_scalar(score[:], r_exp[:], r_small[:, 2:3], None, ALU.mult))
                    dve.sem_inc(c.dve_passed, 1)
                    step(dve.max(top[:], score[:]))
                    dve.tensor_copy(c.weights[:, bass.ds(n, 1), :].rearrange("p a k -> p (a k)"), top[:, 0:2])
                    step(dve.max_index(top_i[:], top[:], score[:]))
                    step(dve.tensor_copy(top_f[:], top_i[:]))
                    dve.tensor_copy(c.choice[:, bass.ds(n, 1), :].rearrange("p a k -> p (a k)"), top_f[:, 0:2])
                    dve.tensor_scalar(chosen[:, 0, :], expert[:], top_f[:, 0:1], None, ALU.is_equal)
                    step(dve.tensor_scalar(chosen[:, 1, :], expert[:], top_f[:, 1:2], None, ALU.is_equal))
                    dve.tensor_tensor(both[:], chosen[:, 0, :], chosen[:, 1, :], ALU.add).then_inc(s["both_done"], 1)
                    dve.wait_ge(s["rank_done"], n + 1)
                    step(dve.tensor_tensor(place[:], ps_r[:, 1, :], region[:], ALU.add))
                    step(dve.tensor_tensor(both_sum[:], both_sum[:], both[:], ALU.add))
                    step(dve.tensor_tensor(placed[:], chosen[:], place[:].rearrange("p (a e) -> p a e", a=1).to_broadcast([P, 2, E]), ALU.mult))
                    step(dve.tensor_reduce(slot_f[:], placed[:], axis=AX.X, op=ALU.add))
                    dve.tensor_copy(c.listed[:, bass.ds(n, 1), :].rearrange("p a k -> p (a k)"), slot_f[:])
                    need(dve, s["scat"], 32 * n)
                    step(dve.tensor_copy(slot_u[:], slot_f[:]))
                    dve.sem_inc(s["slots_done"], 1)

                def one(n, b, t, last):
                    dve.wait_ge(s["hi_done2"], n + 1)
                    dve.tensor_tensor(xT_lo[:].rearrange("p c k -> p (c k)"), ps_xT[:], xT_hi[:].rearrange("p c k -> p (c k)").bitcast(F32),
                                      ALU.subtract).then_inc(s["lo_done2"], 1)
                    for k in range(2):
                        if k == 0:
                            if not last:
                                before_soft(*following(n, b, t))
                        elif not last:
                            after_soft(*following(n, b, t))
                        dve.wait_ge(s["u_done"], 2 * n + k + 1)
                        dve.wait_ge(s["silu_done"], 2 * n + k + 1)
                        dve.tensor_tensor(g[:, k, 0:FH], act_g[:, k, :], ps_gu[:, 1, 0:FH], ALU.mult).then_inc(s["g_ready"], 1)
                        if k == 0:
                            route(n, t)
                        dve.wait_ge(s["gT_hi_done"], 2 * n + k + 1)
                        dve.tensor_tensor(gT_lo[:, k, :], ps_gT[:], gT_hi[:, k, :].bitcast(F32), ALU.subtract).then_inc(s["gT_lo_done"], 1)
                    dve.wait_ge(s["y_done"], n + 1)
                    dve.tensor_tensor(attn_tile(b, t), ps_y[:].rearrange("p (g d) -> p g d", g=HG),
                                      x2[:, t % 2, :].rearrange("p (g d) -> p g d", g=HG), ALU.add).then_inc(s["y_out"], 1)

                before_soft(0, 0, 0)
                after_soft(0, 0, 0)
                tiles(dve, one)

            @block.tensor
            def _(pe):
                def scores(n, b, t):
                    p = t % 2
                    pe.wait_ge(s["q_tile_done"], n + 1)
                    need(pe, s["scaled"], n)
                    for k, (a, z) in enumerate(((0, 0), (0, 1), (1, 0))):
                        last = pe.matmul(ps_sc[:], q_tile[:, p, a, :], c.qk_ctx[1][z][:, bass.ds(b * S, S)],
                                         start=(k == 0), stop=(k == 2))
                    last.then_inc(s["sc_done"], 1)

                def passes(out, stationary, moving, chunks):
                    for q in range(chunks):
                        for k, (a, z) in enumerate(((0, 0), (0, 1), (1, 0))):
                            last = pe.matmul(out, stationary[a](q), moving[z](q), start=(q == 0 and k == 0),
                                             stop=(q == chunks - 1 and k == 2))
                    return last

                xT = [lambda q, w=w: w[:, q, :] for w in (xT_hi, xT_lo)]

                def gate(n, k):
                    need(pe, s["silu_done"], 2 * n + k)
                    passes(ps_gu[:, 0, 0:FH], xT, [lambda q, w=w: gate_cols(w[:, k, :], 0, q) for w in (sw_hi, sw_lo)], DC).then_inc(s["g_done"], 1)

                def up(n, k):
                    need(pe, s["g_ready"], 2 * n + k)
                    passes(ps_gu[:, 1, 0:FH], xT, [lambda q, w=w: gate_cols(w[:, k, :], 1, q) for w in (sw_hi, sw_lo)], DC).then_inc(s["u_done"], 1)

                def turn(n, k):
                    pe.wait_ge(s["g_ready"], 2 * n + k + 1)
                    need(pe, s["gT_lo_done"], 2 * n + k)
                    for q in range(FC):
                        last = pe.transpose(ps_gT[:, q * P:(q + 1) * P], g[:, k, q * P:(q + 1) * P], c.ident[:])
                    last.then_inc(s["gT_turned"], 1)

                def down(n, k):
                    pe.wait_ge(s["gT_lo_done"], 2 * n + k + 1)
                    if k == 0:
                        need(pe, s["y_out"], n)
                    gT = [lambda q, w=w: w[:, k, q * P:(q + 1) * P] for w in (gT_hi, gT_lo)]
                    ws = [lambda q, w=w: down_cols(w[:, k, :], q) for w in (sw_hi, sw_lo)]
                    for q in range(FC):
                        for j, (a, z) in enumerate(((0, 0), (0, 1), (1, 0))):
                            last = pe.matmul(ps_y[:], gT[a](q), ws[z](q), start=(k == 0 and q == 0 and j == 0),
                                             stop=(k == 1 and q == FC - 1 and j == 2))
                    if k == 1:
                        last.then_inc(s["y_done"], 1)

                def router(n):
                    need(pe, s["slots_done"], n)
                    passes(ps_r[:, 0, :], xT, [lambda q, w=w: w[:, q, :] for w in (gw_hi, gw_lo)], DC).then_inc(s["r_logits"], 1)

                def ranks(n):
                    pe.wait_ge(s["both_done"], n + 1)
                    pe.matmul(ps_r[:, 1, :], before[:], both[:], start=True, stop=False)
                    pe.matmul(ps_r[:, 1, :], ones[:], both_sum[:], start=False, stop=True).then_inc(s["rank_done"], 1)

                def one(n, b, t, last):
                    pe.wait_ge(s["x2_done"], n + 1)
                    for q in range(DC):
                        z = pe.transpose(ps_xT[:, q * P:(q + 1) * P], x2[:, t % 2, q * P:(q + 1) * P], c.ident[:])
                    z.then_inc(s["x2_turned"], 1)
                    if not last:
                        scores(*following(n, b, t))
                    pe.wait_ge(s["lo_done2"], n + 1)
                    gate(n, 0)
                    up(n, 0)
                    router(n)
                    gate(n, 1)
                    turn(n, 0)
                    ranks(n)
                    up(n, 1)
                    down(n, 0)
                    turn(n, 1)
                    down(n, 1)

                pe.wait_ge(s["setup"], 1)
                pe.wait_ge(s["const_step"], 3)
                scores(0, 0, 0)
                tiles(pe, one)


NJ = 2 * T // P + E - 1
ROWS = E * T + NJ * P


def plan(nc, c):
    with ExitStack() as ctx:
        m = Memory(nc, ctx)
        ones = m.sb("plan_ones", [P, P], BF16)
        count = m.sb("count", [P, E])
        at_i = m.sb("at_i", [P, NT], I32)
        at = m.sb("at", [P, NT])
        more = m.sb("more", [P, E, NT])
        length = m.sb("length", [P, E])
        end = m.sb("end", [P, E])
        tile_i = m.sb("tile_i", [P, NJ], I32)
        tile = m.sb("tile", [P, NJ])
        past = m.sb("past", [P, NJ, E])
        gone = m.sb("gone", [P, NJ, E])
        e_of = m.sb("e_of", [P, NJ])
        start = m.sb("start", [P, NJ])
        row = m.sb("row", [P, NJ])
        shift = m.sb("shift_e", [P, E])
        is_e = m.sb("is_e", [P, NT * 2, E])
        moved = m.sb("moved", [P, NT * 2])
        ps_count = m.ps("ps_count", [P, E])
        built, counted, step = m.sem("plan_built"), m.sem("counted"), m.sem("plan_step")
        with nc.Block() as block:
            @block.gpsimd
            def _(pool):
                pool.memset(ones[:], 1.0)
                pool.iota(at_i[:], pattern=[[P, NT]], base=0, channel_multiplier=0)
                pool.iota(tile_i[:], pattern=[[1, NJ]], base=0, channel_multiplier=0).then_inc(built, 1)

            @block.tensor
            def _(pe):
                pe.wait_ge(built, 1)
                pe.matmul(ps_count[:], ones[:], c.both_sum[:], start=True, stop=True).then_inc(counted, 1)

            @block.vector
            def _(dve):
                k = [0]

                def link(ins):
                    k[0] += 1
                    ins.then_inc(step, 1)
                    dve.wait_ge(step, k[0])

                dve.wait_ge(built, 1)
                dve.tensor_copy(at[:], at_i[:])
                link(dve.tensor_copy(tile[:], tile_i[:]))
                dve.wait_ge(counted, 1)
                link(dve.tensor_copy(count[:], ps_count[:]))
                link(dve.tensor_tensor(more[:], count[:].rearrange("p (e a) -> p e a", a=1).to_broadcast([P, E, NT]),
                                       at[:].rearrange("p (a n) -> p a n", a=1).to_broadcast([P, E, NT]), ALU.is_gt))
                link(dve.tensor_reduce(length[:], more[:], axis=AX.X, op=ALU.add))
                link(dve.tensor_copy(end[:], length[:]))
                for e in range(1, E):
                    link(dve.tensor_tensor(end[:, e:e + 1], end[:, e:e + 1], end[:, e - 1:e], ALU.add))
                link(dve.tensor_tensor(past[:], tile[:].rearrange("p (j a) -> p j a", a=1).to_broadcast([P, NJ, E]),
                                       end[:].rearrange("p (a e) -> p a e", a=1).to_broadcast([P, NJ, E]), ALU.is_ge))
                dve.tensor_tensor(gone[:], past[:], length[:].rearrange("p (a e) -> p a e", a=1).to_broadcast([P, NJ, E]), ALU.mult)
                link(dve.tensor_reduce(e_of[:], past[:], axis=AX.X, op=ALU.add))
                link(dve.tensor_reduce(start[:], gone[:], axis=AX.X, op=ALU.add))
                link(dve.tensor_tensor(row[:], tile[:], start[:], ALU.subtract))
                link(dve.tensor_scalar(row[:], row[:], float(P), None, ALU.mult))
                link(dve.scalar_tensor_tensor(row[:], e_of[:], float(T), row[:], ALU.mult, ALU.add))
                dve.tensor_copy(c.first_row[:], row[0:1, :])
                link(dve.tensor_tensor(shift[:], end[:], length[:], ALU.subtract))
                link(dve.tensor_scalar(shift[:], shift[:], float(P), None, ALU.mult))
                link(dve.scalar_tensor_tensor(shift[:], tile[:, 0:E], -float(T), shift[:], ALU.mult, ALU.add))
                link(dve.tensor_tensor(is_e[:], c.choice[:].rearrange("p n (k a) -> p (n k) a", a=1).to_broadcast([P, NT * 2, E]),
                                       tile[:, 0:E].rearrange("p (a e) -> p a e", a=1).to_broadcast([P, NT * 2, E]), ALU.is_equal))
                link(dve.tensor_tensor(is_e[:], is_e[:], shift[:].rearrange("p (a e) -> p a e", a=1).to_broadcast([P, NT * 2, E]), ALU.mult))
                link(dve.tensor_reduce(moved[:], is_e[:], axis=AX.X, op=ALU.add))
                dve.tensor_tensor(c.slots[:].rearrange("p n k -> p (n k)"), c.listed[:].rearrange("p n k -> p (n k)"), moved[:], ALU.add)
                dve.tensor_scalar(c.expert_of[:], e_of[0:1, :], float(E - 1), None, ALU.min)


def experts(nc, c, w_gate, w_up, w_down, x2_dram, table_dram, y_dram):
    with ExitStack() as ctx:
        m = Memory(nc, ctx)
        w = m.sb("w_all", [P, E * WCOLS])
        who = m.sb("who", [P, 2, 1], U32)
        xg = m.sb("xg", [P, 2, D])
        xT = m.sb("xgT", [P, 2, D])
        act_g = m.sb("e_act", [P, 2, FH])
        g = m.sb("e_g", [P, 2, FC * P])
        gT = m.sb("e_gT", [P, 2, FC * P])
        y = m.sb("e_y", [P, 2, D])
        ps_xT = m.ps("e_ps_xT", [P, D])
        ps_g = m.ps("e_ps_g", [P, S])
        ps_u = m.ps("e_ps_u", [P, S])
        ps_gT = m.ps("e_ps_gT", [P, FC * P])
        ps_y = m.ps("e_ps_y", [P, D])
        names = "w_in who0 who1 x_in0 x_in1 turned xT_done g_done silu_done u_done g_ready gT_turned gT_done y_done y_out y_st0 y_st1 padded".split()
        s = {k: m.sem("e_" + k) for k in names}
        top = E * T + (NJ - 1) * P

        def pairs(eng, one, first, last):
            assert first % 2 == 1 and (last - first) % 2 == 1
            one(first, 1)
            one(first + 1, 0)
            with eng.Fori(1, (last - first + 1) // 2) as i:
                one(2 * i + first, 1)
                one(2 * i + first + 1, 0)

        with nc.Block() as block:
            @block.sync
            def _(sp):
                def list_in(j, p):
                    need(sp, s[f"x_in{p}"], 16 * ((j - p) // 2) if isinstance(j, int) else 8 * (j - p))
                    row = sp.value_load(c.first_row[0:1, bass.ds(j, 1)], min_val=0, max_val=top)
                    sp.dma_start(who[:, p, :], table_dram[bass.ds(row, P), :], allow_slow_non_contiguous=True).then_inc(s[f"who{p}"], 16)

                def weights_in(e):
                    base = e * WCOLS
                    src = [w_gate[e].rearrange("(c p) h -> p c h", p=P), w_up[e].rearrange("(c p) h -> p c h", p=P)]
                    for up in range(2):
                        sp.dma_start(w[:, base + up * DC * FH:base + (up + 1) * DC * FH].rearrange("p (c h) -> p c h", h=FH),
                                     src[up]).then_inc(s["w_in"], 16)
                    down = w[:, base + 2 * DC * FH:base + WCOLS].rearrange("p (c d) -> p c d", d=D)
                    sp.dma_start(down[:, 0:2, :], w_down[e, 0:2 * P, :].rearrange("(c p) d -> p c d", p=P)).then_inc(s["w_in"], 16)
                    sp.dma_start(down[0:FCR, 2, :], w_down[e, 2 * P:FH, :]).then_inc(s["w_in"], 16)

                list_in(0, 0)
                list_in(1, 1)
                for e in range(E):
                    if e:
                        sp.wait_ge(s["w_in"], 64 * e)
                    weights_in(e)
                    list_in(e + 2, e % 2)
                first = E + 2
                with sp.Fori(0, (NJ - first) // 2) as i:
                    list_in(2 * i + first, 0)
                    list_in(2 * i + first + 1, 1)
                if (NJ - first) % 2:
                    list_in(NJ - 1, 0)

            @block.gpsimd
            def _(pool):
                def gather(j, p):
                    pool.wait_ge(s[f"who{p}"], 16 * ((j - p) // 2) + 16 if isinstance(j, int) else 8 * (j - p) + 16)
                    need(pool, s["turned"], j - 1)
                    pool.sem_inc(c.pool_passed, 1)
                    pool.indirect_dma_start(out=xg[:, p, :], out_offset=None, in_=x2_dram[:],
                                            in_offset=bass.IndirectOffsetOnAxis(ap=who[:, p, :], axis=0)).then_inc(s[f"x_in{p}"], 16)

                pool.memset(g[:], 0.0).then_inc(s["padded"], 1)
                gather(0, 0)
                pairs(pool, gather, 1, NJ - 1)

            @block.scalar
            def _(act):
                def x_out(j, p):
                    act.wait_ge(s["turned"], j + 1)
                    act.activation(xT[:, p, :], ps_xT[:], ACT.Copy).then_inc(s["xT_done"], 1)

                def silu(j, p):
                    act.wait_ge(s["g_done"], j + 1)
                    act.activation(act_g[:, p, :], ps_g[:, 0:FH], ACT.Silu).then_inc(s["silu_done"], 1)

                def y_store(j, p):
                    act.wait_ge(s["y_done"], j + 1)
                    need(act, s[f"y_st{p}"], 16 * ((j - p) // 2) if isinstance(j, int) else 8 * (j - p))
                    act.activation(y[:, p, :], ps_y[:], ACT.Copy).then_inc(s["y_out"], 1)
                    act.wait_ge(s["y_out"], j + 1)
                    act.dma_start(y_dram[bass.ds(j * P, P), :], y[:, p, :]).then_inc(s[f"y_st{p}"], 16)

                def one(j, p, first=False, last=False):
                    if not last:
                        x_out(j + 1, 1 - p)
                    silu(j, p)
                    if not first:
                        y_store(j - 1, 1 - p)

                x_out(0, 0)
                one(0, 0, first=True)
                pairs(act, one, 1, NJ - 3)
                one(NJ - 2, 1)
                one(NJ - 1, 0, last=True)
                y_store(NJ - 1, 0)
                act.wait_ge(s["y_st0"], 16 * ((NJ + 1) // 2))
                act.wait_ge(s["y_st1"], 16 * (NJ // 2))

            @block.vector
            def _(dve):
                def multiply(j, p):
                    dve.wait_ge(s["u_done"], j + 1)
                    dve.wait_ge(s["silu_done"], j + 1)
                    dve.tensor_tensor(g[:, p, 0:FH], act_g[:, p, :], ps_u[:, 0:FH], ALU.mult).then_inc(s["g_ready"], 1)

                def gT_out(j, p):
                    dve.wait_ge(s["gT_turned"], j + 1)
                    dve.tensor_copy(gT[:, p, :], ps_gT[:]).then_inc(s["gT_done"], 1)

                def one(j, p, first=False):
                    if not first:
                        gT_out(j - 1, 1 - p)
                    multiply(j, p)

                dve.wait_ge(s["padded"], 1)
                one(0, 0, first=True)
                pairs(dve, one, 1, NJ - 1)
                gT_out(NJ - 1, 0)

            @block.tensor
            def _(pe):
                def weights_of(j):
                    e = pe.value_load(c.expert_of[0:1, bass.ds(j, 1)], min_val=0, max_val=E - 1)
                    pe.wait_ge(s["w_in"], 64 * e + 64)
                    return e * WCOLS

                def x_turn(j, p):
                    pe.wait_ge(s[f"x_in{p}"], 16 * ((j - p) // 2) + 16 if isinstance(j, int) else 8 * (j - p) + 16)
                    need(pe, s["xT_done"], j)
                    for q in range(DC):
                        last = pe.transpose(ps_xT[:, q * P:(q + 1) * P], xg[:, p, q * P:(q + 1) * P], c.ident[:])
                    last.then_inc(s["turned"], 1)

                def hidden(j, p, base, up):
                    if not up:
                        pe.wait_ge(s["xT_done"], j + 1)
                    need(pe, s["g_ready"] if up else s["silu_done"], j)
                    for q in range(DC):
                        last = pe.matmul((ps_u if up else ps_g)[:, 0:FH], xT[:, p, q * P:(q + 1) * P],
                                         w[:, bass.ds(base + (up * DC + q) * FH, FH)], start=(q == 0), stop=(q == DC - 1))
                    last.then_inc(s["u_done"] if up else s["g_done"], 1)

                def g_turn(j, p):
                    pe.wait_ge(s["g_ready"], j + 1)
                    need(pe, s["gT_done"], j)
                    for q in range(FC):
                        last = pe.transpose(ps_gT[:, q * P:(q + 1) * P], g[:, p, q * P:(q + 1) * P], c.ident[:])
                    last.then_inc(s["gT_turned"], 1)

                def down(j, p, base):
                    pe.wait_ge(s["gT_done"], j + 1)
                    need(pe, s["y_out"], j)
                    for q in range(FC):
                        rows = P if q < FC - 1 else FCR
                        last = pe.matmul(ps_y[:], gT[0:rows, p, q * P:(q + 1) * P],
                                         w[0:rows, bass.ds(base + 2 * DC * FH + q * D, D)], start=(q == 0), stop=(q == FC - 1))
                    last.then_inc(s["y_done"], 1)

                def one(j, p, first=False, last=False):
                    if not last:
                        x_turn(j + 1, 1 - p)
                    base = weights_of(j)
                    hidden(j, p, base, 0)
                    if not first:
                        g_turn(j - 1, 1 - p)
                    hidden(j, p, base, 1)
                    if not first:
                        down(j - 1, 1 - p, weights_of(j - 1))

                x_turn(0, 0)
                one(0, 0, first=True)
                pairs(pe, one, 1, NJ - 3)
                one(NJ - 2, 1)
                one(NJ - 1, 0, last=True)
                g_turn(NJ - 1, 0)
                down(NJ - 1, 0, weights_of(NJ - 1))


def combine(nc, c, y_dram, out):
    with ExitStack() as ctx:
        m = Memory(nc, ctx)
        place = m.sb("place_now", [P, 2, 2, 1], U32)
        yy = m.sb("yy", [P, 2, 2, D])
        r3 = m.sb("r3", [P, 2, 2, D])
        stats = m.sb("stats3", [P, 6])
        mv = m.sb("mv3", [P, 2])
        rstd = m.sb("rstd3", [P, 2])
        half = m.sb("half3", [P, 1])
        o = m.sb("o", [P, 2, D])
        names = "half place y_in0 y_in1 add0 add1 stats mv ve rstd o_done o_st0 o_st1".split()
        s = {k: m.sem("c_" + k) for k in names}
        out_rows = out.rearrange("b (t p) d -> p (b t) d", p=P)

        def tiles(eng, one):
            for t in range(2):
                one(t, 0, t, True)
            for t in range(2, TT):
                one(t, 0, t, False)
            with eng.Fori(1, B) as b:
                for t in range(TT):
                    one(b * TT + t, b, t, False)

        def uses(b, t):
            return 2 * b + t // 2

        with nc.Block() as block:
            @block.gpsimd
            def _(pool):
                pool.memset(half[:], -0.5).then_inc(s["half"], 1)
                pool.wait_ge(s["half"], 1)

                def fetch(n, b, t, fresh):
                    p = t % 2
                    if not fresh:
                        pool.wait_ge(s["add1"], n - 1)
                        pool.wait_ge(s[f"y_in{p}"], 32 * uses(b, t))
                    for k in range(2):
                        last = pool.tensor_copy(place[:, p, k, :], c.slots[:, bass.ds(n, 1), k:k + 1].rearrange("p a k -> p (a k)"))
                    last.then_inc(s["place"], 1)
                    wait_apart(pool, s["place"], n + 1, c.pool_passed)
                    for k in range(2):
                        pool.indirect_dma_start(out=yy[:, p, k, :], out_offset=None, in_=y_dram[:],
                                                in_offset=bass.IndirectOffsetOnAxis(ap=place[:, p, k, :], axis=0)).then_inc(s[f"y_in{p}"], 16)

                def root(n):
                    wait_apart(pool, s["mv"], n + 1, c.pool_passed)
                    pool.tensor_scalar(rstd[:, 0:1], mv[:, 1:2], EPS, None, ALU.add).then_inc(s["ve"], 1)
                    pool.wait_ge(s["ve"], n + 1)
                    pool.tensor_tensor(rstd[:, 1:2], rstd[:, 0:1], half[:], ALU.pow).then_inc(s["rstd"], 1)

                fetch(0, 0, 0, True)
                fetch(1, 0, 1, True)
                with pool.Fori(0, B - 1) as b:
                    for t in range(TT):
                        root(b * TT + t)
                        nb, nt = (b, t + 2) if t < 2 else (b + 1, t - 2)
                        fetch(b * TT + t + 2, nb, nt, False)
                for t in range(TT):
                    n = (B - 1) * TT + t
                    root(n)
                    if t < 2:
                        fetch(n + 2, B - 1, t + 2, False)

            @block.vector
            def _(dve):
                dve.wait_ge(s["half"], 1)

                def one(n, b, t, fresh):
                    p = t % 2
                    base = c.attn[:, bass.ds(b * HG, HG), t * P:(t + 1) * P]
                    wt = [c.weights[:, bass.ds(n, 1), k:k + 1].rearrange("p a k -> p (a k)") for k in range(2)]
                    dve.wait_ge(s[f"y_in{p}"], 32 * uses(b, t) + 32)
                    dve.scalar_tensor_tensor(r3[:, p, 0, :].rearrange("p (g d) -> p g d", g=HG), yy[:, p, 0, :].rearrange("p (g d) -> p g d", g=HG),
                                             wt[0], base, ALU.mult, ALU.add).then_inc(s["add0"], 1)
                    dve.wait_ge(s["add0"], n + 1)
                    dve.scalar_tensor_tensor(r3[:, p, 1, :], yy[:, p, 1, :], wt[1], r3[:, p, 0, :], ALU.mult, ALU.add).then_inc(s["add1"], 1)
                    dve.wait_ge(s["add1"], n + 1)
                    dve.bn_stats(stats[:], r3[:, p, 1, :]).then_inc(s["stats"], 1)
                    wait_apart(dve, s["stats"], n + 1, c.dve_passed)
                    dve.bn_aggr(mv[:], stats[:]).then_inc(s["mv"], 1)
                    dve.wait_ge(s["rstd"], n + 1)
                    if not fresh:
                        dve.wait_ge(s[f"o_st{p}"], 16 * uses(b, t))
                    dve.tensor_scalar(o[:, p, :], r3[:, p, 1, :], mv[:, 0:1], rstd[:, 1:2], ALU.subtract, ALU.mult).then_inc(s["o_done"], 1)

                tiles(dve, one)

            @block.sync
            def _(sp):
                def one(n, b, t, fresh):
                    sp.wait_ge(s["o_done"], n + 1)
                    sp.dma_start(out_rows[:, bass.ds(n, 1), :].rearrange("p a d -> p (a d)"), o[:, t % 2, :]).then_inc(s[f"o_st{t % 2}"], 16)

                tiles(sp, one)
                for k in range(2):
                    sp.wait_ge(s[f"o_st{k}"], 8 * NT)


def decoder(nc, x, ctx_512, mask_SxS2_bk1, mask_BxS2_bf0, L0_attn_Wq, L0_attn_bq, L0_attn_Wk, L0_attn_bk,
            L0_attn_Wv, L0_attn_bv, L0_xattn_Wq, L0_xattn_bq, L0_xattn_Wk, L0_xattn_bk, L0_ffn_gate_w,
            L0_ffn_w_gate, L0_ffn_w_up, L0_ffn_w_down, L0_ffn_sw_gate, L0_ffn_sw_up, L0_ffn_sw_down, out):
    def dram(name, shape, dt=F32):
        return nc.dram_tensor(name, shape, dt, kind="Internal").ap()

    qk_dram = dram("qk_dram", [2, 2, U, P, S])
    norm_dram = dram("norm_dram", [B * H, S])
    x2_dram = dram("x2_dram", [T, D])
    table_dram = dram("table_dram", [ROWS, 1], U32)
    y_dram = dram("y_dram", [NJ * P, D])

    with ExitStack() as ctx:
        m = Memory(nc, ctx)
        c = Kept()
        c.pool_passed, c.dve_passed = m.sem("pool_passed"), m.sem("dve_passed")
        build_constants(nc, m, c, table_dram)
        c.weights = m.sb("weights", [P, NT, 2])
        c.slots = m.sb("slots", [P, NT, 2], U32)
        c.listed = m.sb("listed", [P, NT, 2])
        c.choice = m.sb("choice", [P, NT, 2])
        c.both_sum = m.sb("both_sum", [P, E], BF16)
        c.first_row = m.sb("first_row", [1, NJ], I32)
        c.expert_of = m.sb("expert_of", [1, NJ], I32)
        c.bar = m.sb("bar_kept", [P, TT, B * H])
        c.attn = m.sb("attn", [P, U, S])
        with ExitStack() as ctx2:
            m2 = Memory(nc, ctx2)
            c.qk_ctx = [[m2.sb(f"qk_ctx{a}{b}", [P, B * S], F32R) for b in range(2)] for a in range(2)]
            with ExitStack() as ctx3:
                c.v = Memory(nc, ctx3).sb("v", [P, U, TT * P])
                project(nc, c, x, L0_attn_Wq, L0_attn_bq, L0_attn_Wk, L0_attn_bk, L0_attn_Wv, L0_attn_bv, qk_dram, norm_dram)
                choose_queries(nc, c, norm_dram, ctx_512, L0_xattn_Wq, L0_xattn_bq, L0_xattn_Wk, L0_xattn_bk)
                attend(nc, c, qk_dram)
            cross_and_shared(nc, c, x, mask_SxS2_bk1, mask_BxS2_bf0, L0_ffn_gate_w, L0_ffn_sw_gate, L0_ffn_sw_up,
                             L0_ffn_sw_down, x2_dram, table_dram)
        plan(nc, c)
        experts(nc, c, L0_ffn_w_gate, L0_ffn_w_up, L0_ffn_w_down, x2_dram, table_dram, y_dram)
        combine(nc, c, y_dram, out)


_INS = ["x", "ctx_512", "mask_SxS2_bk1", "mask_BxS2_bf0", "L0_attn_Wq", "L0_attn_bq", "L0_attn_Wk", "L0_attn_bk",
        "L0_attn_Wv", "L0_attn_bv", "L0_xattn_Wq", "L0_xattn_bq", "L0_xattn_Wk", "L0_xattn_bk", "L0_ffn_gate_w",
        "L0_ffn_w_gate", "L0_ffn_w_up", "L0_ffn_w_down", "L0_ffn_sw_gate", "L0_ffn_sw_up", "L0_ffn_sw_down"]


def kernel(**inputs):
    import numpy as _np
    import concourse.bacc as _bacc
    from concourse import mybir as _mybir
    from concourse.bass_utils import run_bass_kernel_spmd as _run

    nc = _bacc.Bacc("TRN2", target_bir_lowering=False, num_devices=1)
    arrays, args = {}, []
    for name in _INS:
        a = _np.ascontiguousarray(inputs[name])
        arrays[f"in_{name}_dram"] = a
        args.append(nc.dram_tensor(f"in_{name}_dram", a.shape, _mybir.dt.from_np(a.dtype), kind="ExternalInput").ap())
    shape = tuple(inputs["x"].shape)
    out = nc.dram_tensor("out_0_dram", shape, _mybir.dt.float32, kind="ExternalOutput").ap()
    decoder(nc, *args, out)
    r = _run(nc, [arrays], core_ids=[0])
    return r.results[0]["out_0_dram"]
```

```python
from contextlib import ExitStack

import concourse.bass as bass
from concourse import mybir

P = 128
F32 = mybir.dt.float32
F32R = mybir.dt.float32r
BF16 = mybir.dt.bfloat16
I32 = mybir.dt.int32
U32 = mybir.dt.uint32
U8 = mybir.dt.uint8
ALU = mybir.AluOpType
ACT = mybir.ActivationFunctionType
AX = mybir.AxisListType

B, S, D = 4, 512, 512
H, HD = 16, 32
DC = D // P
TT = S // P
HG = H * HD // P
HPG = P // HD
U = B * HG
BLOCK, TOPK = 128, 64
NEG_SEL = -1.0e30
SENTINEL = 3.0e38


class Memory:

    def __init__(self, nc, ctx):
        self.nc, self.ctx, self.sems = nc, ctx, []

    def sb(self, name, shape, dt=F32):
        return self.ctx.enter_context(self.nc.sbuf_tensor(name, shape, dt))

    def ps(self, name, shape, dt=F32):
        return self.ctx.enter_context(self.nc.psum_tensor(name, shape, dt))

    def sem(self, name):
        if not self.sems:
            self.ctx.callback(self.clear)
        self.sems.append(self.nc.alloc_semaphore(name=name))
        return self.sems[-1]

    def clear(self):
        self.nc.clear_and_free_semaphores(self.sems)
        self.nc.all_engine_barrier()


def wait_apart(eng, sem, value, passed):
    eng.wait_ge(sem, value)
    eng.sem_inc(passed, 1)


class Kept:
    pass


def build_constants(nc, m, c, table_dram):
    c.ident = m.sb("ident", [P, P])
    c.ident_bf = m.sb("ident_bf", [P, P], BF16)
    c.head_cols = m.sb("head_cols", [P, HG, H])
    R = 3 * HD
    c.window = m.sb("window", [P, S])
    zeros = m.sb("zeros", [P, table_dram.shape[0] // P], U32)
    built, cleared, table_out = m.sem("constants_step"), m.sem("zeros_done"), m.sem("table_out")
    with nc.Block() as block:
        @block.vector
        def _(dve):
            dve.memset(zeros[:], 0).then_inc(cleared, 1)

        @block.sync
        def _(sp):
            sp.wait_ge(cleared, 1)
            sp.dma_start(table_dram.rearrange("(p n) a -> p (n a)", p=P), zeros[:]).then_inc(table_out, 16)
            sp.wait_ge(table_out, 16)

        @block.gpsimd
        def _(pool):
            pool.memset(c.ident[:], 0.0)
            pool.memset(c.ident_bf[:], 0.0)
            pool.memset(c.window[:], 0.0)
            pool.memset(c.head_cols[:], 1.0).then_inc(built, 1)
            pool.wait_ge(built, 1)
            for t in (c.ident, c.ident_bf):
                pool.affine_select(out=t[:], in_=t[:], compare_op=ALU.not_equal, fill=1.0, base=0,
                                   pattern=[[-1, P]], channel_multiplier=1)
            pool.affine_select(out=c.head_cols[:], in_=c.head_cols[:], compare_op=ALU.is_ge, fill=0.0,
                               base=0, pattern=[[P, HG], [-HD, H]], channel_multiplier=1).then_inc(built, 1)
            pool.wait_ge(built, 2)
            pool.affine_select(out=c.head_cols[:], in_=c.head_cols[:], compare_op=ALU.is_ge, fill=0.0,
                               base=HD - 1, pattern=[[-P, HG], [HD, H]], channel_multiplier=-1)
            n = 2
            for row in (R, R + 1):
                pool.affine_select(out=c.window[:], in_=c.window[:], compare_op=ALU.not_equal, fill=1.0, base=-row,
                                   pattern=[[0, S]], channel_multiplier=1).then_inc(built, 1)
                n += 1
                pool.wait_ge(built, n)
            for t in range(TT):
                lo, hi = max(0, BLOCK * t - BLOCK // 2), min(S, BLOCK * t + 3 * BLOCK // 2)
                for a, b in ((0, lo), (hi, S)):
                    if b > a:
                        pool.affine_select(out=c.window[:, a:b], in_=c.window[:, a:b], compare_op=ALU.not_equal,
                                           fill=1.0, base=-(R + 2 + t), pattern=[[0, b - a]],
                                           channel_multiplier=1).then_inc(built, 1)
                        n += 1
                        pool.wait_ge(built, n)


def project(nc, c, x, wq, bq, wk, bk, wv, bv, qk_dram, norm_dram):
    with ExitStack() as ctx:
        m = Memory(nc, ctx)
        w_raw = c.attn[:, 0:2 * DC, :].rearrange("p (n c) d -> p n c d", c=DC)
        w_hi = m.sb("w_hi", [P, 3, DC, D], F32R)
        w_lo = m.sb("w_lo", [P, 3, DC, D], F32R)
        x_in = m.sb("x_in", [P, TT, D])
        xT_hi = m.sb("xT_hi", [P, DC, S], F32R)
        xT_lo = m.sb("xT_lo", [P, DC, S], F32R)
        bias_qk = m.sb("bias_qk", [P, 2, HG])
        bias_v = m.sb("bias_v", [P, D])
        raw = c.attn[:, 2 * DC:2 * DC + 4, :]
        parts = m.sb("parts", [P, 4, 2, S], F32R)
        squares = c.attn[:, 2 * DC + 4:2 * DC + 8, :]
        norm_sb = m.sb("norm_sb", [H, S])
        ps_tr = m.ps("ps_tr", [P, 2, S])
        ps_proj = m.ps("ps_proj", [P, 4, S])
        ps_norm = m.ps("ps_norm", [H, S])

        w_loaded = [m.sem(f"w_loaded{n}") for n in range(3)]
        bias_loaded, x_loaded = m.sem("bias_loaded"), m.sem("x_loaded")
        w_hi_done, w_split = m.sem("w_hi_done"), m.sem("w_split")
        x_turned, xT_hi_done, xT_lo_done = m.sem("x_turned"), m.sem("xT_hi_done"), m.sem("xT_lo_done")
        proj_done, qk_out, v_out = m.sem("proj_done"), m.sem("qk_out"), m.sem("v_out")
        hi_done, lo_done, raw_used = m.sem("hi_done"), m.sem("lo_done"), m.sem("raw_used")
        parts_stored = [m.sem(f"parts_stored{k}") for k in range(4)]
        squares_done, norm_acc, norm_out, norm_stored = (
            m.sem("squares_done"), m.sem("norm_acc"), m.sem("norm_out"), m.sem("norm_stored"))

        with nc.Block() as block:
            @block.sync
            def _(sp):
                for n, w in enumerate((wq, wk, wv)):
                    if n == 2:
                        sp.wait_ge(w_split, 1)
                    sp.dma_start(w_raw[:, n % 2], w.rearrange("(c p) n -> p c n", p=P)).then_inc(w_loaded[n], 16)
                    if n == 0:
                        sp.dma_start(x_in[:], x[0:1].rearrange("b (t p) d -> p (b t) d", p=P)).then_inc(x_loaded, 16)
                def store_parts(i):
                    for n in range(2 * HG):
                        sp.wait_ge(lo_done, 2 * HG * i + n + 1)
                        sp.dma_start(qk_dram[n // HG, :, bass.ds(i * HG + n % HG, 1)].rearrange("h a p n -> (a p) h n"),
                                     parts[:, n % 4].bitcast(F32)).then_inc(parts_stored[n % 4], 16)

                with sp.Fori(0, B - 1) as i:
                    sp.wait_ge(x_turned, 4 * i + 4)
                    sp.dma_start(x_in[:], x[bass.ds(i + 1, 1)].rearrange("b (t p) d -> p (b t) d", p=P)).then_inc(x_loaded, 16)
                    store_parts(i)
                store_parts(B - 1)
                for k in range(4):
                    sp.wait_ge(parts_stored[k], 32 * B + 16)
                sp.wait_ge(norm_stored, 16 * B + 16)

            @block.scalar
            def _(act):
                act.dma_start(bias_qk[:, 0, :], bq.rearrange("(g p) -> p g", p=P), allow_slow_non_contiguous=True).then_inc(bias_loaded, 16)
                act.dma_start(bias_qk[:, 1, :], bk.rearrange("(g p) -> p g", p=P), allow_slow_non_contiguous=True).then_inc(bias_loaded, 16)
                act.dma_start(bias_v[:], bv.rearrange("(a n) -> a n", a=1).to_broadcast([P, D])).then_inc(bias_loaded, 16)
                for n in range(3):
                    act.wait_ge(w_loaded[n], 16)
                    act.activation(w_hi[:, n], w_raw[:, n % 2], ACT.Copy).then_inc(w_hi_done, 1)
                act.wait_ge(bias_loaded, 48)
                with act.Fori(0, B) as i:
                    for dc in range(DC):
                        act.wait_ge(x_turned, 4 * i + dc + 1)
                        if dc == 0:
                            act.wait_ge(v_out, 4 * i + 4)
                        act.activation(xT_hi[:, dc, :], ps_tr[:, dc % 2, :], ACT.Copy).then_inc(xT_hi_done, 1)
                    for n in range(2 * HG):
                        act.wait_ge(proj_done, 12 * i + n + 1)
                        act.wait_ge(raw_used, 8 * i + n + 1)
                        act.activation(raw[:, n % 4, :], ps_proj[:, n % 4, :], ACT.Identity,
                                       bias=bias_qk[:, n // HG, n % HG:n % HG + 1]).then_inc(qk_out, 1)
                    act.wait_ge(norm_acc, i + 2)
                    act.wait_ge(norm_stored, 16 * i + 16)
                    act.activation(norm_sb[:], ps_norm[:], ACT.Copy).then_inc(norm_out, 1)
                    act.wait_ge(norm_out, i + 2)
                    act.dma_start(norm_dram[bass.ds(i * H, H), :], norm_sb[:]).then_inc(norm_stored, 16)

            @block.vector
            def _(dve):
                for n in range(3):
                    dve.wait_ge(w_hi_done, n + 1)
                    dve.tensor_tensor(w_lo[:, n], w_raw[:, n % 2], w_hi[:, n].bitcast(F32), ALU.subtract).then_inc(w_split, 1)
                dve.wait_ge(bias_loaded, 48)
                with dve.Fori(0, B) as i:
                    for dc in range(DC):
                        dve.wait_ge(xT_hi_done, 4 * i + dc + 1)
                        dve.tensor_tensor(xT_lo[:, dc, :], ps_tr[:, dc % 2, :], xT_hi[:, dc, :].bitcast(F32),
                                          ALU.subtract).then_inc(xT_lo_done, 1)
                    for n in range(2 * HG):
                        dve.wait_ge(qk_out, 8 * i + n + 1)
                        dve.wait_ge(parts_stored[n % 4], 32 * i + 16 * (n // 4) + 16)
                        dve.tensor_copy(parts[:, n % 4, 0, :], raw[:, n % 4, :]).then_inc(hi_done, 1)
                    for t in range(TT):
                        n = 2 * HG + t
                        dve.wait_ge(proj_done, 12 * i + n + 1)
                        dve.tensor_tensor(c.v[:, bass.ds(i * HG, HG), t * P:(t + 1) * P],
                                          ps_proj[:, n % 4, :].rearrange("p (g d) -> p g d", g=HG),
                                          bias_v[:].rearrange("p (g d) -> p g d", g=HG), ALU.add).then_inc(v_out, 1)

            @block.gpsimd
            def _(pool):
                pool.sem_inc(v_out, 4)
                pool.sem_inc(norm_stored, 16)
                pool.sem_inc(norm_out, 1)
                pool.sem_inc(norm_acc, 1)
                pool.sem_inc(raw_used, 4)
                for k in range(4):
                    pool.sem_inc(parts_stored[k], 16)
                with pool.Fori(0, B) as i:
                    pool.wait_ge(norm_acc, i + 1)
                    for n in range(2 * HG):
                        pool.wait_ge(hi_done, 8 * i + n + 1)
                        if n < HG:
                            pool.tensor_tensor(squares[:, n, :], raw[:, n, :], raw[:, n, :], ALU.mult).then_inc(squares_done, 1)
                        pool.tensor_tensor(parts[:, n % 4, 1, :], raw[:, n % 4, :], parts[:, n % 4, 0, :].bitcast(F32),
                                           ALU.subtract).then_inc(lo_done, 1)
                        pool.wait_ge(lo_done, 8 * i + n + 1)
                        if n < HG:
                            pool.wait_ge(squares_done, 4 * i + n + 1)
                        pool.sem_inc(raw_used, 1)

            @block.tensor
            def _(pe):
                pe.wait_ge(w_split, 3)
                with pe.Fori(0, B) as i:
                    pe.wait_ge(x_loaded, 16 * i + 16)
                    for dc in range(DC):
                        if dc >= 2:
                            pe.wait_ge(xT_lo_done, 4 * i + dc - 1)
                        for t in range(TT):
                            last = pe.transpose(ps_tr[:, dc % 2, t * P:(t + 1) * P],
                                                x_in[:, t, dc * P:(dc + 1) * P], c.ident[:])
                        last.then_inc(x_turned, 1)

                    def product(n, stationary, moving):
                        if n < 4:
                            pe.wait_ge(v_out, 4 * i + n + 1)
                        else:
                            pe.wait_ge(qk_out, 8 * i + n - 3)
                        for dc in range(DC):
                            if n == 0:
                                pe.wait_ge(xT_lo_done, 4 * i + dc + 1)
                            for k, (a, b) in enumerate(((0, 0), (0, 1), (1, 0))):
                                last = pe.matmul(ps_proj[:, n % 4, :], stationary[a](dc), moving[b](dc),
                                                 start=(dc == 0 and k == 0), stop=(dc == DC - 1 and k == 2))
                        last.then_inc(proj_done, 1)

                    for n in range(2 * HG):
                        g, which = n % HG, n // HG
                        product(n, [lambda dc, w=w: w[:, which, dc, g * P:(g + 1) * P] for w in (w_hi, w_lo)],
                                [lambda dc, t=t: t[:, dc, :] for t in (xT_hi, xT_lo)])
                    pe.wait_ge(norm_out, i + 1)
                    for g in range(HG):
                        pe.wait_ge(squares_done, 4 * i + g + 1)
                        last = pe.matmul(ps_norm[:], c.head_cols[:, g, :], squares[:, g, :],
                                         start=(g == 0), stop=(g == HG - 1))
                    last.then_inc(norm_acc, 1)
                    for t in range(TT):
                        product(2 * HG + t, [lambda dc, x=x_: x[:, dc, t * P:(t + 1) * P] for x_ in (xT_hi, xT_lo)],
                                [lambda dc, w=w: w[:, 2, dc, :] for w in (w_hi, w_lo)])


def choose_queries(nc, c, norm_dram, context, x_wq, x_bq, x_wk, x_bk):
    with ExitStack() as ctx:
        m = Memory(nc, ctx)
        work = m.sb("work", [B * H, S + 2])
        top8 = m.sb("top8", [B * H, 8])
        bar = m.sb("bar", [B * H, S])
        w_in = m.sb("xw_in", [P, 2, P])
        w_sb = m.sb("xw_sb", [P, 2, P])
        wT_hi = m.sb("xwT_hi", [P, 2, P], F32R)
        wT_lo = m.sb("xwT_lo", [P, 2, P], F32R)
        bias = m.sb("x_bias", [P, 2])
        c_in = m.sb("c_in", [P, TT, P])
        cT = m.sb("cT", [P, S])
        cT_hi = m.sb("cT_hi", [P, S], F32R)
        cT_lo = m.sb("cT_lo", [P, S], F32R)
        c_raw = m.sb("c_raw", [P, 2, S])
        ps_bar = m.ps("ps_bar", [P, TT, B * H])
        ps_w = m.ps("ps_w", [P, 2, P])
        ps_c = m.ps("ps_c", [P, S])
        ps_qk = m.ps("ps_qk", [P, 2, S])
        loaded, step, turned = m.sem("norms_loaded"), m.sem("choose_step"), m.sem("bar_turned")
        w_loaded, b_loaded, c_loaded = m.sem("xw_loaded"), m.sem("xb_loaded"), m.sem("c_loaded")
        w_turned, w_copied, w_hi_done, w_lo_done = m.sem("xw_turned"), m.sem("xw_copied"), m.sem("xw_hi"), m.sem("xw_lo")
        c_turned, c_copied, c_hi_done, c_lo_done = m.sem("c_turned"), m.sem("c_copied"), m.sem("c_hi"), m.sem("c_lo")
        qk_done, qk_copied, qk_hi_done, qk_lo_done = m.sem("qk_done"), m.sem("qk_copied"), m.sem("qk_hi"), m.sem("qk_lo")
        with nc.Block() as block:
            @block.sync
            def _(sp):
                sp.dma_start(work[:, 0:S], norm_dram[:]).then_inc(loaded, 16)
                sp.dma_start(w_in[:, 0, :], x_wq).then_inc(w_loaded, 16)
                sp.dma_start(w_in[:, 1, :], x_wk).then_inc(w_loaded, 16)
                for n, b in enumerate((x_bq, x_bk)):
                    sp.dma_start(bias[:, n:n + 1], b.rearrange("(p a) -> p a", a=1),
                                 allow_slow_non_contiguous=True).then_inc(b_loaded, 16)
                sp.dma_start(c_in[:], context[0:1].rearrange("b (t p) d -> p (b t) d", p=P)).then_inc(c_loaded, 16)
                with sp.Fori(1, B) as i:
                    sp.wait_ge(c_turned, i)
                    sp.dma_start(c_in[:], context[bass.ds(i, 1)].rearrange("b (t p) d -> p (b t) d", p=P)).then_inc(c_loaded, 16)

            @block.vector
            def _(dve):
                dve.memset(work[:, S:S + 2], SENTINEL).then_inc(step, 1)
                dve.wait_ge(loaded, 16)
                for r in range(TOPK // 8):
                    dve.wait_ge(step, 2 * r + 1)
                    dve.max(top8[:], work[:]).then_inc(step, 1)
                    dve.wait_ge(step, 2 * r + 2)
                    dve.match_replace(work[:], top8[:], work[:], -1.0).then_inc(step, 1)
                n = TOPK // 4 + 1
                dve.wait_ge(step, n)
                dve.tensor_scalar(bar[:], work[:, 0:S], 0.0, NEG_SEL, ALU.is_ge, ALU.mult).then_inc(step, 1)
                dve.wait_ge(step, n + 1)
                dve.memset(bar[:, 0:1], 0.0)
                dve.memset(bar[:, S - 1:S], 0.0).then_inc(step, 1)
                dve.wait_ge(turned, 1)
                dve.tensor_copy(c.bar[:].rearrange("p t n -> p (t n)"),
                                ps_bar[:].rearrange("p t n -> p (t n)"))

            @block.scalar
            def _(act):
                act.wait_ge(w_turned, 1)
                act.activation(w_sb[:], ps_w[:], ACT.Copy).then_inc(w_copied, 1)
                act.activation(wT_hi[:], ps_w[:], ACT.Copy).then_inc(w_hi_done, 1)
                act.wait_ge(b_loaded, 32)
                with act.Fori(0, B) as i:
                    act.wait_ge(c_turned, i + 1)
                    act.wait_ge(c_lo_done, i + 1)
                    act.wait_ge(qk_done, 2 * i + 2)
                    act.activation(cT[:], ps_c[:], ACT.Copy).then_inc(c_copied, 1)
                    act.activation(cT_hi[:], ps_c[:], ACT.Copy).then_inc(c_hi_done, 1)
                    for n in range(2):
                        act.wait_ge(qk_done, 2 * i + n + 3)
                        act.wait_ge(qk_lo_done, 2 * i + n + 1)
                        act.activation(c_raw[:, n, :], ps_qk[:, n, :], ACT.Identity, bias=bias[:, n:n + 1]).then_inc(qk_copied, 1)

            @block.gpsimd
            def _(pool):
                pool.sem_inc(c_lo_done, 1)
                pool.sem_inc(qk_done, 2)
                pool.sem_inc(qk_lo_done, 2)
                pool.wait_ge(w_copied, 1)
                pool.wait_ge(w_hi_done, 1)
                pool.tensor_tensor(wT_lo[:], w_sb[:], wT_hi[:].bitcast(F32), ALU.subtract).then_inc(w_lo_done, 1)
                with pool.Fori(0, B) as i:
                    pool.wait_ge(c_copied, i + 1)
                    pool.wait_ge(c_hi_done, i + 1)
                    pool.tensor_tensor(cT_lo[:], cT[:], cT_hi[:].bitcast(F32), ALU.subtract).then_inc(c_lo_done, 1)
                    for n in range(2):
                        hi, lo = c.qk_ctx[n][0][:, bass.ds(i * S, S)], c.qk_ctx[n][1][:, bass.ds(i * S, S)]
                        pool.wait_ge(qk_copied, 2 * i + n + 1)
                        pool.tensor_copy(hi, c_raw[:, n, :]).then_inc(qk_hi_done, 1)
                        pool.wait_ge(qk_hi_done, 2 * i + n + 1)
                        pool.tensor_tensor(lo, c_raw[:, n, :], hi.bitcast(F32), ALU.subtract).then_inc(qk_lo_done, 1)

            @block.tensor
            def _(pe):
                pe.wait_ge(w_loaded, 32)
                for n in range(2):
                    last = pe.transpose(ps_w[:, n, :], w_in[:, n, :], c.ident[:])
                last.then_inc(w_turned, 1)
                pe.wait_ge(w_lo_done, 1)
                with pe.Fori(0, B) as i:
                    pe.wait_ge(c_loaded, 16 * i + 16)
                    for t in range(TT):
                        last = pe.transpose(ps_c[:, t * P:(t + 1) * P], c_in[:, t, :], c.ident[:])
                    last.then_inc(c_turned, 1)
                    pe.wait_ge(c_lo_done, i + 2)
                    for n in range(2):
                        pe.wait_ge(qk_lo_done, 2 * i + n + 1)
                        for k, (a, b) in enumerate(((wT_hi, cT_hi), (wT_hi, cT_lo), (wT_lo, cT_hi))):
                            last = pe.matmul(ps_qk[:, n, :], a[:, n, :], b[:], start=(k == 0), stop=(k == 2))
                        last.then_inc(qk_done, 1)
                pe.wait_ge(step, TOPK // 4 + 3)
                for t in range(TT):
                    last = pe.transpose(ps_bar[:, t, :], bar[:, t * P:(t + 1) * P], c.ident[0:B * H, 0:B * H])
                last.then_inc(turned, 1)


SCALE = float(HD) ** -0.5
NU = HPG * TT
BR = 3 * HD
NDMA = 16 * 12
SLOTS = 3
EARLY = 5
GW = 10


def need(eng, sem, value):
    if not isinstance(value, int) or value > 0:
        eng.wait_ge(sem, value)


def attend(nc, c, qk_dram):
    with ExitStack() as ctx:
        m = Memory(nc, ctx)
        q4 = m.sb("q4", [P, SLOTS, HPG, S], F32R)
        k4 = m.sb("k4", [P, SLOTS, HPG, S], F32R)
        vu = m.sb("vu", [P, TT, P])
        ones = m.sb("ones_sum", [P, HD])
        probs = m.sb("probs", [P, TT, HPG, S])
        pair_sum = m.sb("pair_sum", [P, 2, HPG, S])
        outT = m.sb("outT", [P, S])
        sumT = m.sb("sumT", [P, S])
        first_rows = m.sb("first_rows", [P, HPG])
        rsum = m.sb("rsum", [P, TT, HPG])
        maxima = m.sb("maxima", [P, TT * (HPG * GW + 2)])
        m_all = m.sb("m_all", [P, TT, HPG])
        m_win = m.sb("m_win", [P, TT, HPG])
        m_bar = m.sb("m_bar", [P, TT, HPG])
        m_row = m.sb("m_row", [P, TT, HPG])
        turn_in = m.sb("turn_in", [P, TT * (P + 1) + 4], BF16)
        ps_s = m.ps("ps_s", [P, 2, S])
        ps_st = m.ps("ps_st", [P, 2, S])
        ps_o = m.ps("ps_o", [P, S])
        ps_sum = m.ps("ps_sum", [P, S])
        ps_back = m.ps("ps_back", [P, S])
        ps_both = m.ps("ps_turn_rows", [P, S])
        ps_turn = ps_both[:, 0:S // 2].bitcast(BF16)
        ps_rows = ps_both[:, S // 2:S // 2 + TT * HPG].rearrange("p (t j) -> p t j", j=HPG)

        unit_in = [m.sem(f"unit_in{p}") for p in range(SLOTS)]
        v_in = m.sem("v_in")
        s_done, s_reduced = m.sem("s_done"), m.sem("s_reduced")
        st_done, exp_done = m.sem("st_done"), m.sem("exp_done")
        pv_done, added, sums_done = m.sem("pv_done"), m.sem("added"), m.sem("sums_done")
        evacuated, backed, recip_done, normed = m.sem("evacuated"), m.sem("backed"), m.sem("recip_done"), m.sem("normed")
        row_step, turn_ready, turned, shift_ready = m.sem("row_step"), m.sem("turn_ready"), m.sem("turned"), m.sem("shift_ready")
        cleared, window_in = m.sem("cleared"), m.sem("window_in")

        def slot(t, u):
            return t[:, bass.ds(u, 1), :].rearrange("p a n -> p (a n)")

        def units(eng, unit):
            unit(0, 0, 0)
            rounds = (U - 2) // SLOTS
            with eng.Fori(0, rounds) as i:
                for k in range(1, SLOTS + 1):
                    unit(SLOTS * i + k, k % SLOTS, i + k // SLOTS)
            for u in range(SLOTS * rounds + 1, U):
                unit(u, u % SLOTS, u // SLOTS)

        def is_last(u):
            return isinstance(u, int) and u == U - 1

        with nc.Block() as block:
            @block.gpsimd
            def _(pool):
                pool.sem_inc(backed, 1)
                pool.sem_inc(normed, 1)
                pool.memset(ones[:], 1.0)
                pool.memset(turn_in[:], 0.0)
                pool.memset(first_rows[:], 0.0)
                pool.memset(maxima[:], -SENTINEL).then_inc(cleared, 1)
                pool.wait_ge(cleared, 1)
                pool.affine_select(out=first_rows[:], in_=first_rows[:], compare_op=ALU.not_equal, fill=1.0, base=0,
                                   pattern=[[-HD, HPG]], channel_multiplier=1).then_inc(cleared, 1)

                def unit(u, p, uses):
                    need(pool, pv_done, TT * u)
                    pool.tensor_copy(vu[:].rearrange("p t d -> p (t d)"), slot(c.v, u)).then_inc(v_in, 1)
                    for h in range(2):
                        pool.wait_ge(exp_done, NU * u + 2 * HPG * (h + 1))
                        need(pool, sums_done, 2 * (u - 1) + h + 1)
                        pool.tensor_tensor(pair_sum[:, h], probs[:, 2 * h], probs[:, 2 * h + 1], ALU.add).then_inc(added, 1)

                units(pool, unit)

            @block.sync
            def _(sp):
                def load_unit(u, p, first):
                    if not first:
                        sp.wait_ge(st_done, NU * (u - SLOTS + 1))
                    for k in range(2):
                        for r in range(3):
                            for tile, which, part in ((q4, 0, r // 2), (k4, 1, r % 2)):
                                src = qk_dram[which, part, bass.ds(u, 1), 2 * HD * k:2 * HD * (k + 1)]
                                sp.dma_start(tile[HD * r:HD * (r + 1), p, 2 * k:2 * k + 2, :].bitcast(F32),
                                             src.rearrange("a (j p) n -> p (a j) n", p=HD)).then_inc(unit_in[p], 16)

                for u in range(SLOTS):
                    load_unit(u, u, True)
                with sp.Fori(1, U // SLOTS) as i:
                    for p in range(SLOTS):
                        load_unit(SLOTS * i + p, p, False)
                for u in range(U // SLOTS * SLOTS, U):
                    load_unit(u, u % SLOTS, False)

            @block.tensor
            def _(pe):
                def score(u, p, x, uses):
                    j, t = divmod(x, TT)
                    if x == 0:
                        pe.wait_ge(unit_in[p], NDMA * uses + NDMA)
                    need(pe, s_reduced, NU * u + x - 1)
                    pe.matmul(ps_s[:, x % 2, :], q4[0:BR, p, j, t * P:(t + 1) * P], k4[0:BR, p, j, :],
                              start=True, stop=True).then_inc(s_done, 1)

                def turn(u):
                    pe.wait_ge(turn_ready, u + 1)
                    need(pe, shift_ready, HPG * u)
                    need(pe, recip_done, u - 1)
                    for t in range(TT):
                        last = pe.transpose(ps_turn[:, t * P:(t + 1) * P], turn_in[:, t * P:(t + 1) * P], c.ident_bf[:])
                    last.then_inc(turned, 1)

                def weigh(u, kc):
                    pe.wait_ge(exp_done, NU * u + HPG * (kc + 1))
                    if kc == 0:
                        pe.wait_ge(v_in, u + 1)
                        need(pe, evacuated, 2 * u)
                    for j in range(HPG):
                        last = pe.matmul(ps_o[HD * j:HD * (j + 1), :], vu[:, kc, HD * j:HD * (j + 1)],
                                         probs[:, kc, j, :], start=(kc == 0), stop=(kc == TT - 1))
                    last.then_inc(pv_done, 1)

                def sums(u, h):
                    pe.wait_ge(added, 2 * u + h + 1)
                    if h == 0:
                        need(pe, evacuated, 2 * u)
                    for j in range(HPG):
                        last = pe.matmul(ps_sum[HD * j:HD * (j + 1), :], ones[:], pair_sum[:, h, j, :],
                                         start=(h == 0), stop=(h == 1))
                    last.then_inc(sums_done, 1)

                def back(u):
                    pe.wait_ge(evacuated, 2 * u + 2)
                    pe.wait_ge(normed, u + 1)
                    for t in range(TT):
                        pe.matmul(ps_rows[:, t, :], sumT[:, t * P:(t + 1) * P], first_rows[:], start=True, stop=True)
                        last = pe.transpose(ps_back[:, t * P:(t + 1) * P], outT[:, t * P:(t + 1) * P], c.ident[:])
                    last.then_inc(backed, 1)

                def unit(u, p, uses):
                    first, last = isinstance(u, int) and u == 0, is_last(u)
                    for s in range(NU):
                        kc, j = divmod(s, HPG)
                        if kc == 0:
                            pe.wait_ge(shift_ready, HPG * u + j + 1)
                        need(pe, exp_done, NU * u + s - 1)
                        pe.matmul(ps_st[:, s % 2, :], k4[:, p, j, kc * P:(kc + 1) * P], q4[:, p, j, :],
                                  start=True, stop=True).then_inc(st_done, 1)
                        if s < NU - EARLY and not last:
                            score(u + 1, (p + 1) % SLOTS, s + EARLY, uses + (p + 1) // SLOTS)
                        if s >= NU - EARLY and not (isinstance(u, int) and u > U - 3):
                            score(u + 2, (p + 2) % SLOTS, s - (NU - EARLY), uses + (p + 2) // SLOTS)
                        if not first:
                            if s == 1:
                                weigh(u - 1, 3)
                            if s == 7:
                                sums(u - 1, 1)
                            if s == 10:
                                back(u - 1)
                        if s in (11, 12, 13):
                            weigh(u, s - 11)
                        if s == 14 and not last:
                            turn(u + 1)
                        if s == 15:
                            sums(u, 0)
                    if last:
                        weigh(u, 3)
                        sums(u, 1)
                        back(u)

                pe.wait_ge(window_in, SLOTS * HPG)
                pe.wait_ge(cleared, 2)
                for x in range(NU):
                    score(0, 0, x, 0)
                turn(0)
                for x in range(EARLY):
                    score(1, 1, x, 0)
                units(pe, unit)

            @block.scalar
            def _(act):
                def take_shift(u, p, j):
                    if j == 0:
                        act.wait_ge(turned, u + 1)
                        need(act, st_done, NU * (u - SLOTS + 1))
                    act.activation(q4[BR:P, p, j, :], ps_turn[HD * j:HD * (j + 1), :], ACT.Copy).then_inc(shift_ready, 1)

                def evacuate(u):
                    act.wait_ge(pv_done, TT * u + TT)
                    act.wait_ge(sums_done, 2 * u + 2)
                    act.wait_ge(backed, u + 1)
                    act.activation(outT[:], ps_o[:], ACT.Copy).then_inc(evacuated, 1)
                    act.activation(sumT[:], ps_sum[:], ACT.Copy).then_inc(evacuated, 1)

                def unit(u, p, uses):
                    first, last = isinstance(u, int) and u == 0, is_last(u)
                    for s in range(NU):
                        kc, j = divmod(s, HPG)
                        act.wait_ge(st_done, NU * u + s + 1)
                        if j == 0:
                            need(act, pv_done, TT * (u - 1) + kc + 1)
                            if kc % 2 == 0:
                                need(act, added, 2 * (u - 1) + kc // 2 + 1)
                        act.activation(probs[:, kc, j, :], ps_st[:, s % 2, :], ACT.Exp, scale=SCALE).then_inc(exp_done, 1)
                        if s == 8 and not first:
                            evacuate(u - 1)
                        if s >= 14 and not last:
                            for j in range(2):
                                take_shift(u + 1, (p + 1) % SLOTS, 2 * (s - 14) + j)
                    if last:
                        evacuate(u)

                for j in range(HPG):
                    take_shift(0, 0, j)
                units(act, unit)

            @block.vector
            def _(dve):
                by_tile = maxima[:, 0:TT * HPG * GW].rearrange("p (t j g) -> p t j g", j=HPG, g=GW)
                windows = maxima[:].rearrange("p (t x) -> p t x", t=TT)[:, :, 0:HPG * GW].rearrange(
                    "p t (j g) -> p t j g", g=GW)[:, :, :, 0:4]
                rows = turn_in[:, 0:TT * P].rearrange("p (t j r) -> p t j r", j=HPG, r=HD)
                bar_rows = turn_in[:, 2:2 + TT * (P + 1)].rearrange("p (t x) -> p t x", t=TT)[:, :, 0:P:HD]

                def reduce(u, x):
                    j, t = divmod(x, TT)
                    dve.wait_ge(s_done, NU * u + x + 1)
                    dve.tensor_reduce(by_tile[:, t, j, 1:9], ps_s[:, x % 2, :].rearrange("p (g n) -> p g n", n=S // 8),
                                      axis=AX.X, op=ALU.max).then_inc(s_reduced, 1)

                def row_maxima(u):
                    k = [0]

                    def step(ins):
                        k[0] += 1
                        ins.then_inc(row_step, 1)
                        dve.wait_ge(row_step, 6 * u + k[0])

                    bar = c.bar[:, :, bass.ds(HPG * u, HPG)]
                    dve.wait_ge(s_reduced, NU * u + NU)
                    dve.tensor_reduce(m_win[:].rearrange("p t j -> p t j"), windows, axis=AX.X, op=ALU.max)
                    step(dve.tensor_reduce(m_all[:], by_tile, axis=AX.X, op=ALU.max))
                    step(dve.tensor_tensor(m_bar[:], m_all[:], bar, ALU.add))
                    step(dve.tensor_tensor(m_row[:], m_bar[:], m_win[:], ALU.max))
                    need(dve, turned, u)
                    step(dve.tensor_scalar(rows[:, :, :, 0], m_row[:], -1.0, None, ALU.mult))
                    dve.scalar_tensor_tensor(rows[:, :, :, 1], m_row[:], -1.0, rows[:, :, :, 0],
                                             ALU.mult, ALU.subtract).then_inc(row_step, 1)
                    k[0] += 1
                    step(dve.tensor_copy(bar_rows, bar))
                    dve.sem_inc(turn_ready, 1)

                def normalise(u):
                    dve.wait_ge(backed, u + 2)
                    dve.reciprocal(rsum[:], ps_rows).then_inc(recip_done, 1)
                    dve.wait_ge(recip_done, u + 1)
                    dve.tensor_tensor(slot(c.attn, u).rearrange("p (t w) -> p t w", w=HD), ps_back[:].rearrange("p (t w) -> p t w", w=HD),
                                      rsum[:].rearrange("p t (j a) -> p (t j) a", a=1).to_broadcast([P, TT * HPG, HD]),
                                      ALU.mult).then_inc(normed, 1)

                def unit(u, p, uses):
                    first, last = isinstance(u, int) and u == 0, is_last(u)
                    if not last:
                        for x in range(EARLY, NU):
                            reduce(u + 1, x)
                        row_maxima(u + 1)
                    if not first:
                        normalise(u - 1)
                    if not (isinstance(u, int) and u > U - 3):
                        for x in range(EARLY):
                            reduce(u + 2, x)
                    if last:
                        normalise(u)

                for p in range(SLOTS):
                    for j in range(HPG):
                        dve.tensor_copy(k4[BR:P, p, j, :], c.window[BR:P, :]).then_inc(window_in, 1)
                dve.wait_ge(cleared, 1)
                for x in range(NU):
                    reduce(0, x)
                row_maxima(0)
                for x in range(EARLY):
                    reduce(1, x)
                units(dve, unit)


EPS = 1e-5
C = 128
XSCALE = float(C) ** -0.5
E, FH = 8, 352
FC = 3
FCR = FH - 2 * P
WCOLS = 2 * DC * FH + FC * D
T = B * S
NT = T // P
MASKED = -1.0e30


def gate_cols(w, up, dc):
    return w[:, (up * DC + dc) * FH:(up * DC + dc + 1) * FH]


def down_cols(w, fc):
    return w[:, 2 * DC * FH + fc * D:2 * DC * FH + (fc + 1) * D]


def cross_and_shared(nc, c, x, mask, pad_mask, gate_w, sw_gate, sw_up, sw_down, x2_dram, table_dram):
    with ExitStack() as ctx:
        m = Memory(nc, ctx)
        sw_hi = m.sb("sw_hi", [P, 2, WCOLS], F32R)
        sw_lo = m.sb("sw_lo", [P, 2, WCOLS], F32R)
        sw_raw = m.sb("sw_raw", [P, 2, FC * D])
        am = m.sb("am", [P, TT, S])
        pm = m.sb("pm", [P, B, S])
        gw = m.sb("gw", [P, DC, E])
        gw_hi = m.sb("gw_hi", [P, DC, E], F32R)
        gw_lo = m.sb("gw_lo", [P, DC, E], F32R)
        before = m.sb("before", [P, P], BF16)
        ones = m.sb("ones", [P, P], BF16)
        expert = m.sb("expert", [P, E])
        region = m.sb("region", [P, E])
        expert_i = m.sb("expert_i", [P, E], I32)
        token_i = m.sb("token_i", [P, NT], U32)
        token = m.sb("token", [P, 1], U32)
        half = m.sb("half", [P, 1])
        q_tile = m.sb("q_tile", [P, 2, 2, P], F32R)
        x_in = m.sb("x_tile", [P, 2, D])
        r1 = m.sb("r1", [P, 2, D])
        stats = m.sb("stats", [P, 2, 6])
        mv = m.sb("mv", [P, 2, 2])
        rstd = m.sb("rstd", [P, 2, 2])
        x1 = m.sb("x1", [P, 2, D])
        sc = m.sb("sc", [P, 2, D])
        small = m.sb("small", [P, 2, 8])
        x2 = m.sb("x2", [P, 2, D])
        am8 = x2[:, 0, :].bitcast(U8).rearrange("p (t k) -> p t k", t=TT)
        pm8 = x2[:, 1, :].bitcast(U8).rearrange("p (b k) -> p b k", b=B)
        xT_hi = m.sb("x2T_hi", [P, DC, P], F32R)
        xT_lo = m.sb("x2T_lo", [P, DC, P], F32R)
        act_g = m.sb("act_g", [P, 2, FH])
        g = m.sb("g", [P, 2, FC * P])
        gT_hi = m.sb("gT_hi", [P, 2, FC * P], F32R)
        gT_lo = m.sb("gT_lo", [P, 2, FC * P], F32R)
        r_small = m.sb("r_small", [P, 4])
        r_exp = m.sb("r_exp", [P, E])
        score = m.sb("score", [P, E])
        top = m.sb("top", [P, E])
        top_i = m.sb("top_i", [P, E], U32)
        top_f = m.sb("top_f", [P, E])
        chosen = m.sb("chosen", [P, 2, E])
        both = m.sb("both", [P, E], BF16)
        both_sum = c.both_sum
        place = m.sb("place", [P, E])
        placed = m.sb("placed", [P, 2, E])
        slot_f = m.sb("slot_f", [P, 2])
        slot_u = m.sb("slot_u", [P, 2], U32)

        ps_sc = m.ps("ps_sc", [P, S])
        ps_xT = m.ps("ps_xT", [P, D])
        ps_r = m.ps("ps_r", [P, 2, E])
        ps_gu = m.ps("ps_gu", [P, 2, S])
        ps_gT = m.ps("ps_gT", [P, FC * P])
        ps_y = m.ps("ps_y", [P, D])

        names = ("sw_zeroed sw_loaded0 sw_loaded1 sw_hi_done sw_split masks_in gate_in const_step x_ld0 x_ld1 r1_done stats1 mv1 ve1 rstd1 x1_done q_tile_done sc_done "
                 "scaled masked0 masked nmax e_done guard0 guard sum_ok rinv r2_done stats2 mv2 ve2 rstd2 x2_done x2_st0 x2_st1 "
                 "x2_turned hi_done2 lo_done2 r_logits r_max r_e r_step rank_done slots_done scat token_done "
                 "g_done u_done silu_done g_ready gT_turned gT_hi_done gT_lo_done y_done y_out both_done setup").split()
        s = {k: m.sem("p4_" + k) for k in names}

        x_rows = x.rearrange("b (t p) d -> p (b t) d", p=P)
        x2_rows = x2_dram.rearrange("(n p) d -> p n d", p=P)

        def attn_tile(b, t):
            return c.attn[:, bass.ds(b * HG, HG), t * P:(t + 1) * P]

        def tiles(eng, one):
            for t in range(TT):
                one(t, 0, t)
            with eng.Fori(1, B - 1) as b:
                for t in range(TT):
                    one(b * TT + t, b, t)
            for t in range(TT):
                one((B - 1) * TT + t, B - 1, t)

        def piece(w, i):
            k, kind = divmod(i, 3)
            cols = slice(kind * DC * FH, (kind + 1) * DC * FH if kind < 2 else WCOLS)
            return w[:, k, cols], sw_raw[:, i % 2, 0:cols.stop - cols.start]

        def ahead(n, b, t, k):
            if isinstance(n, int) and n + k >= NT:
                return None
            return (n + k, b, t + k) if t + k < TT else (n + k, b + 1, t + k - TT)

        with nc.Block() as block:
            @block.sync
            def _(sp):
                sp.dma_start(am8, mask.rearrange("(t p) k -> p t k", p=P)).then_inc(s["masks_in"], 16)
                sp.dma_start(pm8.rearrange("p b k -> p (b k)"),
                             pad_mask.rearrange("(a b) k -> a (b k)", a=1).to_broadcast([P, B * S])).then_inc(s["masks_in"], 16)
                sp.dma_start(gw[:], gate_w.rearrange("(c p) e -> p c e", p=P)).then_inc(s["gate_in"], 16)

                def load_x(n, t, first):
                    if not first:
                        sp.wait_ge(s["r1_done"], n - 1)
                    sp.dma_start(x_in[:, t % 2, :], x_rows[:, bass.ds(n, 1), :].rearrange("p a d -> p (a d)")).then_inc(s[f"x_ld{t % 2}"], 16)

                load_x(0, 0, True)
                load_x(1, 1, True)
                for i in range(6):
                    k, kind = divmod(i, 3)
                    if i >= 2:
                        sp.wait_ge(s["sw_split"], i - 1)
                    for h in range(2):
                        if kind < 2:
                            src = (sw_gate, sw_up)[kind].rearrange("(c p) h -> p c h", p=P)[:, 2 * h:2 * h + 2, FH * k:FH * (k + 1)]
                            dst = sw_raw[:, i % 2, 2 * h * FH:2 * (h + 1) * FH].rearrange("p (c h) -> p c h", h=FH)
                        elif h == 0:
                            src = sw_down[FH * k:FH * k + 2 * P, :].rearrange("(c p) d -> p c d", p=P)
                            dst = sw_raw[:, i % 2, 0:2 * D].rearrange("p (c d) -> p c d", d=D)
                        else:
                            src, dst = sw_down[FH * k + 2 * P:FH * (k + 1), :], sw_raw[0:FCR, i % 2, 2 * D:3 * D]
                        sp.dma_start(dst, src).then_inc(s[f"sw_loaded{i % 2}"], 16)

                def one(n, b, t):
                    sp.wait_ge(s["x2_done"], n + 1)
                    sp.dma_start(x2_rows[:, bass.ds(n, 1), :].rearrange("p a d -> p (a d)"), x2[:, t % 2, :]).then_inc(s[f"x2_st{t % 2}"], 16)
                    if not (isinstance(n, int) and n + 2 >= NT):
                        load_x(n + 2, t, False)

                tiles(sp, one)
                for k in range(2):
                    sp.wait_ge(s[f"x2_st{k}"], 8 * NT)

            @block.gpsimd
            def _(pool):
                step = s["const_step"]
                pool.memset(before[:], 1.0)
                pool.memset(ones[:], 1.0)
                pool.memset(half[:], -0.5)
                pool.memset(both_sum[:], 0.0)
                pool.memset(g[:], 0.0)
                pool.iota(token_i[:], pattern=[[P, NT]], base=0, channel_multiplier=1)
                pool.iota(expert_i[:], pattern=[[1, E]], base=0, channel_multiplier=0).then_inc(step, 1)
                pool.wait_ge(step, 1)
                pool.affine_select(out=before[:], in_=before[:], compare_op=ALU.is_gt, fill=0.0, base=0,
                                   pattern=[[1, P]], channel_multiplier=-1)
                pool.tensor_copy(expert[:], expert_i[:]).then_inc(step, 1)
                pool.wait_ge(step, 2)
                pool.tensor_scalar(region[:], expert[:], float(T), None, ALU.mult).then_inc(step, 1)

                def add_attn(n, b, t):
                    p = t % 2
                    pool.wait_ge(s[f"x_ld{p}"], 32 * b + 16 * (t // 2) + 16)
                    need(pool, s["x2_done"], n - 1)
                    pool.tensor_tensor(r1[:, p, :].rearrange("p (g d) -> p g d", g=HG),
                                       x_in[:, p, :].rearrange("p (g d) -> p g d", g=HG), attn_tile(b, t), ALU.add).then_inc(s["r1_done"], 1)

                def take_query(n, b, t):
                    need(pool, s["sc_done"], n - 1)
                    for k in range(2):
                        src = c.qk_ctx[0][k][:, bass.ds(n * P, P)].bitcast(F32)
                        last = pool.tensor_copy(q_tile[:, t % 2, k, :], src)
                    last.then_inc(s["q_tile_done"], 1)

                def root1(n, b, t):
                    root(n, 0, s["mv1"], s["ve1"], s["rstd1"])

                def root2(n, b, t):
                    root(n, 1, s["mv2"], s["ve2"], s["rstd2"])

                def masks(n, b, t):
                    p = t % 2
                    pool.wait_ge(s["scaled"], n + 1)
                    pool.tensor_tensor(sc[:, p, :], sc[:, p, :], am[:, t, :], ALU.add).then_inc(s["masked0"], 1)
                    wait_apart(pool, s["masked0"], n + 1, c.pool_passed)
                    pool.tensor_tensor(sc[:, p, :], sc[:, p, :], pm[:, bass.ds(b, 1), :].rearrange("p a k -> p (a k)"), ALU.add).then_inc(s["masked"], 1)

                def guard(n, b, t):
                    p = t % 2
                    wait_apart(pool, s["nmax"], n + 1, c.pool_passed)
                    pool.tensor_scalar(small[:, p, 2:3], small[:, p, 0:1], -0.1 * MASKED, 0.0, ALU.subtract, ALU.max).then_inc(s["guard0"], 1)
                    wait_apart(pool, s["guard0"], n + 1, c.pool_passed)
                    pool.tensor_scalar(small[:, p, 3:4], small[:, p, 2:3], 1.0e38, 0.0, ALU.mult, ALU.mult).then_inc(s["guard"], 1)

                def root(n, k, ready, mid, done):
                    wait_apart(pool, ready, n + 1, c.pool_passed)
                    pool.tensor_scalar(rstd[:, k, 0:1], mv[:, k, 1:2], EPS, None, ALU.add).then_inc(mid, 1)
                    pool.wait_ge(mid, n + 1)
                    pool.tensor_tensor(rstd[:, k, 1:2], rstd[:, k, 0:1], half[:], ALU.pow).then_inc(done, 1)

                def send(n):
                    need(pool, s["scat"], 32 * n)
                    pool.tensor_copy(token[:], token_i[:, bass.ds(n, 1)]).then_inc(s["token_done"], 1)
                    pool.wait_ge(s["token_done"], n + 1)
                    wait_apart(pool, s["slots_done"], n + 1, c.pool_passed)
                    for k in range(2):
                        pool.indirect_dma_start(out=table_dram[:], out_offset=bass.IndirectOffsetOnAxis(ap=slot_u[:, k:k + 1], axis=0),
                                                in_=token[:], in_offset=None).then_inc(s["scat"], 16)

                pool.wait_ge(s["setup"], 1)
                for step in (add_attn, take_query, root1, masks, guard, root2):
                    step(0, 0, 0)
                for step in (add_attn, take_query, root1, masks):
                    step(1, 0, 1)

                def one(n, b, t):
                    next1, next2 = ahead(n, b, t, 1), ahead(n, b, t, 2)
                    if next1:
                        guard(*next1)
                    if next2:
                        add_attn(*next2)
                    if next1:
                        root2(*next1)
                    if next2:
                        take_query(*next2)
                        root1(*next2)
                    if not (isinstance(n, int) and n == 0):
                        send(n - 1)
                    if next2:
                        masks(*next2)

                tiles(pool, one)
                send(NT - 1)
                pool.wait_ge(s["scat"], 32 * NT)

            @block.scalar
            def _(act):
                act.wait_ge(s["gate_in"], 16)
                act.activation(gw_hi[:], gw[:], ACT.Copy).then_inc(s["gate_in"], 1)

                def split(k):
                    for i in range(3 * k, 3 * k + 3):
                        act.wait_ge(s[f"sw_loaded{i % 2}"], 32 * (i // 2) + 32)
                        if i % 3 == 2:
                            act.wait_ge(s["sw_zeroed"], k + 1)
                        high, raw = piece(sw_hi, i)
                        act.activation(high, raw, ACT.Copy).then_inc(s["sw_hi_done"], 1)

                def soft(n, b, t):
                    p = t % 2
                    act.wait_ge(s["nmax"], n + 1)
                    act.activation(sc[:, p, :], sc[:, p, :], ACT.Exp, bias=small[:, p, 0:1], accum_out=small[:, p, 1:2]).then_inc(s["e_done"], 1)

                def x_high(n, b, t):
                    act.wait_ge(s["x2_turned"], n + 1)
                    need(act, s["u_done"], 2 * n)
                    act.activation(xT_hi[:].rearrange("p c k -> p (c k)"), ps_xT[:], ACT.Copy).then_inc(s["hi_done2"], 1)

                def silu(n, k):
                    act.wait_ge(s["g_done"], 2 * n + k + 1)
                    need(act, s["g_ready"], 2 * n + k - 1)
                    act.activation(act_g[:, k, :], ps_gu[:, 0, 0:FH], ACT.Silu).then_inc(s["silu_done"], 1)

                def g_high(n, k):
                    act.wait_ge(s["gT_turned"], 2 * n + k + 1)
                    act.activation(gT_hi[:, k, :], ps_gT[:], ACT.Copy).then_inc(s["gT_hi_done"], 1)

                def one(n, b, t):
                    silu(n, 0)
                    silu(n, 1)
                    g_high(n, 0)
                    act.wait_ge(s["r_max"], n + 1)
                    act.activation(r_exp[:], ps_r[:, 0, :], ACT.Exp, bias=r_small[:, 0:1], accum_out=r_small[:, 1:2]).then_inc(s["r_e"], 1)
                    next1, next2 = ahead(n, b, t, 1), ahead(n, b, t, 2)
                    if next1:
                        x_high(*next1)
                    g_high(n, 1)
                    if next2:
                        soft(*next2)

                split(0)
                soft(0, 0, 0)
                split(1)
                x_high(0, 0, 0)
                soft(1, 0, 1)
                tiles(act, one)

            @block.vector
            def _(dve):
                dve.wait_ge(s["masks_in"], 32)
                dve.tensor_scalar(am[:], am8, MASKED, None, ALU.mult)
                dve.tensor_scalar(pm[:], pm8, MASKED, None, ALU.mult)
                dve.wait_ge(s["gate_in"], 17)
                dve.tensor_tensor(gw_lo[:], gw[:], gw_hi[:].bitcast(F32), ALU.subtract).then_inc(s["setup"], 1)
                dve.wait_ge(s["const_step"], 3)

                def split(k):
                    for i in range(3 * k, 3 * k + 3):
                        dve.wait_ge(s["sw_hi_done"], i + 1)
                        high, raw = piece(sw_hi, i)
                        dve.tensor_tensor(piece(sw_lo, i)[0], raw, high.bitcast(F32), ALU.subtract).then_inc(s["sw_split"], 1)
                        if i % 3 == 0:
                            dve.wait_ge(s["sw_split"], i + 1)
                            dve.memset(sw_raw[FCR:P, k, 2 * D:3 * D], 0.0).then_inc(s["sw_zeroed"], 1)

                def moments(n, src, k, ready, mid):
                    dve.bn_stats(stats[:, k, :], src).then_inc(ready, 1)
                    wait_apart(dve, ready, n + 1, c.dve_passed)
                    dve.bn_aggr(mv[:, k, :], stats[:, k, :]).then_inc(mid, 1)

                def moments1(n, b, t):
                    dve.wait_ge(s["r1_done"], n + 1)
                    moments(n, r1[:, t % 2, :], 0, s["stats1"], s["mv1"])

                def norm1(n, b, t):
                    p = t % 2
                    dve.wait_ge(s["rstd1"], n + 1)
                    dve.tensor_scalar(x1[:, p, :], r1[:, p, :], mv[:, 0, 0:1], rstd[:, 0, 1:2], ALU.subtract, ALU.mult).then_inc(s["x1_done"], 1)

                def scale(n, b, t):
                    p = t % 2
                    dve.wait_ge(s["sc_done"], n + 1)
                    dve.wait_ge(s["x1_done"], n + 1)
                    dve.scalar_tensor_tensor(sc[:, p, :], ps_sc[:], XSCALE, x1[:, p, :], ALU.mult, ALU.mult).then_inc(s["scaled"], 1)

                def row_max(n, b, t):
                    p = t % 2
                    dve.wait_ge(s["masked"], n + 1)
                    dve.tensor_reduce(small[:, p, 0:1], sc[:, p, :], axis=AX.X, op=ALU.max, negate=True).then_inc(s["nmax"], 1)

                def attended(n, b, t):
                    p = t % 2
                    dve.wait_ge(s["e_done"], n + 1)
                    dve.wait_ge(s["guard"], n + 1)
                    dve.tensor_tensor(small[:, p, 4:5], small[:, p, 1:2], small[:, p, 3:4], ALU.add).then_inc(s["sum_ok"], 1)
                    dve.wait_ge(s["sum_ok"], n + 1)
                    dve.reciprocal(small[:, p, 5:6], small[:, p, 4:5]).then_inc(s["rinv"], 1)
                    dve.wait_ge(s["rinv"], n + 1)
                    dve.scalar_tensor_tensor(r1[:, p, :], sc[:, p, :], small[:, p, 5:6], x1[:, p, :], ALU.mult, ALU.add).then_inc(s["r2_done"], 1)
                    dve.wait_ge(s["r2_done"], n + 1)
                    moments(n, r1[:, p, :], 1, s["stats2"], s["mv2"])

                def norm2(n, b, t):
                    p = t % 2
                    need(dve, s[f"x2_st{p}"], 32 * b + 16 * (t // 2))
                    dve.wait_ge(s["rstd2"], n + 1)
                    dve.tensor_scalar(x2[:, p, :], r1[:, p, :], mv[:, 1, 0:1], rstd[:, 1, 1:2], ALU.subtract, ALU.mult).then_inc(s["x2_done"], 1)

                def x_low(n, b, t):
                    dve.wait_ge(s["hi_done2"], n + 1)
                    dve.tensor_tensor(xT_lo[:].rearrange("p c k -> p (c k)"), ps_xT[:], xT_hi[:].rearrange("p c k -> p (c k)").bitcast(F32),
                                      ALU.subtract).then_inc(s["lo_done2"], 1)

                def multiply(n, k):
                    dve.wait_ge(s["u_done"], 2 * n + k + 1)
                    dve.wait_ge(s["silu_done"], 2 * n + k + 1)
                    dve.tensor_tensor(g[:, k, 0:FH], act_g[:, k, :], ps_gu[:, 1, 0:FH], ALU.mult).then_inc(s["g_ready"], 1)

                def g_low(n, k):
                    dve.wait_ge(s["gT_hi_done"], 2 * n + k + 1)
                    dve.tensor_tensor(gT_lo[:, k, :], ps_gT[:], gT_hi[:, k, :].bitcast(F32), ALU.subtract).then_inc(s["gT_lo_done"], 1)

                RSTEPS = 11

                def choose(n):
                    k = [0]

                    def step(ins):
                        k[0] += 1
                        ins.then_inc(s["r_step"], 1)
                        dve.wait_ge(s["r_step"], RSTEPS * n + k[0])

                    dve.wait_ge(s["r_e"], n + 1)
                    step(dve.reciprocal(r_small[:, 2:3], r_small[:, 1:2]))
                    step(dve.tensor_scalar(score[:], r_exp[:], r_small[:, 2:3], None, ALU.mult))
                    dve.sem_inc(c.dve_passed, 1)
                    step(dve.max(top[:], score[:]))
                    dve.tensor_copy(c.weights[:, bass.ds(n, 1), :].rearrange("p a k -> p (a k)"), top[:, 0:2])
                    step(dve.max_index(top_i[:], top[:], score[:]))
                    step(dve.tensor_copy(top_f[:], top_i[:]))
                    dve.tensor_copy(c.choice[:, bass.ds(n, 1), :].rearrange("p a k -> p (a k)"), top_f[:, 0:2])
                    dve.tensor_scalar(chosen[:, 0, :], expert[:], top_f[:, 0:1], None, ALU.is_equal)
                    step(dve.tensor_scalar(chosen[:, 1, :], expert[:], top_f[:, 1:2], None, ALU.is_equal))
                    dve.tensor_tensor(both[:], chosen[:, 0, :], chosen[:, 1, :], ALU.add).then_inc(s["both_done"], 1)

                def locate(n):
                    k = [6]

                    def step(ins):
                        k[0] += 1
                        ins.then_inc(s["r_step"], 1)
                        dve.wait_ge(s["r_step"], RSTEPS * n + k[0])

                    dve.wait_ge(s["rank_done"], n + 1)
                    step(dve.tensor_tensor(place[:], ps_r[:, 1, :], region[:], ALU.add))
                    step(dve.tensor_tensor(both_sum[:], both_sum[:], both[:], ALU.add))
                    step(dve.tensor_tensor(placed[:], chosen[:], place[:].rearrange("p (a e) -> p a e", a=1).to_broadcast([P, 2, E]), ALU.mult))
                    step(dve.tensor_reduce(slot_f[:], placed[:], axis=AX.X, op=ALU.add))
                    dve.tensor_copy(c.listed[:, bass.ds(n, 1), :].rearrange("p a k -> p (a k)"), slot_f[:])
                    need(dve, s["scat"], 32 * n)
                    step(dve.tensor_copy(slot_u[:], slot_f[:]))
                    dve.sem_inc(s["slots_done"], 1)

                def one(n, b, t):
                    next1, next2 = ahead(n, b, t, 1), ahead(n, b, t, 2)
                    if next1:
                        attended(*next1)
                    multiply(n, 0)
                    if next1:
                        norm2(*next1)
                    if next2:
                        moments1(*next2)
                    if not (isinstance(n, int) and n == 0):
                        locate(n - 1)
                    g_low(n, 0)
                    dve.wait_ge(s["r_logits"], n + 1)
                    dve.tensor_reduce(r_small[:, 0:1], ps_r[:, 0, :], axis=AX.X, op=ALU.max, negate=True).then_inc(s["r_max"], 1)
                    if next2:
                        norm1(*next2)
                    multiply(n, 1)
                    if next2:
                        scale(*next2)
                    if next1:
                        x_low(*next1)
                    g_low(n, 1)
                    choose(n)
                    if next2:
                        row_max(*next2)
                    dve.wait_ge(s["y_done"], n + 1)
                    dve.tensor_tensor(attn_tile(b, t), ps_y[:].rearrange("p (g d) -> p g d", g=HG),
                                      x2[:, t % 2, :].rearrange("p (g d) -> p g d", g=HG), ALU.add).then_inc(s["y_out"], 1)

                for step in (moments1, norm1, scale, row_max):
                    step(0, 0, 0)
                split(0)
                attended(0, 0, 0)
                norm2(0, 0, 0)
                for step in (moments1, norm1, scale):
                    step(1, 0, 1)
                split(1)
                x_low(0, 0, 0)
                row_max(1, 0, 1)
                tiles(dve, one)
                locate(NT - 1)

            @block.tensor
            def _(pe):
                def scores(n, b, t):
                    p = t % 2
                    pe.wait_ge(s["q_tile_done"], n + 1)
                    need(pe, s["scaled"], n)
                    for k, (a, z) in enumerate(((0, 0), (0, 1), (1, 0))):
                        last = pe.matmul(ps_sc[:], q_tile[:, p, a, :], c.qk_ctx[1][z][:, bass.ds(b * S, S)],
                                         start=(k == 0), stop=(k == 2))
                    last.then_inc(s["sc_done"], 1)

                def passes(out, stationary, moving, chunks):
                    for q in range(chunks):
                        for k, (a, z) in enumerate(((0, 0), (0, 1), (1, 0))):
                            last = pe.matmul(out, stationary[a](q), moving[z](q), start=(q == 0 and k == 0),
                                             stop=(q == chunks - 1 and k == 2))
                    return last

                xT = [lambda q, w=w: w[:, q, :] for w in (xT_hi, xT_lo)]

                def gate(n, k):
                    need(pe, s["silu_done"], 2 * n + k)
                    passes(ps_gu[:, 0, 0:FH], xT, [lambda q, w=w: gate_cols(w[:, k, :], 0, q) for w in (sw_hi, sw_lo)], DC).then_inc(s["g_done"], 1)

                def up(n, k):
                    need(pe, s["g_ready"], 2 * n + k)
                    passes(ps_gu[:, 1, 0:FH], xT, [lambda q, w=w: gate_cols(w[:, k, :], 1, q) for w in (sw_hi, sw_lo)], DC).then_inc(s["u_done"], 1)

                def turn(n, k):
                    pe.wait_ge(s["g_ready"], 2 * n + k + 1)
                    need(pe, s["gT_lo_done"], 2 * n + k)
                    for q in range(FC):
                        last = pe.transpose(ps_gT[:, q * P:(q + 1) * P], g[:, k, q * P:(q + 1) * P], c.ident[:])
                    last.then_inc(s["gT_turned"], 1)

                def down(n, k):
                    pe.wait_ge(s["gT_lo_done"], 2 * n + k + 1)
                    if k == 0:
                        need(pe, s["y_out"], n)
                    gT = [lambda q, w=w: w[:, k, q * P:(q + 1) * P] for w in (gT_hi, gT_lo)]
                    ws = [lambda q, w=w: down_cols(w[:, k, :], q) for w in (sw_hi, sw_lo)]
                    for q in range(FC):
                        for j, (a, z) in enumerate(((0, 0), (0, 1), (1, 0))):
                            last = pe.matmul(ps_y[:], gT[a](q), ws[z](q), start=(k == 0 and q == 0 and j == 0),
                                             stop=(k == 1 and q == FC - 1 and j == 2))
                    if k == 1:
                        last.then_inc(s["y_done"], 1)

                def router(n):
                    need(pe, s["slots_done"], n)
                    passes(ps_r[:, 0, :], xT, [lambda q, w=w: w[:, q, :] for w in (gw_hi, gw_lo)], DC).then_inc(s["r_logits"], 1)

                def ranks(n):
                    pe.wait_ge(s["both_done"], n + 1)
                    pe.matmul(ps_r[:, 1, :], before[:], both[:], start=True, stop=False)
                    pe.matmul(ps_r[:, 1, :], ones[:], both_sum[:], start=False, stop=True).then_inc(s["rank_done"], 1)

                def x_turn(n, b, t):
                    pe.wait_ge(s["x2_done"], n + 1)
                    need(pe, s["lo_done2"], n)
                    for q in range(DC):
                        z = pe.transpose(ps_xT[:, q * P:(q + 1) * P], x2[:, t % 2, q * P:(q + 1) * P], c.ident[:])
                    z.then_inc(s["x2_turned"], 1)

                def one(n, b, t):
                    next1, next2 = ahead(n, b, t, 1), ahead(n, b, t, 2)
                    pe.wait_ge(s["lo_done2"], n + 1)
                    gate(n, 0)
                    up(n, 0)
                    if not (isinstance(n, int) and n == 0):
                        ranks(n - 1)
                    gate(n, 1)
                    turn(n, 0)
                    router(n)
                    up(n, 1)
                    if next1:
                        x_turn(*next1)
                    if next2:
                        scores(*next2)
                    down(n, 0)
                    turn(n, 1)
                    down(n, 1)

                pe.wait_ge(s["setup"], 1)
                pe.wait_ge(s["const_step"], 3)
                scores(0, 0, 0)
                scores(1, 0, 1)
                x_turn(0, 0, 0)
                pe.wait_ge(s["sw_split"], 6)
                tiles(pe, one)
                ranks(NT - 1)


NJ = 2 * T // P + E - 1
ROWS = E * T + NJ * P


def plan(nc, c):
    with ExitStack() as ctx:
        m = Memory(nc, ctx)
        ones = m.sb("plan_ones", [P, P], BF16)
        count = m.sb("count", [P, E])
        at_i = m.sb("at_i", [P, NT], I32)
        at = m.sb("at", [P, NT])
        more = m.sb("more", [P, E, NT])
        length = m.sb("length", [P, E])
        end = m.sb("end", [P, E])
        tile_i = m.sb("tile_i", [P, NJ], I32)
        tile = m.sb("tile", [P, NJ])
        past = m.sb("past", [P, NJ, E])
        gone = m.sb("gone", [P, NJ, E])
        e_of = m.sb("e_of", [P, NJ])
        start = m.sb("start", [P, NJ])
        row = m.sb("row", [P, NJ])
        shift = m.sb("shift_e", [P, E])
        is_e = m.sb("is_e", [P, NT * 2, E])
        moved = m.sb("moved", [P, NT * 2])
        ps_count = m.ps("ps_count", [P, E])
        built, counted, step = m.sem("plan_built"), m.sem("counted"), m.sem("plan_step")
        with nc.Block() as block:
            @block.gpsimd
            def _(pool):
                pool.memset(ones[:], 1.0)
                pool.iota(at_i[:], pattern=[[P, NT]], base=0, channel_multiplier=0)
                pool.iota(tile_i[:], pattern=[[1, NJ]], base=0, channel_multiplier=0).then_inc(built, 1)

            @block.tensor
            def _(pe):
                pe.wait_ge(built, 1)
                pe.matmul(ps_count[:], ones[:], c.both_sum[:], start=True, stop=True).then_inc(counted, 1)

            @block.vector
            def _(dve):
                k = [0]

                def link(ins):
                    k[0] += 1
                    ins.then_inc(step, 1)
                    dve.wait_ge(step, k[0])

                dve.wait_ge(built, 1)
                dve.tensor_copy(at[:], at_i[:])
                link(dve.tensor_copy(tile[:], tile_i[:]))
                dve.wait_ge(counted, 1)
                link(dve.tensor_copy(count[:], ps_count[:]))
                link(dve.tensor_tensor(more[:], count[:].rearrange("p (e a) -> p e a", a=1).to_broadcast([P, E, NT]),
                                       at[:].rearrange("p (a n) -> p a n", a=1).to_broadcast([P, E, NT]), ALU.is_gt))
                link(dve.tensor_reduce(length[:], more[:], axis=AX.X, op=ALU.add))
                link(dve.tensor_copy(end[:], length[:]))
                for e in range(1, E):
                    link(dve.tensor_tensor(end[:, e:e + 1], end[:, e:e + 1], end[:, e - 1:e], ALU.add))
                link(dve.tensor_tensor(past[:], tile[:].rearrange("p (j a) -> p j a", a=1).to_broadcast([P, NJ, E]),
                                       end[:].rearrange("p (a e) -> p a e", a=1).to_broadcast([P, NJ, E]), ALU.is_ge))
                dve.tensor_tensor(gone[:], past[:], length[:].rearrange("p (a e) -> p a e", a=1).to_broadcast([P, NJ, E]), ALU.mult)
                link(dve.tensor_reduce(e_of[:], past[:], axis=AX.X, op=ALU.add))
                link(dve.tensor_reduce(start[:], gone[:], axis=AX.X, op=ALU.add))
                link(dve.tensor_tensor(row[:], tile[:], start[:], ALU.subtract))
                link(dve.tensor_scalar(row[:], row[:], float(P), None, ALU.mult))
                link(dve.scalar_tensor_tensor(row[:], e_of[:], float(T), row[:], ALU.mult, ALU.add))
                dve.tensor_copy(c.first_row[:], row[0:1, :])
                link(dve.tensor_tensor(shift[:], end[:], length[:], ALU.subtract))
                link(dve.tensor_scalar(shift[:], shift[:], float(P), None, ALU.mult))
                link(dve.scalar_tensor_tensor(shift[:], tile[:, 0:E], -float(T), shift[:], ALU.mult, ALU.add))
                link(dve.tensor_tensor(is_e[:], c.choice[:].rearrange("p n (k a) -> p (n k) a", a=1).to_broadcast([P, NT * 2, E]),
                                       tile[:, 0:E].rearrange("p (a e) -> p a e", a=1).to_broadcast([P, NT * 2, E]), ALU.is_equal))
                link(dve.tensor_tensor(is_e[:], is_e[:], shift[:].rearrange("p (a e) -> p a e", a=1).to_broadcast([P, NT * 2, E]), ALU.mult))
                link(dve.tensor_reduce(moved[:], is_e[:], axis=AX.X, op=ALU.add))
                dve.tensor_tensor(c.slots[:].rearrange("p n k -> p (n k)"), c.listed[:].rearrange("p n k -> p (n k)"), moved[:], ALU.add)
                dve.tensor_scalar(c.expert_of[:], e_of[0:1, :], float(E - 1), None, ALU.min)


def experts(nc, c, w_gate, w_up, w_down, x2_dram, table_dram, y_dram):
    with ExitStack() as ctx:
        m = Memory(nc, ctx)
        w = m.sb("w_all", [P, E * WCOLS])
        who = m.sb("who", [P, 2, 1], U32)
        xg = m.sb("xg", [P, 2, D])
        xT = m.sb("xgT", [P, 2, D])
        act_g = m.sb("e_act", [P, 2, FH])
        g = m.sb("e_g", [P, 2, FC * P])
        gT = m.sb("e_gT", [P, 2, FC * P])
        y = m.sb("e_y", [P, 2, D])
        ps_xT = m.ps("e_ps_xT", [P, D])
        ps_g = m.ps("e_ps_g", [P, S])
        ps_u = m.ps("e_ps_u", [P, S])
        ps_gT = m.ps("e_ps_gT", [P, FC * P])
        ps_y = m.ps("e_ps_y", [P, D])
        names = "w_in who0 who1 x_in0 x_in1 turned xT_done g_done silu_done u_done g_ready gT_turned gT_done y_done y_out y_st0 y_st1 padded".split()
        s = {k: m.sem("e_" + k) for k in names}
        top = E * T + (NJ - 1) * P

        def pairs(eng, one, first, last):
            assert first % 2 == 1 and (last - first) % 2 == 1
            one(first, 1)
            one(first + 1, 0)
            with eng.Fori(1, (last - first + 1) // 2) as i:
                one(2 * i + first, 1)
                one(2 * i + first + 1, 0)

        with nc.Block() as block:
            @block.sync
            def _(sp):
                def list_in(j, p):
                    need(sp, s[f"x_in{p}"], 16 * ((j - p) // 2) if isinstance(j, int) else 8 * (j - p))
                    row = sp.value_load(c.first_row[0:1, bass.ds(j, 1)], min_val=0, max_val=top)
                    sp.dma_start(who[:, p, :], table_dram[bass.ds(row, P), :], allow_slow_non_contiguous=True).then_inc(s[f"who{p}"], 16)

                def weights_in(e):
                    base = e * WCOLS
                    src = [w_gate[e].rearrange("(c p) h -> p c h", p=P), w_up[e].rearrange("(c p) h -> p c h", p=P)]
                    for up in range(2):
                        sp.dma_start(w[:, base + up * DC * FH:base + (up + 1) * DC * FH].rearrange("p (c h) -> p c h", h=FH),
                                     src[up]).then_inc(s["w_in"], 16)
                    down = w[:, base + 2 * DC * FH:base + WCOLS].rearrange("p (c d) -> p c d", d=D)
                    sp.dma_start(down[:, 0:2, :], w_down[e, 0:2 * P, :].rearrange("(c p) d -> p c d", p=P)).then_inc(s["w_in"], 16)
                    sp.dma_start(down[0:FCR, 2, :], w_down[e, 2 * P:FH, :]).then_inc(s["w_in"], 16)

                list_in(0, 0)
                list_in(1, 1)
                for e in range(E):
                    if e:
                        sp.wait_ge(s["w_in"], 64 * e)
                    weights_in(e)
                    list_in(e + 2, e % 2)
                first = E + 2
                with sp.Fori(0, (NJ - first) // 2) as i:
                    list_in(2 * i + first, 0)
                    list_in(2 * i + first + 1, 1)
                if (NJ - first) % 2:
                    list_in(NJ - 1, 0)

            @block.gpsimd
            def _(pool):
                def gather(j, p):
                    pool.wait_ge(s[f"who{p}"], 16 * ((j - p) // 2) + 16 if isinstance(j, int) else 8 * (j - p) + 16)
                    need(pool, s["turned"], j - 1)
                    pool.sem_inc(c.pool_passed, 1)
                    pool.indirect_dma_start(out=xg[:, p, :], out_offset=None, in_=x2_dram[:],
                                            in_offset=bass.IndirectOffsetOnAxis(ap=who[:, p, :], axis=0)).then_inc(s[f"x_in{p}"], 16)

                pool.memset(g[:], 0.0).then_inc(s["padded"], 1)
                gather(0, 0)
                pairs(pool, gather, 1, NJ - 1)

            @block.scalar
            def _(act):
                def x_out(j, p):
                    act.wait_ge(s["turned"], j + 1)
                    act.activation(xT[:, p, :], ps_xT[:], ACT.Copy).then_inc(s["xT_done"], 1)

                def silu(j, p):
                    act.wait_ge(s["g_done"], j + 1)
                    act.activation(act_g[:, p, :], ps_g[:, 0:FH], ACT.Silu).then_inc(s["silu_done"], 1)

                def y_store(j, p):
                    act.wait_ge(s["y_done"], j + 1)
                    need(act, s[f"y_st{p}"], 16 * ((j - p) // 2) if isinstance(j, int) else 8 * (j - p))
                    act.activation(y[:, p, :], ps_y[:], ACT.Copy).then_inc(s["y_out"], 1)
                    act.wait_ge(s["y_out"], j + 1)
                    act.dma_start(y_dram[bass.ds(j * P, P), :], y[:, p, :]).then_inc(s[f"y_st{p}"], 16)

                def one(j, p, first=False, last=False):
                    if not last:
                        x_out(j + 1, 1 - p)
                    silu(j, p)
                    if not first:
                        y_store(j - 1, 1 - p)

                x_out(0, 0)
                one(0, 0, first=True)
                pairs(act, one, 1, NJ - 3)
                one(NJ - 2, 1)
                one(NJ - 1, 0, last=True)
                y_store(NJ - 1, 0)
                act.wait_ge(s["y_st0"], 16 * ((NJ + 1) // 2))
                act.wait_ge(s["y_st1"], 16 * (NJ // 2))

            @block.vector
            def _(dve):
                def multiply(j, p):
                    dve.wait_ge(s["u_done"], j + 1)
                    dve.wait_ge(s["silu_done"], j + 1)
                    dve.tensor_tensor(g[:, p, 0:FH], act_g[:, p, :], ps_u[:, 0:FH], ALU.mult).then_inc(s["g_ready"], 1)

                def gT_out(j, p):
                    dve.wait_ge(s["gT_turned"], j + 1)
                    dve.tensor_copy(gT[:, p, :], ps_gT[:]).then_inc(s["gT_done"], 1)

                def one(j, p, first=False):
                    if not first:
                        gT_out(j - 1, 1 - p)
                    multiply(j, p)

                dve.wait_ge(s["padded"], 1)
                one(0, 0, first=True)
                pairs(dve, one, 1, NJ - 1)
                gT_out(NJ - 1, 0)

            @block.tensor
            def _(pe):
                def weights_of(j):
                    e = pe.value_load(c.expert_of[0:1, bass.ds(j, 1)], min_val=0, max_val=E - 1)
                    pe.wait_ge(s["w_in"], 64 * e + 64)
                    return e * WCOLS

                def x_turn(j, p):
                    pe.wait_ge(s[f"x_in{p}"], 16 * ((j - p) // 2) + 16 if isinstance(j, int) else 8 * (j - p) + 16)
                    need(pe, s["xT_done"], j)
                    for q in range(DC):
                        last = pe.transpose(ps_xT[:, q * P:(q + 1) * P], xg[:, p, q * P:(q + 1) * P], c.ident[:])
                    last.then_inc(s["turned"], 1)

                def hidden(j, p, base, up):
                    if not up:
                        pe.wait_ge(s["xT_done"], j + 1)
                    need(pe, s["g_ready"] if up else s["silu_done"], j)
                    for q in range(DC):
                        last = pe.matmul((ps_u if up else ps_g)[:, 0:FH], xT[:, p, q * P:(q + 1) * P],
                                         w[:, bass.ds(base + (up * DC + q) * FH, FH)], start=(q == 0), stop=(q == DC - 1))
                    last.then_inc(s["u_done"] if up else s["g_done"], 1)

                def g_turn(j, p):
                    pe.wait_ge(s["g_ready"], j + 1)
                    need(pe, s["gT_done"], j)
                    for q in range(FC):
                        last = pe.transpose(ps_gT[:, q * P:(q + 1) * P], g[:, p, q * P:(q + 1) * P], c.ident[:])
                    last.then_inc(s["gT_turned"], 1)

                def down(j, p, base):
                    pe.wait_ge(s["gT_done"], j + 1)
                    need(pe, s["y_out"], j)
                    for q in range(FC):
                        rows = P if q < FC - 1 else FCR
                        last = pe.matmul(ps_y[:], gT[0:rows, p, q * P:(q + 1) * P],
                                         w[0:rows, bass.ds(base + 2 * DC * FH + q * D, D)], start=(q == 0), stop=(q == FC - 1))
                    last.then_inc(s["y_done"], 1)

                def one(j, p, first=False, last=False):
                    if not last:
                        x_turn(j + 1, 1 - p)
                    base = weights_of(j)
                    hidden(j, p, base, 0)
                    if not first:
                        g_turn(j - 1, 1 - p)
                    hidden(j, p, base, 1)
                    if not first:
                        down(j - 1, 1 - p, weights_of(j - 1))

                x_turn(0, 0)
                one(0, 0, first=True)
                pairs(pe, one, 1, NJ - 3)
                one(NJ - 2, 1)
                one(NJ - 1, 0, last=True)
                g_turn(NJ - 1, 0)
                down(NJ - 1, 0, weights_of(NJ - 1))


def combine(nc, c, y_dram, out):
    with ExitStack() as ctx:
        m = Memory(nc, ctx)
        place = m.sb("place_now", [P, 2, 2, 1], U32)
        yy = m.sb("yy", [P, 2, 2, D])
        r3 = m.sb("r3", [P, 2, 2, D])
        stats = m.sb("stats3", [P, 6])
        mv = m.sb("mv3", [P, 2, 2])
        rstd = m.sb("rstd3", [P, 2, 2])
        half = m.sb("half3", [P, 1])
        o = m.sb("o", [P, 2, D])
        names = "half place y_in0 y_in1 add0 add1 stats mv ve rstd o_done o_st0 o_st1".split()
        s = {k: m.sem("c_" + k) for k in names}
        out_rows = out.rearrange("b (t p) d -> p (b t) d", p=P)

        def tiles(eng, one):
            for t in range(TT):
                one(t, 0, t)
            with eng.Fori(1, B - 1) as b:
                for t in range(TT):
                    one(b * TT + t, b, t)
            for t in range(TT):
                one((B - 1) * TT + t, B - 1, t)

        def uses(b, t):
            return 2 * b + t // 2

        with nc.Block() as block:
            @block.gpsimd
            def _(pool):
                pool.memset(half[:], -0.5).then_inc(s["half"], 1)
                pool.wait_ge(s["half"], 1)

                def fetch(n, b, t, fresh):
                    p = t % 2
                    if not fresh:
                        pool.wait_ge(s["add1"], n - 1)
                        pool.wait_ge(s[f"y_in{p}"], 32 * uses(b, t))
                    for k in range(2):
                        last = pool.tensor_copy(place[:, p, k, :], c.slots[:, bass.ds(n, 1), k:k + 1].rearrange("p a k -> p (a k)"))
                    last.then_inc(s["place"], 1)
                    wait_apart(pool, s["place"], n + 1, c.pool_passed)
                    for k in range(2):
                        pool.indirect_dma_start(out=yy[:, p, k, :], out_offset=None, in_=y_dram[:],
                                                in_offset=bass.IndirectOffsetOnAxis(ap=place[:, p, k, :], axis=0)).then_inc(s[f"y_in{p}"], 16)

                def root(n, p):
                    wait_apart(pool, s["mv"], n + 1, c.pool_passed)
                    pool.tensor_scalar(rstd[:, p, 0:1], mv[:, p, 1:2], EPS, None, ALU.add).then_inc(s["ve"], 1)
                    pool.wait_ge(s["ve"], n + 1)
                    pool.tensor_tensor(rstd[:, p, 1:2], rstd[:, p, 0:1], half[:], ALU.pow).then_inc(s["rstd"], 1)

                fetch(0, 0, 0, True)
                fetch(1, 0, 1, True)
                with pool.Fori(0, B - 1) as b:
                    for t in range(TT):
                        root(b * TT + t, t % 2)
                        nb, nt = (b, t + 2) if t < 2 else (b + 1, t - 2)
                        fetch(b * TT + t + 2, nb, nt, False)
                for t in range(TT):
                    n = (B - 1) * TT + t
                    root(n, t % 2)
                    if t < 2:
                        fetch(n + 2, B - 1, t + 2, False)

            @block.vector
            def _(dve):
                dve.wait_ge(s["half"], 1)

                def add(n, b, t):
                    p = t % 2
                    base = c.attn[:, bass.ds(b * HG, HG), t * P:(t + 1) * P]
                    wt = [c.weights[:, bass.ds(n, 1), k:k + 1].rearrange("p a k -> p (a k)") for k in range(2)]
                    dve.wait_ge(s[f"y_in{p}"], 32 * uses(b, t) + 32)
                    dve.scalar_tensor_tensor(r3[:, p, 0, :].rearrange("p (g d) -> p g d", g=HG), yy[:, p, 0, :].rearrange("p (g d) -> p g d", g=HG),
                                             wt[0], base, ALU.mult, ALU.add).then_inc(s["add0"], 1)
                    dve.wait_ge(s["add0"], n + 1)
                    if not (isinstance(n, int) and n < 2):
                        dve.wait_ge(s["o_done"], n - 1)
                    dve.scalar_tensor_tensor(r3[:, p, 1, :], yy[:, p, 1, :], wt[1], r3[:, p, 0, :], ALU.mult, ALU.add).then_inc(s["add1"], 1)
                    dve.wait_ge(s["add1"], n + 1)
                    dve.bn_stats(stats[:], r3[:, p, 1, :]).then_inc(s["stats"], 1)
                    wait_apart(dve, s["stats"], n + 1, c.dve_passed)
                    dve.bn_aggr(mv[:, p, :], stats[:]).then_inc(s["mv"], 1)

                def one(n, b, t):
                    p = t % 2
                    if not (isinstance(n, int) and n == NT - 1):
                        add(*((n + 1, b, t + 1) if t < TT - 1 else (n + 1, b + 1, 0)))
                    dve.wait_ge(s["rstd"], n + 1)
                    if not (isinstance(n, int) and n < 2):
                        dve.wait_ge(s[f"o_st{p}"], 16 * uses(b, t))
                    dve.tensor_scalar(o[:, p, :], r3[:, p, 1, :], mv[:, p, 0:1], rstd[:, p, 1:2], ALU.subtract, ALU.mult).then_inc(s["o_done"], 1)

                add(0, 0, 0)
                tiles(dve, one)

            @block.sync
            def _(sp):
                def one(n, b, t):
                    sp.wait_ge(s["o_done"], n + 1)
                    sp.dma_start(out_rows[:, bass.ds(n, 1), :].rearrange("p a d -> p (a d)"), o[:, t % 2, :]).then_inc(s[f"o_st{t % 2}"], 16)

                tiles(sp, one)
                for k in range(2):
                    sp.wait_ge(s[f"o_st{k}"], 8 * NT)


def decoder(nc, x, ctx_512, mask_SxS2_bk1, mask_BxS2_bf0, L0_attn_Wq, L0_attn_bq, L0_attn_Wk, L0_attn_bk,
            L0_attn_Wv, L0_attn_bv, L0_xattn_Wq, L0_xattn_bq, L0_xattn_Wk, L0_xattn_bk, L0_ffn_gate_w,
            L0_ffn_w_gate, L0_ffn_w_up, L0_ffn_w_down, L0_ffn_sw_gate, L0_ffn_sw_up, L0_ffn_sw_down, out):
    def dram(name, shape, dt=F32):
        return nc.dram_tensor(name, shape, dt, kind="Internal").ap()

    qk_dram = dram("qk_dram", [2, 2, U, P, S])
    norm_dram = dram("norm_dram", [B * H, S])
    x2_dram = dram("x2_dram", [T, D])
    table_dram = dram("table_dram", [ROWS, 1], U32)
    y_dram = dram("y_dram", [NJ * P, D])

    with ExitStack() as ctx:
        m = Memory(nc, ctx)
        c = Kept()
        c.pool_passed, c.dve_passed = m.sem("pool_passed"), m.sem("dve_passed")
        build_constants(nc, m, c, table_dram)
        c.weights = m.sb("weights", [P, NT, 2])
        c.slots = m.sb("slots", [P, NT, 2], U32)
        c.listed = m.sb("listed", [P, NT, 2])
        c.choice = m.sb("choice", [P, NT, 2])
        c.both_sum = m.sb("both_sum", [P, E], BF16)
        c.first_row = m.sb("first_row", [1, NJ], I32)
        c.expert_of = m.sb("expert_of", [1, NJ], I32)
        c.bar = m.sb("bar_kept", [P, TT, B * H])
        c.attn = m.sb("attn", [P, U, S])
        with ExitStack() as ctx2:
            m2 = Memory(nc, ctx2)
            c.qk_ctx = [[m2.sb(f"qk_ctx{a}{b}", [P, B * S], F32R) for b in range(2)] for a in range(2)]
            with ExitStack() as ctx3:
                c.v = Memory(nc, ctx3).sb("v", [P, U, TT * P])
                project(nc, c, x, L0_attn_Wq, L0_attn_bq, L0_attn_Wk, L0_attn_bk, L0_attn_Wv, L0_attn_bv, qk_dram, norm_dram)
                choose_queries(nc, c, norm_dram, ctx_512, L0_xattn_Wq, L0_xattn_bq, L0_xattn_Wk, L0_xattn_bk)
                attend(nc, c, qk_dram)
            cross_and_shared(nc, c, x, mask_SxS2_bk1, mask_BxS2_bf0, L0_ffn_gate_w, L0_ffn_sw_gate, L0_ffn_sw_up,
                             L0_ffn_sw_down, x2_dram, table_dram)
        plan(nc, c)
        experts(nc, c, L0_ffn_w_gate, L0_ffn_w_up, L0_ffn_w_down, x2_dram, table_dram, y_dram)
        combine(nc, c, y_dram, out)


_INS = ["x", "ctx_512", "mask_SxS2_bk1", "mask_BxS2_bf0", "L0_attn_Wq", "L0_attn_bq", "L0_attn_Wk", "L0_attn_bk",
        "L0_attn_Wv", "L0_attn_bv", "L0_xattn_Wq", "L0_xattn_bq", "L0_xattn_Wk", "L0_xattn_bk", "L0_ffn_gate_w",
        "L0_ffn_w_gate", "L0_ffn_w_up", "L0_ffn_w_down", "L0_ffn_sw_gate", "L0_ffn_sw_up", "L0_ffn_sw_down"]


def kernel(**inputs):
    import numpy as _np
    import concourse.bacc as _bacc
    from concourse import mybir as _mybir
    from concourse.bass_utils import run_bass_kernel_spmd as _run

    nc = _bacc.Bacc("TRN2", target_bir_lowering=False, num_devices=1)
    arrays, args = {}, []
    for name in _INS:
        a = _np.ascontiguousarray(inputs[name])
        arrays[f"in_{name}_dram"] = a
        args.append(nc.dram_tensor(f"in_{name}_dram", a.shape, _mybir.dt.from_np(a.dtype), kind="ExternalInput").ap())
    shape = tuple(inputs["x"].shape)
    out = nc.dram_tensor("out_0_dram", shape, _mybir.dt.float32, kind="ExternalOutput").ap()
    decoder(nc, *args, out)
    r = _run(nc, [arrays], core_ids=[0])
    return r.results[0]["out_0_dram"]
```
